# Optimizing a Trainium2 kernel written in Bass

```python
import numpy as np
import jax
import jax.numpy as jnp

def _softmax(x, axis=-1):
    return jax.nn.softmax(x, axis=axis)

def _gelu(x):
    return jax.nn.gelu(x, approximate=True)

def _silu(x):
    return jax.nn.silu(x)

def _sigmoid(x):
    return jax.nn.sigmoid(x)

def _layernorm(x, axis=-1, eps=1e-05):
    m = jnp.mean(x, axis=axis, keepdims=True)
    v = jnp.var(x, axis=axis, keepdims=True)
    return (x - m) / jnp.sqrt(v + eps)

def _scatter_add(tgt, idx, src, axis=0):
    return tgt.at[idx].add(src)

def _segment_sum(src, seg, n):
    return jax.ops.segment_sum(src, seg, n)
kernel_name = 'mk_adaln_d1_jaxref_r8_867e32'

def setup_inputs(seed: int=0):
    np.random.seed(seed)
    _w = jnp.asarray

    def _L0_attn_setup():
        import jax, jax.numpy as jnp
        import numpy as np
        import math
        D_MODEL = 128
        NUM_HEADS = 16
        D_K = D_MODEL // NUM_HEADS
        B, S = (2, 256)

        def _linear_weight(key, out_f, in_f):
            return jax.random.normal(key, (out_f, in_f), jnp.float32) * math.sqrt(2.0 / in_f)
        key = jax.random.key(seed)
        ks = jax.random.split(key, 5)
        x = jax.random.normal(ks[0], (B, S, D_MODEL), jnp.float32)
        return {'x': x, 'Wq': _linear_weight(ks[1], D_MODEL, D_MODEL), 'bq': jnp.zeros((D_MODEL,), jnp.float32), 'Wk': _linear_weight(ks[2], D_MODEL, D_MODEL), 'bk': jnp.zeros((D_MODEL,), jnp.float32), 'Wv': _linear_weight(ks[3], D_MODEL, D_MODEL), 'bv': jnp.zeros((D_MODEL,), jnp.float32), 'Wo': _linear_weight(ks[4], D_MODEL, D_MODEL), 'bo': jnp.zeros((D_MODEL,), jnp.float32)}
    _L0_attn_in = _L0_attn_setup()

    def _L0_ffn_setup():
        import jax, jax.numpy as jnp
        import numpy as np
        B, T, E = (2, 256, 128)
        NEXP, TOPK, INTER = (8, 2, 176)
        key = jax.random.key(seed)
        ks = jax.random.split(key, 5)
        s = 0.02
        return {'x': jax.random.normal(ks[0], (B, T, E), dtype=jnp.float32), 'gate_w': jax.random.normal(ks[1], (NEXP, E), dtype=jnp.float32) * s, 'wg': jax.random.normal(ks[2], (NEXP, INTER, E), dtype=jnp.float32) * s, 'wu': jax.random.normal(ks[3], (NEXP, INTER, E), dtype=jnp.float32) * s, 'wd': jax.random.normal(ks[4], (NEXP, E, INTER), dtype=jnp.float32) * s}
    _L0_ffn_in = _L0_ffn_setup()
    _L0_c = _w((lambda *s: np.random.randn(*s).astype(np.float32) * 0.05)(16, 128))
    _L0_wmod = _w((lambda *s: np.random.randn(*s).astype(np.float32) * 0.05)(128, 6 * 128) * 128 ** (-0.5))
    _d = {'L0_attn_x': _L0_attn_in['x'], 'L0_attn_Wq': _L0_attn_in['Wq'], 'L0_attn_bq': _L0_attn_in['bq'], 'L0_attn_Wk': _L0_attn_in['Wk'], 'L0_attn_bk': _L0_attn_in['bk'], 'L0_attn_Wv': _L0_attn_in['Wv'], 'L0_attn_bv': _L0_attn_in['bv'], 'L0_attn_Wo': _L0_attn_in['Wo'], 'L0_attn_bo': _L0_attn_in['bo'], 'L0_ffn_gate_w': _L0_ffn_in['gate_w'], 'L0_ffn_wg': _L0_ffn_in['wg'], 'L0_ffn_wu': _L0_ffn_in['wu'], 'L0_ffn_wd': _L0_ffn_in['wd'], 'L0_c': _L0_c, 'L0_wmod': _L0_wmod}
    _x0 = _d['L0_attn_x']
    _d['L0_attn_x'] = jax.random.normal(jax.random.fold_in(jax.random.key(seed), 1), (16, 512, 128), dtype=_x0.dtype)
    del _x0
    return _d

def reference(L0_attn_x, L0_attn_Wq, L0_attn_bq, L0_attn_Wk, L0_attn_bk, L0_attn_Wv, L0_attn_bv, L0_attn_Wo, L0_attn_bo, L0_ffn_gate_w, L0_ffn_wg, L0_ffn_wu, L0_ffn_wd, L0_c, L0_wmod):

    def _L0_attn_ref(x, Wq, bq, Wk, bk, Wv, bv, Wo, bo):
        import jax, jax.numpy as jnp
        import numpy as np
        import math
        D_MODEL = 128
        NUM_HEADS = 16
        D_K = D_MODEL // NUM_HEADS
        B, S = (2, 256)

        def _linear_weight(key, out_f, in_f):
            return jax.random.normal(key, (out_f, in_f), jnp.float32) * math.sqrt(2.0 / in_f)
        b, s, _ = x.shape
        q = jnp.einsum('bsd,ed->bse', x, Wq) + bq
        k = jnp.einsum('bsd,ed->bse', x, Wk) + bk
        v = jnp.einsum('bsd,ed->bse', x, Wv) + bv
        q = q.reshape(b, s, NUM_HEADS, D_K).transpose(0, 2, 1, 3)
        k = k.reshape(b, s, NUM_HEADS, D_K).transpose(0, 2, 1, 3)
        v = v.reshape(b, s, NUM_HEADS, D_K).transpose(0, 2, 1, 3)
        scores = jnp.einsum('bhqd,bhkd->bhqk', q, k) / math.sqrt(D_K)
        attn = jax.nn.softmax(scores, axis=-1)
        out = jnp.einsum('bhqk,bhkd->bhqd', attn, v)
        out = out.transpose(0, 2, 1, 3).reshape(b, s, D_MODEL)
        return jnp.einsum('bsd,ed->bse', out, Wo) + bo

    def _L0_ffn_ref(x, gate_w, wg, wu, wd):
        import jax, jax.numpy as jnp
        import numpy as np
        B, T, E = (2, 256, 128)
        NEXP, TOPK, INTER = (8, 2, 176)
        scores = jnp.einsum('btd,ed->bte', x, gate_w)
        topk_scores, topk_idx = jax.lax.top_k(scores, TOPK)
        topk_probs = jax.nn.softmax(topk_scores, axis=-1)
        onehot = jax.nn.one_hot(topk_idx, NEXP, dtype=x.dtype)
        gating = jnp.sum(onehot * topk_probs[..., None], axis=-2)
        g = jnp.einsum('btd,eid->btei', x, wg)
        u = jnp.einsum('btd,eid->btei', x, wu)
        h = jax.nn.silu(g) * u
        expert_out = jnp.einsum('btei,edi->bted', h, wd)
        y = jnp.sum(gating[..., None] * expert_out, axis=-2)
        return y
    x = L0_attn_x
    mod = (_silu(L0_c) @ L0_wmod).reshape(L0_c.shape[0], 6, 1, -1)
    sa, ca, ga, sb, cb, gb = (mod[:, 0], mod[:, 1], mod[:, 2], mod[:, 3], mod[:, 4], mod[:, 5])
    ga = (2 * (ga >= 0) - 1) * jnp.maximum(jnp.abs(ga), 0.25)
    gb = (2 * (gb >= 0) - 1) * jnp.maximum(jnp.abs(gb), 0.25)
    h = _layernorm(x, axis=-1) * (1 + ca) + sa
    x = x + ga * _L0_attn_ref(h, L0_attn_Wq, L0_attn_bq, L0_attn_Wk, L0_attn_bk, L0_attn_Wv, L0_attn_bv, L0_attn_Wo, L0_attn_bo)
    h = _layernorm(x, axis=-1) * (1 + cb) + sb
    x = x + gb * _L0_ffn_ref(h, L0_ffn_gate_w, L0_ffn_wg, L0_ffn_wu, L0_ffn_wd)
    return x

_drawn_inputs = setup_inputs


def setup_inputs(seed=0):
    import zlib

    import numpy as np

    out = dict(_drawn_inputs(seed))
    spreads = {'L0_attn_bq': (0.0, 0.687),
     'L0_attn_bk': (0.0, 0.8),
     'L0_attn_bv': (0.0, 0.1),
     'L0_attn_bo': (0.0, 0.327)}
    factors = {'L0_ffn_gate_w': 8.0, 'L0_ffn_wg': 8.0, 'L0_ffn_wu': 8.0, 'L0_ffn_wd': 8.0}
    for name, (base, spread) in spreads.items():
        noise = np.random.default_rng([zlib.crc32(name.encode()), seed]).standard_normal(out[name].shape)
        drawn = base * np.exp(spread * noise) if base else spread * noise
        out[name] = jnp.asarray(drawn.astype(out[name].dtype))
    for name, factor in factors.items():
        out[name] = (out[name] * factor).astype(out[name].dtype)
    return out
```

```python
import math
from contextlib import ExitStack

import concourse.bass as bass
import numpy as np
from concourse import mybir

F32 = mybir.dt.float32
BF16 = mybir.dt.bfloat16
ALU = mybir.AluOpType
ACT = mybir.ActivationFunctionType
AX = mybir.AxisListType

P = 128
NB, S, D = 16, 512, 128
NH, DK = 16, 8
NE, INTER = 8, 176
QT = S // P
NT = NB * QT
HID = NE * INTER
NC = HID // P
EPS = 1e-5
SCALE = 1.0 / math.sqrt(DK)
PAIRS = NH // 2
GROUP = 4
NG = NH // GROUP
NS = NB * NG
TERMS = 6
SIDE = 64
SHIFT = TERMS * DK
VW = 32
STACK_DMAS = 18
PRM = 16
RSTD, NMR, CA, SA, GA, GABO, CB, SB, GB = 0, 4, 8, 9, 10, 11, 12, 13, 14
ST_BANK, S_BANK, PV_BANK, MISC_BANK = 0, 3, 6, 7
TURN = 3
ROUTE_STEPS = 21


def lin(f, n, d):
    if d is None:
        return f(n)
    assert f(n + 4) - f(n + 2) == f(n + 2) - f(n)
    return d * (f(n + 2) - f(n)) + f(n)


def wait(eng, sem, f, n, d):
    v = lin(f, n, d)
    if not isinstance(v, int) or v > 0:
        eng.wait_ge(sem, v)


def batch_of(n, d):
    return n if d is None else d * 2 + n


def turn(i):
    last = NH * QT - 1
    before = i - TURN if i >= TURN else max(j for j in range(last + 1) if j % TURN == i % TURN) - last - 1
    return i % TURN, i - before


def misc_at(b, k):
    g, r = divmod(k, GROUP)
    s = NG * b + g
    if r == 0:
        step = ("shift", s + 1, NS)
    elif r == 1:
        step = ("o", s - 2, NS)
    else:
        step = {3: ("v", b + 1, NB), 6: ("oT", b - 1, NB), 7: ("y", b - 1, NB), 10: ("x1", b - 1, NB),
                11: ("hT", b + 2, NB), 14: ("q", b + 2, NB), 15: ("k", b + 2, NB)}.get(k)
    return step[:2] if step and 0 <= step[1] < step[2] else None


def misc_order():
    steps = [("hT", 0), ("q", 0), ("k", 0)]
    for b in range(-1, NB + 1):
        steps += [misc_at(b, k) for k in range(NH) if misc_at(b, k)]
    return {step: i for i, step in enumerate(steps)}


def misc2_at(n, c):
    step = {3: ("h", n + 1), 4: ("route", n + 1), 6: ("out", n - 1), 8: ("gates", n + 1)}.get(c)
    return step if step and 0 <= step[1] < NB else None


def misc2_order():
    steps = []
    for n in range(-1, NB + 1):
        steps += [misc2_at(n, c) for c in range(NC) if misc2_at(n, c)]
    return {step: i for i, step in enumerate(steps)}


def adaln_block(nc, x, Wq, bq, Wk, bk, Wv, bv, Wo, bo, gate_w, wg, wu, wd, c, wmod,
                ident_c, rows_c, rank_c, out):
    with ExitStack() as ctx:
        def sb(name, shape, dt=F32):
            return ctx.enter_context(nc.sbuf_tensor(name, shape, dt))

        def sem(name):
            return ctx.enter_context(nc.semaphore(name))

        q_parts_d = nc.dram_tensor("q_parts_d", [NB, 3, P, S], BF16, kind="Internal").ap()
        k_parts_d = nc.dram_tensor("k_parts_d", [NB, 3, P, S], BF16, kind="Internal").ap()
        prm_d = nc.dram_tensor("prm_d", [NB, P, PRM], F32, kind="Internal").ap()
        prm2_d = nc.dram_tensor("prm2_d", [NB, P, PRM], F32, kind="Internal").ap()
        x1_d = nc.dram_tensor("x1_d", [NB, S, D], F32, kind="Internal").ap()
        mv_d = nc.dram_tensor("mv_d", [NB, P, QT * 2], F32, kind="Internal").ap()

        ident = sb("ident", [P, P])
        identb = sb("identb", [P, P], BF16)
        rows_f = sb("rows_f", [3 * NE, NC, P])
        rows = sb("rows", [3 * NE, NC, P], BF16)
        rank = sb("rank", [P, QT, NE])
        w_nat = sb("w_nat", [P, 4, D])
        w_t = sb("w_t", [P, 4, D])
        wqT, wkT, wvT, woT = (w_t[:, i, :] for i in range(4))
        bias = sb("bias", [P, 4])
        b_nat = sb("b_nat", [4, D])
        b_perm = sb("b_perm", [2, D])
        c_nat = sb("c_nat", [NB, D])
        c_silu = sb("c_silu", [NB, D])
        gw_nat = sb("gw_nat", [NE, D])
        gw_t = sb("gw_t", [P, NE])
        c_t = sb("c_t", [P, NB])
        wmod_s = sb("wmod_s", [P, 6 * D])
        mod = sb("mod", [P, 6, NB])
        gtmp = sb("gtmp", [P, 3, 2, NB])
        wg_t = sb("wg_t", [P, NC, P])
        wu_t = sb("wu_t", [P, NC, P])
        wd_t = sb("wd_t", [P, NC, D])
        prm = sb("prm", [P, NB, PRM])
        mv = sb("mv", [P, NT, 2])
        st6 = sb("st6", [P, NT, 6])
        rs4 = sb("rs4", [P, 4, NT])

        probs = sb("probs", [P, 2, GROUP, QT * S])
        x_all = probs[:, 0, :, :].rearrange("p a (t d) -> p (a t) d", d=D)
        ffn_nat = probs[:, 1, 0:3, 0:HID]
        ones_rows = probs[0:2, 1, 3, :].bitcast(BF16)
        q_st = [[sb(f"q_st{i}_{side}", [P, PAIRS, S], BF16) for side in range(2)] for i in range(2)]
        k_st = [sb(f"k_st{i}", [P, PAIRS, S], BF16) for i in range(2)]
        v_aug = [sb(f"v_aug{i}", [P, QT, NH, VW]) for i in range(2)]
        x_a = sb("x_a", [P, QT, D])
        prm_a = sb("prm_a", [P, PRM])
        x_n = sb("x_n", [P, QT, D])
        h_t = sb("h_t", [P, S])
        q32 = sb("q32", [P, S])
        k32 = sb("k32", [P, S])
        q_parts = sb("q_parts", [P, 3, S], BF16)
        k_parts = sb("k_parts", [P, 3, S], BF16)
        rest = sb("rest", [P, S])
        maxes = [sb(f"maxes{i}", [P, 2, 2, QT]) for i in range(2)]
        shift = [sb(f"shift{i}", [P, 2, 2, 2, QT], BF16) for i in range(2)]
        shift_t = [sb(f"shift_t{i}", [4 * 2 * QT, P], BF16) for i in range(2)]
        o_aug = [sb(f"o_aug{i}", [P, S]) for i in range(2)]
        o_rs = sb("o_rs", [P, QT, GROUP])
        o_n = sb("o_n", [P, QT, NH, DK])
        o_t = sb("o_t", [P, S])
        z = sb("z", [P, S])
        x_r = sb("x_r", [P, QT, D])
        prm_t = sb("prm_t", [P, PRM])
        x1_s = sb("x1_s", [P, QT, D])
        st_b = sb("st_b", [P, QT, 6])
        mv_b = sb("mv_b", [P, QT, 2])

        hid = [probs[:, 0, i, 0:S] for i in range(3)]
        silu = [probs[:, 1, i, 0:S] for i in range(2)]
        su = [probs[:, 1, 2 + i, 0:S] for i in range(2)]
        h2_t = [probs[:, 0, i, S:2 * S] for i in range(2)]
        gate_t = [sb(f"gate_t{i}", [3 * NE, S], BF16) for i in range(2)]
        route = sb("route", [P, 12, QT, NE])
        top = sb("top", [P, 8, QT])
        gate_parts = sb("gate_parts", [P, QT, 3, NE], BF16)
        out_s = x1_s

        ps = ctx.enter_context(nc.psum_tensor("ps", [P, 8, S], F32))
        misc = ps[:, MISC_BANK, :]
        misc_bf = misc.bitcast(BF16)

        consts_loaded = sem("consts_loaded")
        x_all_loaded = [sem(f"x_all_loaded{i}") for i in range(4)]
        ffn_loaded = sem("ffn_loaded")
        c_ready = sem("c_ready")
        setup_filled = sem("setup_filled")
        setup_drained = sem("setup_drained")
        fills_done = sem("fills_done")
        ones_ready = sem("ones_ready")
        ones_stacked = sem("ones_stacked")
        zeros_ready = sem("zeros_ready")
        zeros_stacked = sem("zeros_stacked")
        dve_step = sem("dve_step")
        var_ready = sem("var_ready")
        rstd_ready = sem("rstd_ready")
        prm_ready = sem("prm_ready")
        prm_stored = sem("prm_stored")
        xa_loaded = sem("xa_loaded")
        xn_ready = sem("xn_ready")
        misc_filled = sem("misc_filled")
        misc_drained = sem("misc_drained")
        pool_step = sem("pool_step")
        split_ready = sem("split_ready")
        parts_stored = sem("parts_stored")
        stack_ready = sem("stack_ready")
        scores_ready = sem("scores_ready")
        maxes_done = sem("maxes_done")
        shift_high = sem("shift_high")
        shift_ready = sem("shift_ready")
        shift_stacked = sem("shift_stacked")
        st_ready = sem("st_ready")
        exps_done = sem("exps_done")
        pv_ready = sem("pv_ready")
        pv_taken = sem("pv_taken")
        o_rs_ready = sem("o_rs_ready")
        xr_loaded = sem("xr_loaded")
        x1_stats = sem("x1_stats")
        stats_ready = sem("stats_ready")
        x1_stored = sem("x1_stored")
        mv_loaded = sem("mv_loaded")
        var2_ready = sem("var2_ready")
        rstd2_ready = sem("rstd2_ready")
        prm2_ready = sem("prm2_ready")
        prm2_stored = sem("prm2_stored")
        xb_loaded = sem("xb_loaded")
        xn2_ready = sem("xn2_ready")
        misc2_filled = sem("misc2_filled")
        misc2_drained = sem("misc2_drained")
        route_step = sem("route_step")
        margin_ready = sem("margin_ready")
        tanh_ready = sem("tanh_ready")
        g_ready = sem("g_ready")
        u_ready = sem("u_ready")
        gate_ready = sem("gate_ready")
        silu_done = sem("silu_done")
        su_done = sem("su_done")
        hid_ready = sem("hid_ready")
        down_done = sem("down_done")
        y_taken = sem("y_taken")
        z_loaded = sem("z_loaded")
        out_stored = sem("out_stored")

        at = misc_order()
        at2 = misc2_order()
        N_CONSTS = 14
        SETUP_W, SETUP_GC, SETUP_MOD, SETUP_FFN = 0, 1, 2, 3
        FFN_GROUPS = [(w, c0, min(4, NC - c0)) for w in range(3) for c0 in range(0, NC, 4)]
        N_SETUP = SETUP_FFN + len(FFN_GROUPS)
        FIRST, LOOP = 2, (NB - 4) // 2

        block = ctx.enter_context(nc.Block())

        @block.sync
        def _(sp):
            def load_const(dst, src):
                sp.dma_start(dst, src).then_inc(consts_loaded, 16)

            load_const(ident[:, :], ident_c)
            load_const(c_nat[:, :], c)
            for q in range(4):
                n = NT // 4
                sp.dma_start(x_all[:, n * q:n * (q + 1), :],
                             x.rearrange("b (t p) d -> p (b t) d", p=P)[:, n * q:n * (q + 1), :]
                             ).then_inc(x_all_loaded[q], 16)
                if q == 0:
                    for i, w in enumerate((Wq, Wk, Wv, Wo)):
                        load_const(w_nat[:, i, :], w)
                    load_const(wmod_s[:, :], wmod)
                    load_const(gw_nat[:, :], gate_w)
                    for i, v in enumerate((bq, bk, bv, bo)):
                        load_const(b_nat[i:i + 1, :], v.rearrange("(o n) -> o n", o=1))
                    load_const(rows_f[:, :, :], rows_c)
                    load_const(rank[:, :, :], rank_c)
            sp.dma_start(ffn_nat[:, 0, :].rearrange("p (k d) -> p k d", d=D),
                         wg.rearrange("e i d -> (e i) d").rearrange("(k p) d -> p k d", p=P)).then_inc(ffn_loaded, 16)
            sp.dma_start(ffn_nat[:, 1, :].rearrange("p (k d) -> p k d", d=D),
                         wu.rearrange("e i d -> (e i) d").rearrange("(k p) d -> p k d", p=P)).then_inc(ffn_loaded, 16)
            sp.dma_start(ffn_nat[:, 2, :].rearrange("p (e i) -> p e i", e=NE),
                         wd.rearrange("e d i -> d e i")).then_inc(ffn_loaded, 16)
            sp.wait_ge(ones_ready, 1)
            for i in range(2):
                for side in range(2):
                    r0 = SIDE * side + SHIFT
                    sp.dma_start(k_st[i][r0:r0 + 2, :, :], ones_rows.rearrange("p (j s) -> p j s", s=S)
                                 ).then_inc(ones_stacked, 16)
            sp.wait_ge(prm_ready, 1)
            sp.dma_start(prm_d.rearrange("b p k -> p b k"), prm[:, :, :]).then_inc(prm_stored, 16)
            sp.wait_ge(prm_stored, 16)

            sp.wait_ge(zeros_ready, 4)
            for i in range(2):
                for side in range(2):
                    spare = slice(SIDE * side + SHIFT + 2, SIDE * (side + 1))
                    for st in (q_st[i][side], k_st[i]):
                        sp.dma_start(st[spare, :, :], q_st[i][1 - side][spare, :, :]).then_inc(zeros_stacked, 16)

            def load_x_a(n, d):
                wait(sp, misc_drained, lambda n: at["hT", n - 1] + 1 if n else 0, n, d)
                b = batch_of(n, d)
                sp.dma_start(x_a[:, :, :], x[b].rearrange("(t p) d -> p t d", p=P)).then_inc(xa_loaded, 16)
                sp.dma_start(prm_a[:, :], prm_d[b]).then_inc(xa_loaded, 16)

            def load_x_r(n, d):
                wait(sp, misc_drained, lambda n: at["x1", n - 1] + 1 if n else 0, n, d)
                b = batch_of(n, d)
                sp.dma_start(x_r[:, :, :], x[b].rearrange("(t p) d -> p t d", p=P)).then_inc(xr_loaded, 16)
                sp.dma_start(prm_t[:, :], prm_d[b]).then_inc(xr_loaded, 16)

            def stack_shift(b, g, d):
                wait(sp, misc_drained, lambda b: at["shift", NG * b + g] + 1, b, d)
                for side in range(2):
                    for part in range(2):
                        row = SIDE * side + SHIFT + part
                        src = 2 * QT * (2 * side + part)
                        sp.dma_start(q_st[b % 2][side][row:row + 1, 2 * g:2 * g + 2, :],
                                     shift_t[g % 2][src:src + 2 * QT, :]).then_inc(shift_stacked, 16)

            def store_parts(n, d):
                b = batch_of(n, d)
                for i, (parts, dram) in enumerate(((q_parts, q_parts_d), (k_parts, k_parts_d))):
                    wait(sp, split_ready, lambda n: 2 * n + i + 1, n, d)
                    sp.dma_start(dram[b].rearrange("t r s -> r t s"), parts[:, :, :]).then_inc(parts_stored, 16)

            def load_stacks(n, d):
                b = batch_of(n, d)
                wait(sp, parts_stored, lambda n: 32 * (n + 1), n, d)
                if d is None and n <= 1:
                    sp.wait_ge(ones_stacked, 64)
                    sp.wait_ge(zeros_stacked, 128)
                for side in range(2):
                    lo, hi = SIDE * side, SIDE * (side + 1)
                    sp.dma_start(q_st[n % 2][side][lo + SHIFT:lo + SHIFT + 2, :, :],
                                 q_st[n % 2][1 - side][lo + SHIFT:lo + SHIFT + 2, :, :]).then_inc(stack_ready, 16)
                    for u in range(TERMS // 2):
                        dst = slice(lo + 2 * DK * u, lo + 2 * DK * (u + 1))
                        for st, dram, parts in ((q_st[n % 2][side], q_parts_d, ((0, 0), (1, 1), (0, 2))[u]),
                                                (k_st[n % 2], k_parts_d, ((1, 2), (1, 2), (0, 1))[u])):
                            first, second = parts
                            if first == second:
                                for t in range(2):
                                    sp.dma_start(st[lo + DK * (2 * u + t):lo + DK * (2 * u + t + 1), :, :],
                                                 dram[b, first, lo:hi, :].rearrange("(e j) s -> e j s", e=DK)
                                                 ).then_inc(stack_ready, 16)
                            else:
                                src = dram[b, first:second + 1:second - first, lo:hi, :]
                                sp.dma_start(st[dst, :, :].rearrange("p j s -> p (j s)"),
                                             src.rearrange("t (e j) s -> t e (j s)", e=DK)).then_inc(stack_ready, 16)

            def store_x1(n, d):
                wait(sp, stats_ready, lambda n: n + 1, n, d)
                b = batch_of(n, d)
                sp.dma_start(x1_d[b].rearrange("(t p) d -> p t d", p=P), x1_s[:, :, :]).then_inc(x1_stored, 16)
                sp.dma_start(mv_d[b], mv_b[:, :, :]).then_inc(x1_stored, 16)

            def batch(b, d=None):
                if b + 2 < NB:
                    load_x_a(b + 2, d)
                if 0 <= b < NB:
                    stack_shift(b, 1, d)
                if b + 1 < NB:
                    store_parts(b + 1, d)
                    load_stacks(b + 1, d)
                if 0 <= b - 1:
                    load_x_r(b - 1, d)
                if 0 <= b < NB:
                    stack_shift(b, 2, d)
                    stack_shift(b, 3, d)
                if 0 <= b - 1:
                    store_x1(b - 1, d)
                if b + 1 < NB:
                    stack_shift(b + 1, 0, d)

            load_x_a(0, None)
            for b in range(-1, FIRST):
                batch(b)
            with sp.Fori(0, LOOP) as d:
                batch(FIRST, d)
                batch(FIRST + 1, d)
            for b in range(FIRST + 2 * LOOP, NB + 1):
                batch(b)

            sp.wait_ge(x1_stored, 32 * NB)
            sp.dma_start(mv[:, :, :].rearrange("p (b t) k -> p b (t k)", b=NB), mv_d.rearrange("b p k -> p b k")
                         ).then_inc(mv_loaded, 16)
            sp.wait_ge(prm2_ready, 1)
            sp.dma_start(prm2_d.rearrange("b p k -> p b k"), prm[:, :, :]).then_inc(prm2_stored, 16)
            sp.wait_ge(prm2_stored, 16)

            def load_x_b(n, d):
                wait(sp, misc2_drained, lambda n: at2["h", n - 1] + 1 if n else 0, n, d)
                b = batch_of(n, d)
                sp.dma_start(x_a[:, :, :], x1_d[b].rearrange("(t p) d -> p t d", p=P)).then_inc(xb_loaded, 16)
                sp.dma_start(prm_a[:, :], prm2_d[b]).then_inc(xb_loaded, 16)

            def load_x_z(n, d):
                wait(sp, misc2_drained, lambda n: at2["out", n - 1] + 1 if n else 0, n, d)
                b = batch_of(n, d)
                sp.dma_start(x_r[:, :, :], x1_d[b].rearrange("(t p) d -> p t d", p=P)).then_inc(z_loaded, 16)
                sp.dma_start(prm_t[:, :], prm2_d[b]).then_inc(z_loaded, 16)

            def store_out(n, d):
                wait(sp, misc2_drained, lambda n: at2["out", n] + 1, n, d)
                sp.dma_start(out[batch_of(n, d)].rearrange("(t p) d -> p t d", p=P), out_s[:, :, :]
                             ).then_inc(out_stored, 16)

            def ffn_block(n, d=None):
                if 0 <= n + 2 < NB:
                    load_x_b(n + 2, d)
                if 0 <= n - 1:
                    store_out(n - 1, d)
                if 0 <= n < NB:
                    load_x_z(n, d)

            load_x_b(0, None)
            for n in range(-1, FIRST):
                ffn_block(n)
            with sp.Fori(0, LOOP) as d:
                ffn_block(FIRST, d)
                ffn_block(FIRST + 1, d)
            for n in range(FIRST + 2 * LOOP, NB + 1):
                ffn_block(n)
            sp.wait_ge(out_stored, 16 * NB)

        @block.tensor
        def _(pe):
            def setup_bank(i):
                if i >= 2:
                    pe.wait_ge(setup_drained, i - 1)
                return ps[:, i % 2, :]

            pe.wait_ge(consts_loaded, 16 * N_CONSTS)
            bank = setup_bank(SETUP_W)
            for i in range(4):
                mm = pe.transpose(bank[:, P * i:P * (i + 1)], w_nat[:, i, :], ident[:, :])
            mm.then_inc(setup_filled, 1)
            bank = setup_bank(SETUP_GC)
            pe.transpose(bank[:, 0:NE], gw_nat[:, :], ident[0:NE, 0:NE])
            pe.wait_ge(c_ready, 2)
            pe.transpose(bank[:, NE:NE + NB], c_silu[:, :], ident[0:NB, 0:NB])
            pe.transpose(bank[:, 32:36], b_nat[:, :], ident[0:4, 0:4])
            pe.transpose(bank[:, 36:38], b_perm[:, :], ident[0:2, 0:2]).then_inc(setup_filled, 1)
            bank = setup_bank(SETUP_MOD)
            pe.wait_ge(setup_drained, SETUP_GC + 1)
            for i in range(6):
                mm = pe.matmul(bank[:, NB * i:NB * (i + 1)], wmod_s[:, D * i:D * (i + 1)], c_t[:, :],
                               start=True, stop=True)
            mm.then_inc(setup_filled, 1)
            pe.wait_ge(ffn_loaded, 48)
            for i, (w, c0, n) in enumerate(FFN_GROUPS):
                bank = setup_bank(SETUP_FFN + i)
                for m in range(n):
                    mm = pe.transpose(bank[:, P * m:P * (m + 1)], ffn_nat[:, w, P * (c0 + m):P * (c0 + m + 1)],
                                      ident[:, :])
                mm.then_inc(setup_filled, 1)
            pe.wait_ge(setup_drained, N_SETUP)
            pe.wait_ge(fills_done, 6)

            def misc_step(kind, n, g, d):
                key = (lambda n: (kind, NG * n + g)) if kind in ("shift", "o") else (lambda n: (kind, n))
                wait(pe, misc_drained, lambda n: at[key(n)], n, d)
                if kind == "hT":
                    wait(pe, xn_ready, lambda n: n + 1, n, d)
                    for t in range(QT):
                        mm = pe.transpose(misc[:, P * t:P * (t + 1)], x_n[:, t, :], ident[:, :])
                elif kind == "q":
                    mm = pe.matmul(misc, wqT, h_t[:, :], start=True, stop=True)
                elif kind == "k":
                    mm = pe.matmul(misc, wkT, h_t[:, :], start=True, stop=True)
                elif kind == "v":
                    for t in range(QT):
                        mm = pe.matmul(misc[:, P * t:P * (t + 1)], h_t[:, P * t:P * (t + 1)], wvT,
                                       start=True, stop=True)
                elif kind == "shift":
                    wait(pe, shift_ready, lambda n: NG * n + g + 1, n, d)
                    mm = pe.transpose(misc_bf[0:8 * QT, 0:P],
                                      shift[g % 2][:, :, :, :, :].rearrange("p a b c q -> p (a b c q)"), identb[:, :])
                elif kind == "o":
                    wait(pe, pv_taken, lambda n: NG * n + g + 1, n, d)
                    for t in range(QT):
                        mm = pe.transpose(misc[:, P * t:P * (t + 1)], o_aug[g % 2][:, P * t:P * (t + 1)], ident[:, :])
                elif kind == "oT":
                    for t in range(QT):
                        mm = pe.transpose(misc[:, P * t:P * (t + 1)],
                                          o_n[:, t, :, :].rearrange("p h e -> p (h e)"), ident[:, :])
                elif kind == "y":
                    mm = pe.matmul(misc, woT, o_t[:, :], start=True, stop=True)
                elif kind == "x1":
                    for t in range(QT):
                        mm = pe.transpose(misc[:, P * t:P * (t + 1)], z[:, P * t:P * (t + 1)], ident[:, :])
                mm.then_inc(misc_filled, 1)

            def batch(b, d=None):
                for k in range(NH):
                    g, hh = divmod(k, GROUP)
                    s = NG * b + g
                    exps, looks = 0 <= s < NS, 0 <= s + 2 < NS
                    side, j = hh % 2, 2 * g + hh // 2
                    hs, gs, bs = hh ^ 1, (g + 2) % NG, b + (g + 2) // NG
                    side_s, js = hs % 2, 2 * gs + hs // 2
                    for t in range(QT):
                        if exps:
                            if hh == 0 and t == 0:
                                wait(pe, shift_stacked, lambda b: 64 * (NG * b + g + 1), b, d)
                            bank, ago = turn(QT * k + t)
                            wait(pe, exps_done, lambda b: QT * (NH * b + k) + t + 1 - ago, b, d)
                            pe.matmul(ps[:, ST_BANK + bank, :], k_st[b % 2][:, j, P * t:P * (t + 1)],
                                      q_st[b % 2][side][:, j, :], start=True, stop=True).then_inc(st_ready, 1)
                        if looks:
                            if k == 8 and t == 0:
                                wait(pe, stack_ready, lambda b: 16 * STACK_DMAS * (b + 2), b, d)
                            bank, ago = turn(QT * (GROUP * gs + hh) + t)
                            wait(pe, maxes_done, lambda b: 16 * (NG * b + g + 2) + 4 * hh + t + 1 - ago, b, d)
                            pe.matmul(ps[:, S_BANK + bank, :], q_st[bs % 2][side_s][:, js, P * t:P * (t + 1)],
                                      k_st[bs % 2][:, js, :], start=True, stop=True).then_inc(scores_ready, 1)
                    if 0 <= s - 1 < NS:
                        gp, bp = (g - 1) % NG, b + (g - 1) // NG
                        if hh == 0:
                            wait(pe, exps_done, lambda b: 16 * (NG * b + g), b, d)
                            wait(pe, pv_taken, lambda b: NG * b + g - 1, b, d)
                            if gp == 0:
                                wait(pe, misc_drained, lambda b: at["v", b] + 1, b, d)
                        for i in range(GROUP):
                            mm = pe.matmul(ps[VW * i:VW * (i + 1), PV_BANK, :], v_aug[bp % 2][:, hh, GROUP * gp + i, :],
                                           probs[:, gp % 2, i, S * hh:S * (hh + 1)], start=(hh == 0), stop=(hh == QT - 1))
                        if hh == QT - 1:
                            mm.then_inc(pv_ready, 1)
                    step = misc_at(b, k)
                    if step:
                        kind, n = step
                        if kind in ("shift", "o"):
                            misc_step(kind, n // NG, n % NG, d)
                        else:
                            misc_step(kind, n, 0, d)

            misc_step("hT", 0, 0, None)
            misc_step("q", 0, 0, None)
            misc_step("k", 0, 0, None)
            for b in range(-1, FIRST):
                batch(b)
            with pe.Fori(0, LOOP) as d:
                batch(FIRST, d)
                batch(FIRST + 1, d)
            for b in range(FIRST + 2 * LOOP, NB + 1):
                batch(b)

            def misc2_step(kind, n, d):
                wait(pe, misc2_drained, lambda n: at2[kind, n], n, d)
                if kind == "h":
                    wait(pe, xn2_ready, lambda n: n + 1, n, d)
                    for t in range(QT):
                        mm = pe.transpose(misc[:, P * t:P * (t + 1)], x_n[:, t, :], ident[:, :])
                elif kind == "route":
                    for t in range(QT):
                        mm = pe.matmul(misc[:, NE * t:NE * (t + 1)], h2_t[n % 2][:, P * t:P * (t + 1)], gw_t[:, :],
                                       start=True, stop=True)
                elif kind == "gates":
                    wait(pe, route_step, lambda n: ROUTE_STEPS * (n + 1), n, d)
                    for t in range(QT):
                        mm = pe.transpose(misc_bf[0:3 * NE, P * t:P * (t + 1)],
                                          gate_parts[:, t, :, :].rearrange("p a e -> p (a e)"), identb[:, :])
                elif kind == "out":
                    wait(pe, y_taken, lambda n: n + 1, n, d)
                    for t in range(QT):
                        mm = pe.transpose(misc[:, P * t:P * (t + 1)], z[:, P * t:P * (t + 1)], ident[:, :])
                mm.then_inc(misc2_filled, 1)

            def ffn_block(n, d=None):
                for ch in range(NC):
                    if 0 <= n < NB:
                        par = (n + ch) % 2
                        if ch == 0:
                            wait(pe, misc2_drained, lambda n: at2["gates", n] + 1, n, d)
                        wait(pe, silu_done, lambda n: NC * n + ch - 1, n, d)
                        pe.matmul(ps[:, par, :], wg_t[:, ch, :], h2_t[n % 2], start=True, stop=True).then_inc(g_ready, 1)
                        wait(pe, su_done, lambda n: NC * n + ch - 1, n, d)
                        pe.matmul(ps[:, 2 + par, :], wu_t[:, ch, :], h2_t[n % 2], start=True, stop=True).then_inc(u_ready, 1)
                        wait(pe, hid_ready, lambda n: NC * n + ch, n, d)
                        pe.matmul(ps[:, 4, :], rows[:, ch, :], gate_t[n % 2][:, :], start=True, stop=True
                                  ).then_inc(gate_ready, 1)
                    nd, cd = (n, ch - 2) if ch >= 2 else (n - 1, NC - 2 + ch)
                    if 0 <= nd < NB:
                        wait(pe, hid_ready, lambda n: NC * n + ch - 1, n, d)
                        if cd == 0:
                            wait(pe, y_taken, lambda n: n - 1, n, d)
                        pe.matmul(ps[:, 5 + nd % 2, :], wd_t[:, cd, :], hid[cd % 3], start=(cd == 0), stop=(cd == NC - 1)
                                  ).then_inc(down_done, 1)
                    step = misc2_at(n, ch)
                    if step:
                        misc2_step(*step, d)

            for n in range(-1, FIRST):
                ffn_block(n)
            with pe.Fori(0, LOOP) as d:
                ffn_block(FIRST, d)
                ffn_block(FIRST + 1, d)
            for n in range(FIRST + 2 * LOOP, NB + 1):
                ffn_block(n)

        @block.scalar
        def _(act):
            act.wait_ge(consts_loaded, 16 * N_CONSTS)
            act.activation(c_silu[:, :], c_nat[:, :], ACT.Silu).then_inc(c_ready, 1)
            act.copy(b_perm[:, :].rearrange("p (h e j) -> p j h e", h=2, e=DK),
                     b_nat[0:2, :].rearrange("p (j h e) -> p j h e", h=2, e=DK)).then_inc(c_ready, 1)
            act.wait_ge(setup_filled, SETUP_W + 1)
            bank = ps[:, SETUP_W % 2, :]
            for i in range(2):
                act.copy(w_t[:, i, :].rearrange("p (h e j) -> p j h e", h=2, e=DK),
                         bank[:, P * i:P * (i + 1)].rearrange("p (j h e) -> p j h e", h=2, e=DK))
            act.copy(w_t[:, 2:4, :].rearrange("p a d -> p (a d)"), bank[:, 2 * P:4 * P]).then_inc(setup_drained, 1)
            act.wait_ge(setup_filled, SETUP_GC + 1)
            bank = ps[:, SETUP_GC % 2, :]
            act.copy(gw_t[:, :], bank[:, 0:NE])
            act.copy(bias[:, 2:4], bank[:, 34:36])
            act.copy(bias[:, 0:2], bank[:, 36:38])
            act.copy(c_t[:, :], bank[:, NE:NE + NB]).then_inc(setup_drained, 1)
            act.wait_ge(setup_filled, SETUP_MOD + 1)
            act.copy(mod[:, :, :].rearrange("p a b -> p (a b)"), ps[:, SETUP_MOD % 2, 0:6 * NB]).then_inc(setup_drained, 1)
            for i, (w, c0, n) in enumerate(FFN_GROUPS):
                act.wait_ge(setup_filled, SETUP_FFN + i + 1)
                act.copy((wg_t, wu_t, wd_t)[w][:, c0:c0 + n, :].rearrange("p k d -> p (k d)"),
                         ps[:, (SETUP_FFN + i) % 2, 0:P * n]).then_inc(setup_drained, 1)
            act.wait_ge(var_ready, 1)
            act.activation(rs4[:, 2, :], rs4[:, 1, :], ACT.Sqrt).then_inc(rstd_ready, 1)

            def normalise(n, d, loaded, filled, key, where, ready):
                wait(act, loaded, lambda n: 32 * (n + 1), n, d)
                wait(act, filled, lambda n: where[key, n - 1] + 1 if n else 0, n, d)
                for t in range(QT):
                    ins = act.activation(x_n[:, t, :], x_a[:, t, :], ACT.Identity,
                                         scale=prm_a[:, RSTD + t:RSTD + t + 1], bias=prm_a[:, NMR + t:NMR + t + 1])
                ins.then_inc(ready, 1)

            def misc_drain(kind, n, d):
                wait(act, misc_filled, lambda n: at[kind, n] + 1, n, d)
                if kind == "hT":
                    ins = act.activation(h_t[:, :], misc, ACT.Identity, scale=prm_a[:, CA:CA + 1], bias=prm_a[:, SA:SA + 1])
                elif kind in ("q", "k"):
                    full, high, col = (q32, q_parts[:, 0, :], 0) if kind == "q" else (k32, k_parts[:, 1, :], 1)
                    wait(act, parts_stored, lambda n: 32 * n, n, d)
                    act.activation(full[:, :], misc, ACT.Identity, bias=bias[:, col:col + 1])
                    ins = act.activation(high, misc, ACT.Identity, bias=bias[:, col:col + 1])
                elif kind == "v":
                    wait(act, pv_ready, lambda n: NG * (n - 1), n, d)
                    ins = act.copy(v_aug[n % 2][:, :, :, 0:DK], misc.rearrange("p (t h e) -> p t h e", t=QT, e=DK))
                elif kind == "oT":
                    ins = act.activation(o_t[:, :], misc, ACT.Identity, bias=bias[:, 2:3])
                elif kind == "y":
                    wait(act, xr_loaded, lambda n: 32 * (n + 1), n, d)
                    ins = act.activation(z[:, :], misc, ACT.Identity, scale=prm_t[:, GA:GA + 1], bias=prm_t[:, GABO:GABO + 1])
                ins.then_inc(misc_drained, 1)

            def batch(b, d=None):
                for k in range(NH):
                    g, hh = divmod(k, GROUP)
                    s = NG * b + g
                    if hh == 0 and 0 <= s - 2 < NS:
                        wait(act, pv_ready, lambda b: NG * b + g - 1, b, d)
                        if s - 4 >= 0:
                            wait(act, misc_filled, lambda b: at["o", NG * b + g - 4] + 1, b, d)
                        act.copy(o_aug[g % 2][:, :], ps[:, PV_BANK, :]).then_inc(pv_taken, 1)
                    if 0 <= s < NS:
                        for t in range(QT):
                            wait(act, st_ready, lambda b: QT * (NH * b + k) + t + 1, b, d)
                            act.activation(probs[:, g % 2, hh, S * t:S * (t + 1)], ps[:, ST_BANK + turn(QT * k + t)[0], :],
                                           ACT.Exp, scale=SCALE).then_inc(exps_done, 1)
                    if k == 8 and b + 2 < NB:
                        normalise(b + 2, d, xa_loaded, misc_filled, "hT", at, xn_ready)
                    step = misc_at(b, k)
                    if step and step[0] in ("hT", "q", "k", "v", "oT", "y"):
                        misc_drain(*step, d)

            normalise(0, None, xa_loaded, misc_filled, "hT", at, xn_ready)
            misc_drain("hT", 0, None)
            misc_drain("q", 0, None)
            misc_drain("k", 0, None)
            for b in range(-1, FIRST):
                batch(b)
            with act.Fori(0, LOOP) as d:
                batch(FIRST, d)
                batch(FIRST + 1, d)
            for b in range(FIRST + 2 * LOOP, NB + 1):
                batch(b)

            act.wait_ge(var2_ready, 1)
            act.activation(rs4[:, 2, :], rs4[:, 1, :], ACT.Sqrt).then_inc(rstd2_ready, 1)

            def ffn_block(n, d=None):
                for ch in range(NC):
                    if 0 <= n < NB:
                        par = (n + ch) % 2
                        wait(act, g_ready, lambda n: NC * n + ch + 1, n, d)
                        wait(act, su_done, lambda n: NC * n + ch - 1, n, d)
                        act.activation(silu[par], ps[:, par, :], ACT.Silu).then_inc(silu_done, 1)
                    if ch == 1 and 0 <= n + 1 < NB:
                        normalise(n + 1, d, xb_loaded, misc2_filled, "h", at2, xn2_ready)
                    if ch == 2 and 0 <= n - 1:
                        wait(act, z_loaded, lambda n: 32 * n, n, d)
                        wait(act, down_done, lambda n: NC * n, n, d)
                        if n - 2 >= 0:
                            wait(act, misc2_filled, lambda n: at2["out", n - 2] + 1, n, d)
                        act.activation(z[:, :], ps[:, 5 + (n - 1) % 2, :], ACT.Identity, scale=prm_t[:, GB:GB + 1]
                                       ).then_inc(y_taken, 1)
                    if ch == 3 and 0 <= n + 1 < NB:
                        wait(act, misc2_filled, lambda n: at2["h", n + 1] + 1, n, d)
                        act.activation(h2_t[(n + 1) % 2], misc, ACT.Identity, scale=prm_a[:, CB:CB + 1], bias=prm_a[:, SB:SB + 1]
                                       ).then_inc(misc2_drained, 1)
                    if ch == 6 and 0 <= n + 1 < NB:
                        wait(act, margin_ready, lambda n: n + 2, n, d)
                        act.activation(top[:, 5, :], top[:, 4, :], ACT.Tanh, scale=0.5).then_inc(tanh_ready, 1)

            for n in range(-1, FIRST):
                ffn_block(n)
            with act.Fori(0, LOOP) as d:
                ffn_block(FIRST, d)
                ffn_block(FIRST + 1, d)
            for n in range(FIRST + 2 * LOOP, NB + 1):
                ffn_block(n)

        @block.vector
        def _(dve):
            steps = [0]

            def settled(ins):
                steps[0] += 1
                ins.then_inc(dve_step, 1)
                dve.wait_ge(dve_step, steps[0])

            def moments_to_rstd(asked, answered):
                settled(dve.tensor_scalar(rs4[:, 0, :], mv[:, :, 1], EPS, None, ALU.add))
                dve.reciprocal(rs4[:, 1, :], rs4[:, 0, :]).then_inc(asked, 1)
                dve.wait_ge(answered, 1)
                settled(dve.tensor_tensor(rs4[:, 3, :], rs4[:, 2, :], rs4[:, 2, :], ALU.mult))
                settled(dve.tensor_tensor(rs4[:, 3, :], rs4[:, 3, :], rs4[:, 0, :], ALU.mult))
                settled(dve.tensor_scalar(rs4[:, 3, :], rs4[:, 3, :], -0.5, 1.5, ALU.mult, ALU.add))
                rstd = prm[:, :, RSTD:RSTD + QT]
                settled(dve.tensor_tensor(rstd, rs4[:, 2, :].rearrange("p (b t) -> p b t", t=QT),
                                          rs4[:, 3, :].rearrange("p (b t) -> p b t", t=QT), ALU.mult))
                settled(dve.scalar_tensor_tensor(prm[:, :, NMR:NMR + QT], mv[:, :, 0].rearrange("p (b t) -> p b t", t=QT),
                                                 -1.0, rstd, ALU.mult, ALU.mult))

            for q in range(4):
                dve.wait_ge(x_all_loaded[q], 16)
                for t in range(NT // 4 * q, NT // 4 * (q + 1)):
                    ins = dve.bn_stats(st6[:, t, :], x_all[:, t, :])
                settled(ins)
                for t in range(NT // 4 * q, NT // 4 * (q + 1)):
                    ins = dve.bn_aggr(mv[:, t, :], st6[:, t, :])
            settled(ins)
            moments_to_rstd(var_ready, rstd_ready)
            dve.wait_ge(setup_drained, SETUP_MOD + 1)
            settled(dve.memset(prm[:, :, GB + 1:PRM], 0.0))
            for col, i, plus in ((SA, 0, 0.0), (CA, 1, 1.0), (SB, 3, 0.0), (CB, 4, 1.0)):
                settled(dve.tensor_scalar(prm[:, :, col], mod[:, i, :], plus, None, ALU.add))
            gates = mod[:, 2:6:3, :]
            sign, size, neg = gtmp[:, 0], gtmp[:, 1], gtmp[:, 2]
            settled(dve.tensor_scalar(sign, gates, 0.0, 2.0, ALU.is_ge, ALU.mult))
            settled(dve.tensor_scalar(sign, sign, -1.0, None, ALU.add))
            settled(dve.tensor_scalar(neg, gates, -1.0, None, ALU.mult))
            settled(dve.tensor_tensor(size, neg, gates, ALU.max))
            settled(dve.tensor_scalar(size, size, 0.25, None, ALU.max))
            settled(dve.tensor_tensor(prm[:, :, GA], sign[:, 0, :], size[:, 0, :], ALU.mult))
            settled(dve.tensor_tensor(prm[:, :, GB], sign[:, 1, :], size[:, 1, :], ALU.mult))
            dve.tensor_scalar(prm[:, :, GABO], prm[:, :, GA], bias[:, 3:4], None, ALU.mult).then_inc(prm_ready, 1)

            def misc_drain(kind, n, g, d):
                key = (lambda n: (kind, NG * n + g)) if kind in ("shift", "o") else (lambda n: (kind, n))
                if kind == "shift":
                    wait(dve, misc_filled, lambda n: at[key(n)] + 1, n, d)
                    wait(dve, shift_stacked, lambda n: 64 * (NG * n + g - 1), n, d)
                    dve.tensor_copy(shift_t[g % 2][:, :], misc_bf[0:8 * QT, 0:P]).then_inc(misc_drained, 1)
                elif kind == "o":
                    wait(dve, misc_filled, lambda n: at[key(n)] + 1, n, d)
                    v = misc.rearrange("p (t i e) -> p t i e", t=QT, i=GROUP)
                    dve.reciprocal(o_rs[:, :, :], v[:, :, :, DK]).then_inc(o_rs_ready, 1)
                    wait(dve, o_rs_ready, lambda n: NG * n + g + 1, n, d)
                    dve.tensor_tensor(o_n[:, :, GROUP * g:GROUP * (g + 1), :], v[:, :, :, 0:DK],
                                      o_rs[:, :, :].unsqueeze(3).to_broadcast([P, QT, GROUP, DK]), ALU.mult
                                      ).then_inc(misc_drained, 1)
                elif kind == "x1":
                    wait(dve, misc_filled, lambda n: at[key(n)] + 1, n, d)
                    wait(dve, xr_loaded, lambda n: 32 * (n + 1), n, d)
                    wait(dve, x1_stored, lambda n: 32 * n, n, d)
                    dve.tensor_tensor(x1_s[:, :, :].rearrange("p t d -> p (t d)"), misc,
                                      x_r[:, :, :].rearrange("p t d -> p (t d)"), ALU.add).then_inc(misc_drained, 1)
                    wait(dve, misc_drained, lambda n: at[key(n)] + 1, n, d)
                    for t in range(QT):
                        ins = dve.bn_stats(st_b[:, t, :], x1_s[:, t, :])
                    ins.then_inc(x1_stats, 1)

            def batch(b, d=None):
                for k in range(NH):
                    g, hh = divmod(k, GROUP)
                    s = NG * b + g
                    if k == 12 and 0 <= b - 1:
                        wait(dve, x1_stats, lambda b: b, b, d)
                    if 0 <= s + 2 < NS:
                        hs = hh ^ 1
                        for t in range(QT):
                            wait(dve, scores_ready, lambda b: 16 * (NG * b + g + 2) + 4 * hh + t + 1, b, d)
                            bank = turn(QT * (GROUP * ((g + 2) % NG) + hh) + t)[0]
                            dve.tensor_reduce(maxes[g % 2][:, hs % 2, hs // 2, t:t + 1], ps[:, S_BANK + bank, :],
                                              AX.X, ALU.max).then_inc(maxes_done, 1)
                        if hh == GROUP - 1:
                            wait(dve, maxes_done, lambda b: 16 * (NG * b + g + 3), b, d)
                            if s >= 0:
                                wait(dve, misc_filled, lambda b: at["shift", NG * b + g] + 1, b, d)
                            m = maxes[g % 2][:, :, :, :].rearrange("p a c q -> p a (c q)")
                            high, low = (shift[g % 2][:, :, i, :, :].rearrange("p a c q -> p a (c q)") for i in range(2))
                            dve.tensor_scalar(high, m, -1.0, None, ALU.mult).then_inc(shift_high, 1)
                            wait(dve, shift_high, lambda b: NG * b + g + 3, b, d)
                            dve.scalar_tensor_tensor(low, m, -1.0, high, ALU.mult, ALU.subtract).then_inc(shift_ready, 1)
                    if k == 12 and 0 <= b - 1:
                        for t in range(QT):
                            ins = dve.bn_aggr(mv_b[:, t, :], st_b[:, t, :])
                        ins.then_inc(stats_ready, 1)
                    step = misc_at(b, k)
                    if step and step[0] in ("shift", "o"):
                        misc_drain(step[0], step[1] // NG, step[1] % NG, d)
                    elif step and step[0] == "x1":
                        misc_drain(step[0], step[1], 0, d)

            for b in range(-1, FIRST):
                batch(b)
            with dve.Fori(0, LOOP) as d:
                batch(FIRST, d)
                batch(FIRST + 1, d)
            for b in range(FIRST + 2 * LOOP, NB + 1):
                batch(b)

            dve.wait_ge(mv_loaded, 16)
            dve.wait_ge(prm_stored, 16)
            moments_to_rstd(var2_ready, rstd2_ready)
            dve.nop().then_inc(prm2_ready, 1)

            def router(n, d):
                done = [0]

                def step(ins):
                    done[0] += 1
                    i = done[0]
                    ins.then_inc(route_step, 1)
                    wait(dve, route_step, lambda n: ROUTE_STEPS * n + i, n, d)

                def wide(v):
                    return top[:, v, :].unsqueeze(2).to_broadcast([P, QT, NE])

                scores, left, eq, one, gate, tmp = (route[:, i, :, :] for i in range(6))
                two = route[:, 6, :, :]
                for pick, src, v in ((one, scores, 0), (two, left, 1)):
                    step(dve.tensor_reduce(top[:, v, :], src, AX.X, ALU.max))
                    step(dve.tensor_tensor(eq, src, wide(v), ALU.is_equal))
                    step(dve.tensor_tensor(tmp, eq, rank[:, :, :], ALU.mult))
                    step(dve.tensor_reduce(top[:, 2, :], tmp, AX.X, ALU.max))
                    step(dve.tensor_tensor(pick, tmp, wide(2), ALU.is_equal))
                    if v == 0:
                        step(dve.scalar_tensor_tensor(left, pick, -3.0e38, src, ALU.mult, ALU.add))
                step(dve.tensor_tensor(top[:, 4, :], top[:, 0, :], top[:, 1, :], ALU.subtract))
                dve.nop().then_inc(margin_ready, 1)
                wait(dve, tanh_ready, lambda n: n + 1, n, d)
                step(dve.tensor_scalar(top[:, 6, :], top[:, 5, :], 0.5, 0.5, ALU.mult, ALU.add))
                step(dve.tensor_scalar(top[:, 7, :], top[:, 5, :], -0.5, 0.5, ALU.mult, ALU.add))
                step(dve.tensor_tensor(gate, one, wide(6), ALU.mult))
                step(dve.tensor_tensor(tmp, two, wide(7), ALU.mult))
                step(dve.tensor_tensor(gate, gate, tmp, ALU.add))
                step(dve.tensor_copy(gate_parts[:, :, 0, :], gate))
                step(dve.tensor_tensor(tmp, gate, gate_parts[:, :, 0, :], ALU.subtract))
                step(dve.tensor_copy(gate_parts[:, :, 1, :], tmp))
                step(dve.tensor_tensor(gate_parts[:, :, 2, :], tmp, gate_parts[:, :, 1, :], ALU.subtract))
                assert done[0] == ROUTE_STEPS

            def ffn_block(n, d=None):
                for ch in range(NC):
                    if 0 <= n < NB:
                        par = (n + ch) % 2
                        wait(dve, silu_done, lambda n: NC * n + ch + 1, n, d)
                        wait(dve, u_ready, lambda n: NC * n + ch + 1, n, d)
                        dve.tensor_tensor(su[par], silu[par], ps[:, 2 + par, :], ALU.mult).then_inc(su_done, 1)
                        wait(dve, su_done, lambda n: NC * n + ch + 1, n, d)
                        wait(dve, gate_ready, lambda n: NC * n + ch + 1, n, d)
                        before = {0: 1, 1: 1, 2: 4}.get(ch, 2)
                        wait(dve, down_done, lambda n: NC * n + ch - before, n, d)
                        dve.tensor_tensor(hid[ch % 3], su[par], ps[:, 4, :], ALU.mult).then_inc(hid_ready, 1)
                    if ch == 4 and 0 <= n + 1 < NB:
                        wait(dve, misc2_filled, lambda n: at2["route", n + 1] + 1, n, d)
                        dve.tensor_copy(route[:, 0, :, :].rearrange("p t e -> p (t e)"), misc[:, 0:QT * NE]
                                        ).then_inc(misc2_drained, 1)
                        wait(dve, misc2_drained, lambda n: at2["route", n + 1] + 1, n, d)
                        router(n + 1, d)
                    if ch == 6 and 0 <= n - 1:
                        wait(dve, misc2_filled, lambda n: at2["out", n - 1] + 1, n, d)
                        wait(dve, out_stored, lambda n: 16 * (n - 1), n, d)
                        wait(dve, z_loaded, lambda n: 32 * n, n, d)
                        dve.tensor_tensor(out_s[:, :, :].rearrange("p t d -> p (t d)"), misc,
                                          x_r[:, :, :].rearrange("p t d -> p (t d)"), ALU.add).then_inc(misc2_drained, 1)
                    if ch == 8 and 0 <= n + 1 < NB:
                        wait(dve, misc2_filled, lambda n: at2["gates", n + 1] + 1, n, d)
                        dve.tensor_copy(gate_t[(n + 1) % 2][:, :], misc_bf[0:3 * NE, 0:S]).then_inc(misc2_drained, 1)

            for n in range(-1, FIRST):
                ffn_block(n)
            with dve.Fori(0, LOOP) as d:
                ffn_block(FIRST, d)
                ffn_block(FIRST + 1, d)
            for n in range(FIRST + 2 * LOOP, NB + 1):
                ffn_block(n)

        @block.gpsimd
        def _(pool):
            pool.memset(ones_rows, 1.0).then_inc(ones_ready, 1)
            for i in range(2):
                for side in range(2):
                    pool.memset(q_st[i][side][SIDE * (1 - side):SIDE * (2 - side), :, :], 0.0).then_inc(zeros_ready, 1)
                    pool.wait_ge(zeros_ready, 2 * i + side + 1)
            for i in range(2):
                pool.memset(v_aug[i][:, :, :, DK + 1:VW], 0.0).then_inc(fills_done, 1)
                pool.memset(v_aug[i][:, :, :, DK:DK + 1], 1.0).then_inc(fills_done, 1)

            pool.wait_ge(consts_loaded, 16 * N_CONSTS)
            pool.tensor_copy(identb[:, :], ident[:, :]).then_inc(fills_done, 1)
            pool.tensor_copy(rows[:, :, :], rows_f[:, :, :]).then_inc(fills_done, 1)

            def split(kind, n, d):
                i = 0 if kind == "q" else 1
                full, parts, high, mid, low = (q32, q_parts, 0, 1, 2) if kind == "q" else (k32, k_parts, 1, 2, 0)
                wait(pool, misc_drained, lambda n: at[kind, n] + 1, n, d)
                pool.tensor_tensor(parts[:, mid, :], full[:, :], parts[:, high, :], ALU.subtract).then_inc(pool_step, 1)
                wait(pool, split_ready, lambda n: 2 * n + i, n, d)
                pool.tensor_tensor(rest[:, :], full[:, :], parts[:, high, :], ALU.subtract).then_inc(pool_step, 1)
                wait(pool, pool_step, lambda n: 4 * n + 2 * i + 2, n, d)
                pool.tensor_tensor(parts[:, low, :], rest[:, :], parts[:, mid, :], ALU.subtract).then_inc(split_ready, 1)

            def batch(b, d=None):
                if b + 1 < NB:
                    split("q", b + 1, d)
                    split("k", b + 1, d)

            for b in range(-1, FIRST):
                batch(b)
            with pool.Fori(0, LOOP) as d:
                batch(FIRST, d)
                batch(FIRST + 1, d)
            for b in range(FIRST + 2 * LOOP, NB + 1):
                batch(b)


_INS = ["L0_attn_x", "L0_attn_Wq", "L0_attn_bq", "L0_attn_Wk", "L0_attn_bk", "L0_attn_Wv", "L0_attn_bv",
        "L0_attn_Wo", "L0_attn_bo", "L0_ffn_gate_w", "L0_ffn_wg", "L0_ffn_wu", "L0_ffn_wd", "L0_c", "L0_wmod"]


def shape_constants():
    ident = np.eye(P, dtype=np.float32)
    unit_expert = np.arange(HID) // INTER
    rows = (unit_expert[None, :] == np.arange(3 * NE)[:, None] % NE).reshape(3 * NE, NC, P)
    rank = np.broadcast_to(np.arange(NE, 0, -1, dtype=np.float32), (P, QT, NE))
    return {"ident_c": ident, "rows_c": rows.astype(np.float32), "rank_c": np.ascontiguousarray(rank)}


def kernel(**inputs):
    import concourse.bacc as bacc
    from concourse.bass_utils import run_bass_kernel_spmd

    nc = bacc.Bacc("TRN2", target_bir_lowering=False, num_devices=1)
    arrays = {name: np.ascontiguousarray(inputs[name]) for name in _INS}
    arrays.update(shape_constants())
    args = [nc.dram_tensor(name, a.shape, mybir.dt.from_np(a.dtype), kind="ExternalInput").ap()
            for name, a in arrays.items()]
    args.append(nc.dram_tensor("out", (NB, S, D), F32, kind="ExternalOutput").ap())
    adaln_block(nc, *args)
    result = run_bass_kernel_spmd(nc, [arrays], core_ids=[0])
    return result.results[0]["out"]
```

```python
import math
from contextlib import ExitStack

import concourse.bass as bass
import numpy as np
from concourse import mybir

F32 = mybir.dt.float32
BF16 = mybir.dt.bfloat16
I32 = mybir.dt.int32
U32 = mybir.dt.uint32
ALU = mybir.AluOpType
ACT = mybir.ActivationFunctionType
AX = mybir.AxisListType

P = 128
NB, S, D = 16, 512, 128
NH, DK = 16, 8
NE, INTER = 8, 176
QT = S // P
NT = NB * QT
HID = NE * INTER
NC = HID // P
HALF = INTER // 2
EPS = 1e-5
SCALE = 1.0 / math.sqrt(DK)
PAIRS = NH // 2
GROUP = 4
NG = NH // GROUP
NS = NB * NG
TERMS = 6
SIDE = 64
SHIFT = TERMS * DK
VW = 32
STACK_DMAS = 18
PRM = 12
RSTD, NMR, CA, SA, GA, GABO = 0, 4, 8, 9, 10, 11
ST_BANK, S_BANK, PV_BANK, MISC_BANK = 0, 3, 6, 7
XT_BANK, GU_BANK, HT_BANK, Y_BANK = 0, 2, 4, 6
TURN = 3
SBB = 4
NSB = NB // SBB
FULL = SBB * QT
REGION = FULL + 1
REGIONS = NE + 1
TILES = 2 * SBB * QT + NE
SPARE = 8
X_ROWS = (NSB * REGIONS * REGION + SPARE) * P
NTILE = NSB * TILES
PAIR = 2 * TILES // SBB
NPAIR = NTILE // PAIR
SLOTS = 5
ROW_PAD = -SLOTS % 4
LAG = SBB // 2
ROW_C, ROW_S, ROW_KEEP, ROW_BASE, ROW_G, ROW_N = 0, D, 2 * D, 2 * D + 1, 2 * D + 1 + NE, 3 * D + 1 + NE
RT_P, RT_N, RT_ROW, RT_RANK, RT_COLS = 0, 2 * QT, 2 * QT + NE, 4 * QT + NE, 6 * QT + NE
MAP_TILE, MAP_TRI, MAP_THR, MAP_BASE, MAP_FROM, MAP_FILL = (sum((TILES, NE * NE, FULL, NTILE, NSB * NE)[:i]) for i in range(6))
MAP_N = MAP_FILL + NSB * NE + SPARE
ROOT_SEED = float(0x5F3759DF)
LN_STEPS, ROUTE_STEPS = 12, 23


def lin(f, n, d):
    if d is None:
        return f(n)
    assert f(n + 4) - f(n + 2) == f(n + 2) - f(n)
    return d * (f(n + 2) - f(n)) + f(n)


def wait(eng, sem, f, n, d):
    v = lin(f, n, d)
    if not isinstance(v, int) or v > 0:
        eng.wait_ge(sem, v)


def batch_of(n, d):
    return n if d is None else d * 2 + n


def turn(i):
    last = NH * QT - 1
    before = i - TURN if i >= TURN else max(j for j in range(last + 1) if j % TURN == i % TURN) - last - 1
    return i % TURN, i - before


def along(eng, sem, f, q, d):
    v = f(q) if d is None else d * (f(q + 1) - f(q)) + f(q)
    if not isinstance(v, int) or v > 0:
        eng.wait_ge(sem, v)


def misc_at(b, k, end):
    g, r = divmod(k, GROUP)
    s = NG * b + g
    if not end:
        step = {5: ("h2T", b - 2, NB), 9: ("score", b - 2, NB), 14: ("where", b - 2, NB)}.get(k)
    elif r == 0:
        step = ("shift", s + 1, NS)
    elif r == 1:
        step = ("o", s - 2, NS)
    else:
        step = {3: ("v", b + 1, NB), 6: ("hT", b + 2, NB), 7: ("oT", b - 1, NB), 10: ("y", b - 1, NB),
                11: ("x1", b - 1, NB), 14: ("q", b + 2, NB), 15: ("k", b + 2, NB)}.get(k)
    return step[:2] if step and 0 <= step[1] < step[2] else None


def misc_order():
    steps = [("hT", 0), ("q", 0), ("k", 0)]
    for b in range(-1, NB + 3):
        steps += [misc_at(b, k, end) for k in range(NH) for end in (0, 1) if misc_at(b, k, end)]
    return {step: i for i, step in enumerate(steps)}


def adaln_block(nc, x, Wq, bq, Wk, bk, Wv, bv, Wo, bo, gate_w, wg, wu, wd, c, wmod,
                ident_c, tri_c, rank_c, slots_c, map_c, out):
    with ExitStack() as ctx:
        def sb(name, shape, dt=F32):
            return ctx.enter_context(nc.sbuf_tensor(name, shape, dt))

        def sem(name):
            return ctx.enter_context(nc.semaphore(name))

        q_parts_d = nc.dram_tensor("q_parts_d", [NB, 3, P, S], BF16, kind="Internal").ap()
        k_parts_d = nc.dram_tensor("k_parts_d", [NB, 3, P, S], BF16, kind="Internal").ap()
        prm_d = nc.dram_tensor("prm_d", [NB, P, PRM], F32, kind="Internal").ap()
        row_d = nc.dram_tensor("row_d", [NB, ROW_N], F32, kind="Internal").ap()
        route_d = nc.dram_tensor("route_d", [NB, P, RT_COLS], F32, kind="Internal").ap()
        xs_d = nc.dram_tensor("xs_d", [X_ROWS, D], F32, kind="Internal").ap()
        ys_d = nc.dram_tensor("ys_d", [NTILE * P, D], F32, kind="Internal").ap()
        from_d = nc.dram_tensor("from_d", [NB, P, 2 * QT], U32, kind="Internal").ap()
        x1_d = nc.dram_tensor("x1_d", [NB, S, D], F32, kind="Internal").ap()

        ident = sb("ident", [P, P])
        identb = sb("identb", [P, P], BF16)
        tri = sb("tri", [P, P])
        ones = sb("ones", [P, P])
        zeros = sb("zeros", [P, D])
        maps = sb("maps", [1, MAP_N])
        rank = sb("rank", [P, QT, NE])
        w_t = sb("w_t", [P, 4, D])
        wqT, wkT, wvT, woT = (w_t[:, i, :] for i in range(4))
        bias = sb("bias", [P, 4])
        b_nat = sb("b_nat", [4, D])
        b_perm = sb("b_perm", [2, D])
        c_nat = sb("c_nat", [NB, D])
        c_silu = sb("c_silu", [NB, D])
        gw_nat = sb("gw_nat", [NE, D])
        gw_t = sb("gw_t", [P, NE])
        c_t = sb("c_t", [P, NB])
        wmod_s = sb("wmod_s", [P, 6 * D])
        mod = sb("mod", [P, 3, NB])
        gtmp = sb("gtmp", [P, 3, NB])
        mod_r = sb("mod_r", [NB, 3, D])
        row_s = sb("row_s", [NB, ROW_N])
        wg_t = sb("wg_t", [P, NC, P])
        wu_t = sb("wu_t", [P, NC, P])
        wd_t = sb("wd_t", [HALF, 2 * NE, D])
        prm = sb("prm", [P, NB, PRM])
        mv = sb("mv", [P, NT, 2])

        probs = sb("probs", [P, 2, GROUP, QT * S])
        x_all = probs[:, 0, :, :].rearrange("p a (t d) -> p (a t) d", d=D)
        ffn_nat = probs[:, 1, 0:3, 0:HID]
        ones_rows = probs[0:2, 1, 3, :].bitcast(BF16)
        w_nat = probs[:, 1, 0, HID:HID + 4 * D].rearrange("p (a d) -> p a d", d=D)
        st6 = probs[:, 1, 1, HID:HID + 6 * NT].rearrange("p (t k) -> p t k", k=6)
        rs4 = probs[:, 1, 1, HID + 6 * NT:HID + 10 * NT].rearrange("p (a t) -> p a t", t=NT)
        gtmp_r = probs[0:NB, 1, 2, HID:HID + 3 * D].rearrange("p (a d) -> p a d", d=D)
        q_st = [[sb(f"q_st{i}_{side}", [P, PAIRS, S], BF16) for side in range(2)] for i in range(2)]
        k_st = [sb(f"k_st{i}", [P, PAIRS, S], BF16) for i in range(2)]
        v_aug = [sb(f"v_aug{i}", [P, QT, NH, VW]) for i in range(2)]
        x_a = sb("x_a", [P, QT, D])
        prm_a = sb("prm_a", [P, PRM])
        x_n = sb("x_n", [P, QT, D])
        h_t = sb("h_t", [P, S])
        q32 = sb("q32", [P, S])
        k32 = sb("k32", [P, S])
        q_parts = sb("q_parts", [P, 3, S], BF16)
        k_parts = sb("k_parts", [P, 3, S], BF16)
        rest = sb("rest", [P, S])
        one = sb("one", [P, 1])
        maxes = [sb(f"maxes{i}", [P, 2, 2, QT]) for i in range(2)]
        shift = [sb(f"shift{i}", [P, 2, 2, 2, QT], BF16) for i in range(2)]
        shift_t = [sb(f"shift_t{i}", [4 * 2 * QT, P], BF16) for i in range(2)]
        o_aug = [sb(f"o_aug{i}", [P, S]) for i in range(2)]
        o_rs = sb("o_rs", [P, QT, GROUP])
        o_n = sb("o_n", [P, QT, NH, DK])
        o_t = sb("o_t", [P, S])
        z = sb("z", [P, S])
        x_r = sb("x_r", [P, QT, D])
        prm_t = sb("prm_t", [P, PRM])
        x1_s = sb("x1_s", [P, QT, D])
        st_b = sb("st_b", [P, QT, 6])
        mv_b = sb("mv_b", [P, QT, 2])
        ln2 = sb("ln2", [P, 4, QT])
        row = [sb(f"row{i}", [P, ROW_G]) for i in range(2)]
        h2 = [sb(f"h2_{i}", [P, QT, D]) for i in range(2)]
        h2_t = sb("h2_t", [P, S])
        route = sb("route", [P, 8, QT, NE])
        chosen = sb("chosen", [P, 2, QT, NE])
        top = sb("top", [P, 4, QT])
        odds = sb("odds", [P, 2, QT])
        before = sb("before", [P, 2, NE])
        route_o = sb("route_o", [P, RT_COLS])
        rows_o = sb("rows_o", [P, 2 * QT], U32)

        spare = probs[:, :, :, :].rearrange("p a b s -> p (a b s)")
        taken = [0]

        def part(n):
            taken[0] += n
            return spare[:, taken[0] - n:taken[0]]

        x_in = [part(D) for _ in range(SLOTS)]
        y_out = [part(D) for _ in range(SLOTS)]
        x_t = [part(P) for _ in range(2)]
        silu = [part(INTER) for _ in range(2)]
        hid = [part(INTER) for _ in range(2)]
        hid_t = [part(2 * P)[0:HALF] for _ in range(2)]
        picked = [[[part(D) for _ in range(2)] for _ in range(QT)] for _ in range(2)]
        x1_l = [part(S) for _ in range(2)]
        gate_l = [part(D) for _ in range(2)]
        route_l = [part(RT_COLS) for _ in range(2)]
        rows_l = [part(2 * QT).bitcast(U32) for _ in range(2)]
        out_s = [part(S) for _ in range(2)]
        route_all = part(NB * RT_COLS).rearrange("p (b k) -> p b k", k=RT_COLS)
        is_expert = part(NB * 2 * QT * NE)
        moves = part(NSB * NE)[0:1]
        rows_move = part(NB * 2 * QT)
        rows_from = part(NB * 2 * QT).bitcast(U32)
        counts = part(NSB * NE).rearrange("p (s e) -> p s e", e=NE)
        needs = part(NSB * NE * FULL)[0:1]
        need = part(NSB * NE)[0:1]
        uptos = part(NSB * NE * NE)[0:1]
        upto = part(NSB * NE)[0:1]
        done = part(NSB * TILES * NE)[0:1]
        owner = part(NTILE)[0:1]
        start = part(NTILE)[0:1]
        tile_row = part(ROW_PAD + NTILE + SLOTS)[0:1].bitcast(I32)
        tile_expert = part(4 + NTILE)[0:1].bitcast(I32)
        fill_row = part(NSB * NE + SPARE)[0:1].bitcast(I32)
        gone = sb("gone", [P, 1])

        ps = ctx.enter_context(nc.psum_tensor("ps", [P, 8, S], F32))
        misc = ps[:, MISC_BANK, :]
        misc_bf = misc.bitcast(BF16)

        consts_loaded = sem("consts_loaded")
        x_all_loaded = [sem(f"x_all_loaded{i}") for i in range(4)]
        ffn_loaded = sem("ffn_loaded")
        c_ready = sem("c_ready")
        setup_filled = sem("setup_filled")
        setup_drained = sem("setup_drained")
        fills_done = sem("fills_done")
        ones_ready = sem("ones_ready")
        one_ready = sem("one_ready")
        ones_stacked = sem("ones_stacked")
        zeros_ready = sem("zeros_ready")
        zeros_stacked = sem("zeros_stacked")
        dve_step = sem("dve_step")
        prm_ready = sem("prm_ready")
        prm_stored = sem("prm_stored")
        xa_loaded = sem("xa_loaded")
        xn_ready = sem("xn_ready")
        misc_filled = sem("misc_filled")
        misc_drained = sem("misc_drained")
        pool_step = sem("pool_step")
        split_ready = sem("split_ready")
        parts_stored = sem("parts_stored")
        stack_ready = sem("stack_ready")
        scores_ready = sem("scores_ready")
        maxes_done = sem("maxes_done")
        shift_high = sem("shift_high")
        shift_ready = sem("shift_ready")
        shift_stacked = sem("shift_stacked")
        st_ready = sem("st_ready")
        exps_done = sem("exps_done")
        pv_ready = sem("pv_ready")
        pv_taken = sem("pv_taken")
        o_rs_ready = sem("o_rs_ready")
        xr_loaded = sem("xr_loaded")
        x1_stats = sem("x1_stats")
        stats_ready = sem("stats_ready")
        x1_stored = sem("x1_stored")
        row_stored = sem("row_stored")
        row_loaded = [sem(f"row_loaded{i}") for i in range(2)]
        blank_stored = sem("blank_stored")
        ln_step = sem("ln_step")
        ln2_step = sem("ln2_step")
        h2_ready = sem("h2_ready")
        route_step = sem("route_step")
        odds_ready = sem("odds_ready")
        scattered = sem("scattered")
        route_stored = sem("route_stored")
        counts_loaded = sem("counts_loaded")
        counts_ready = sem("counts_ready")
        counts_summed = sem("counts_summed")
        map_ready = sem("map_ready")
        moves_ready = sem("moves_ready")
        moves_spread = sem("moves_spread")
        from_ready = sem("from_ready")
        from_stored = sem("from_stored")
        filled = sem("filled")
        x_loaded = [sem(f"x_loaded{i}") for i in range(SLOTS)]
        y_stored = [sem(f"y_stored{i}") for i in range(SLOTS)]
        xt_ready = sem("xt_ready")
        xt_taken = sem("xt_taken")
        gu_ready = sem("gu_ready")
        silu_done = sem("silu_done")
        hid_ready = sem("hid_ready")
        hidt_ready = sem("hidt_ready")
        hidt_taken = sem("hidt_taken")
        y_ready = sem("y_ready")
        y_taken = sem("y_taken")
        sums_loaded = [sem(f"sums_loaded{i}") for i in range(2)]
        gone_step = sem("gone_step")
        gathered = [[sem(f"gathered{i}_{t}") for t in range(QT)] for i in range(2)]
        sum_step = sem("sum_step")
        out_stored = [sem(f"out_stored{i}") for i in range(2)]

        at = misc_order()
        N_CONSTS = 16
        SETUP_W, SETUP_GC, SETUP_MOD, SETUP_FFN = 0, 1, 2, 3
        FFN_GROUPS = ([(w, c0, min(4, NC - c0), P) for w in range(2) for c0 in range(0, NC, 4)]
                      + [(2, c0, 4, HALF) for c0 in range(0, 2 * NE, 4)])
        N_SETUP = SETUP_FFN + len(FFN_GROUPS)
        FIRST, LOOP = 4, (NB - 6) // 2

        block = ctx.enter_context(nc.Block())

        @block.sync
        def _(sp):
            def load_const(dst, src):
                sp.dma_start(dst, src).then_inc(consts_loaded, 16)

            load_const(ident[:, :], ident_c)
            load_const(c_nat[:, :], c)
            for q in range(4):
                n = NT // 4
                sp.dma_start(x_all[:, n * q:n * (q + 1), :],
                             x.rearrange("b (t p) d -> p (b t) d", p=P)[:, n * q:n * (q + 1), :]
                             ).then_inc(x_all_loaded[q], 16)
                if q == 0:
                    for i, w in enumerate((Wq, Wk, Wv, Wo)):
                        load_const(w_nat[:, i, :], w)
                    load_const(wmod_s[:, :], wmod)
                    load_const(gw_nat[:, :], gate_w)
                    for i, v in enumerate((bq, bk, bv, bo)):
                        load_const(b_nat[i:i + 1, :], v.rearrange("(o n) -> o n", o=1))
                    load_const(rank[:, :, :], rank_c)
                    load_const(tri[:, :], tri_c)
                    load_const(row_s[:, ROW_KEEP:ROW_G], slots_c)
                    load_const(maps[:, :], map_c)
            sp.dma_start(ffn_nat[:, 0, :].rearrange("p (k d) -> p k d", d=D),
                         wg.rearrange("e i d -> (e i) d").rearrange("(k p) d -> p k d", p=P)).then_inc(ffn_loaded, 16)
            sp.dma_start(ffn_nat[:, 1, :].rearrange("p (k d) -> p k d", d=D),
                         wu.rearrange("e i d -> (e i) d").rearrange("(k p) d -> p k d", p=P)).then_inc(ffn_loaded, 16)
            sp.dma_start(ffn_nat[:, 2, :].rearrange("p (e i) -> p e i", e=NE),
                         wd.rearrange("e d i -> d e i")).then_inc(ffn_loaded, 16)
            sp.wait_ge(ones_ready, 1)
            for i in range(2):
                for side in range(2):
                    r0 = SIDE * side + SHIFT
                    sp.dma_start(k_st[i][r0:r0 + 2, :, :], ones_rows.rearrange("p (j s) -> p j s", s=S)
                                 ).then_inc(ones_stacked, 16)
            sp.wait_ge(prm_ready, 1)
            sp.dma_start(prm_d.rearrange("b p k -> p b k"), prm[:, :, :]).then_inc(prm_stored, 16)
            sp.dma_start(row_d, row_s[:, :]).then_inc(row_stored, 16)
            sp.wait_ge(prm_stored, 16)
            sp.wait_ge(row_stored, 16)

            sp.wait_ge(zeros_ready, 4)
            sp.wait_ge(one_ready, 2)
            for i in range(2):
                for side in range(2):
                    unused = slice(SIDE * side + SHIFT + 2, SIDE * (side + 1))
                    for st in (q_st[i][side], k_st[i]):
                        sp.dma_start(st[unused, :, :], q_st[i][1 - side][unused, :, :]).then_inc(zeros_stacked, 16)
            for i in range(NSB):
                r0 = (i * REGIONS + NE) * REGION * P
                sp.dma_start(xs_d[r0:r0 + NE * P, :].rearrange("(t p) d -> p t d", p=P),
                             zeros[:, :].unsqueeze(1).to_broadcast([P, NE, D])).then_inc(blank_stored, 16)

            def load_x_a(n, d):
                wait(sp, misc_drained, lambda n: at["hT", n - 1] + 1 if n else 0, n, d)
                b = batch_of(n, d)
                sp.dma_start(x_a[:, :, :], x[b].rearrange("(t p) d -> p t d", p=P)).then_inc(xa_loaded, 16)
                sp.dma_start(prm_a[:, :], prm_d[b]).then_inc(xa_loaded, 16)

            def load_x_r(n, d):
                wait(sp, misc_drained, lambda n: at["x1", n - 1] + 1 if n else 0, n, d)
                b = batch_of(n, d)
                sp.dma_start(x_r[:, :, :], x[b].rearrange("(t p) d -> p t d", p=P)).then_inc(xr_loaded, 16)
                sp.dma_start(prm_t[:, :], prm_d[b]).then_inc(xr_loaded, 16)

            def stack_shift(b, g, d):
                wait(sp, misc_drained, lambda b: at["shift", NG * b + g] + 1, b, d)
                for side in range(2):
                    for part in range(2):
                        row = SIDE * side + SHIFT + part
                        src = 2 * QT * (2 * side + part)
                        sp.dma_start(q_st[b % 2][side][row:row + 1, 2 * g:2 * g + 2, :],
                                     shift_t[g % 2][src:src + 2 * QT, :]).then_inc(shift_stacked, 16)

            def store_parts(i, n, d):
                b = batch_of(n, d)
                parts, dram = ((q_parts, q_parts_d), (k_parts, k_parts_d))[i]
                wait(sp, split_ready, lambda n: 2 * n + i + 1, n, d)
                sp.dma_start(dram[b].rearrange("t r s -> r t s"), parts[:, :, :]).then_inc(parts_stored, 16)

            def load_stacks(n, d):
                b = batch_of(n, d)
                wait(sp, parts_stored, lambda n: 32 * (n + 1), n, d)
                if d is None and n <= 1:
                    sp.wait_ge(ones_stacked, 64)
                    sp.wait_ge(zeros_stacked, 128)
                for side in range(2):
                    lo, hi = SIDE * side, SIDE * (side + 1)
                    sp.dma_start(q_st[n % 2][side][lo + SHIFT:lo + SHIFT + 2, :, :],
                                 q_st[n % 2][1 - side][lo + SHIFT:lo + SHIFT + 2, :, :]).then_inc(stack_ready, 16)
                    for u in range(TERMS // 2):
                        dst = slice(lo + 2 * DK * u, lo + 2 * DK * (u + 1))
                        for st, dram, parts in ((q_st[n % 2][side], q_parts_d, ((0, 0), (1, 1), (0, 2))[u]),
                                                (k_st[n % 2], k_parts_d, ((1, 2), (1, 2), (0, 1))[u])):
                            first, second = parts
                            if first == second:
                                for t in range(2):
                                    sp.dma_start(st[lo + DK * (2 * u + t):lo + DK * (2 * u + t + 1), :, :],
                                                 dram[b, first, lo:hi, :].rearrange("(e j) s -> e j s", e=DK)
                                                 ).then_inc(stack_ready, 16)
                            else:
                                src = dram[b, first:second + 1:second - first, lo:hi, :]
                                sp.dma_start(st[dst, :, :].rearrange("p j s -> p (j s)"),
                                             src.rearrange("t (e j) s -> t e (j s)", e=DK)).then_inc(stack_ready, 16)

            def store_x1(n, d):
                wait(sp, misc_drained, lambda n: at["x1", n] + 1, n, d)
                b = batch_of(n, d)
                sp.dma_start(x1_d[b].rearrange("(t p) d -> p t d", p=P), x1_s[:, :, :]).then_inc(x1_stored, 16)

            def load_row(n, d):
                wait(sp, route_step, lambda n: ROUTE_STEPS * (n - 1), n, d)
                b = batch_of(n, d)
                sp.dma_start(row[n % 2][:, :], row_d[bass.ds(b, 1), 0:ROW_G].to_broadcast([P, ROW_G])
                             ).then_inc(row_loaded[n % 2], 16)

            def store_route(n, d):
                wait(sp, route_step, lambda n: ROUTE_STEPS * (n + 1), n, d)
                b = batch_of(n, d)
                sp.dma_start(route_d[b], route_o[:, :]).then_inc(route_stored, 16)

            def batch(b, d=None):
                if b + 2 < NB:
                    load_x_a(b + 2, d)
                if 0 <= b < NB:
                    stack_shift(b, 1, d)
                if b + 1 < NB:
                    store_parts(1, b + 1, d)
                    load_stacks(b + 1, d)
                if 0 <= b - 1 < NB:
                    load_x_r(b - 1, d)
                if 0 <= b < NB:
                    stack_shift(b, 2, d)
                if 0 <= b - 3 < NB:
                    store_route(b - 3, d)
                if 0 <= b < NB:
                    stack_shift(b, 3, d)
                if b + 1 < NB:
                    stack_shift(b + 1, 0, d)
                if 0 <= b - 1 < NB:
                    store_x1(b - 1, d)
                    load_row(b - 1, d)
                if b + 2 < NB:
                    store_parts(0, b + 2, d)

            load_x_a(0, None)
            store_parts(0, 0, None)
            for b in range(-1, FIRST):
                batch(b)
            with sp.Fori(0, LOOP) as d:
                batch(FIRST, d)
                batch(FIRST + 1, d)
            for b in range(FIRST + 2 * LOOP, NB + 3):
                batch(b)

            sp.wait_ge(route_stored, 16 * NB)
            sp.dma_start(route_all, route_d.rearrange("b p k -> p b k")).then_inc(counts_loaded, 16)
            sp.wait_ge(map_ready, 1)

            def values(table, at, n, d, step, high):
                place = slice(at, at + n) if d is None else bass.ds(d * step + at, n)
                return nc.values_load_multi_w_load_instructions(
                    table[:, place], engines=[mybir.EngineType.SP], min_val=0, max_val=high,
                    skip_runtime_bounds_check_because="a place within its expert's region, or behind its last row")[1]

            def fill(n, q=0, d=None, first=0):
                rows = values(fill_row, first, n, d, QT, X_ROWS - P)
                if first:
                    along(sp, filled, lambda q: 16 * (NE + QT * (q + 1)), q, d)
                for r0 in rows:
                    sp.dma_start(xs_d[bass.ds(r0, P), :], zeros[:, :]).then_inc(filled, 16)

            def load_tile(m, q, d, row):
                along(sp, xt_ready, lambda q: PAIR * q + m + 1 - SLOTS, q, d)
                sp.dma_start(x_in[m % SLOTS], xs_d[bass.ds(row, P), :]).then_inc(x_loaded[m % SLOTS], 16)

            def store_tile(m, q, d):
                i = PAIR * q + m
                y_written = PAIR * q + m + 1 if d is None else sp.snap(d * PAIR + (PAIR * q + m + 1))
                if 0 <= m < SLOTS and q >= LAG:
                    along(sp, y_stored[m], lambda q: 16 * PAIR // SLOTS * q, q, d)
                sp.wait_ge(y_taken, y_written)
                sp.dma_start(ys_d[bass.ds(i * P if d is None else d * (PAIR * P) + i * P, P), :], y_out[m % SLOTS]).then_inc(y_stored[m % SLOTS], 16)

            def load_sums(j, q, d):
                along(sp, sum_step, lambda q: 32 * (q - LAG - 1) + 16 * (j + 1), q, d)
                n = 2 * (q - LAG) + j
                b = n if d is None else d * 2 + n
                sp.dma_start(route_l[j], route_d[b]).then_inc(sums_loaded[j], 16)
                sp.dma_start(rows_l[j], from_d[b]).then_inc(sums_loaded[j], 16)
                sp.dma_start(x1_l[j].rearrange("p (t d) -> p t d", d=D), x1_d[b].rearrange("(t p) d -> p t d", p=P)
                             ).then_inc(sums_loaded[j], 16)
                sp.dma_start(gate_l[j], row_d[bass.ds(b, 1), ROW_G:ROW_N].to_broadcast([P, D])).then_inc(sums_loaded[j], 16)

            def store_out(j, q, d):
                along(sp, sum_step, lambda q: 32 * (q - LAG) + 16 * (j + 1), q, d)
                n = 2 * (q - LAG) + j
                b = n if d is None else d * 2 + n
                sp.dma_start(out[b].rearrange("(t p) d -> p t d", p=P), out_s[j].rearrange("p (t d) -> p t d", d=D)
                             ).then_inc(out_stored[j], 16)

            def pair(q, d=None):
                for m in range(PAIR):
                    if m % 4 == 0 and PAIR * q + m < NTILE:
                        rows = values(tile_row, ROW_PAD + PAIR * q + m + SLOTS, 4, d, PAIR, X_ROWS - P)
                    if m == 0 and q < NPAIR - 1:
                        fill(QT, q, d, NE + QT * (q + 1))
                    if m == 3 and 0 <= q - 1 - LAG < NPAIR:
                        store_out(0, q - 1, d)
                    if m == 8 and LAG <= q < NPAIR + LAG:
                        load_sums(0, q, d)
                    if m == 11 and 0 <= q - 1 - LAG < NPAIR:
                        store_out(1, q - 1, d)
                    if m == 12 and LAG <= q < NPAIR + LAG:
                        load_sums(1, q, d)
                    if PAIR * q + m + SLOTS < NTILE:
                        load_tile(m + SLOTS, q, d, rows[m % 4])
                    if 0 <= PAIR * q + m - 3 < NTILE:
                        store_tile(m - 3, q, d)
                    elif 3 <= m < 3 + SLOTS and q == NPAIR:
                        sp.wait_ge(y_stored[m - 3], 16 * PAIR // SLOTS * q)

            fill(NE + QT)
            sp.wait_ge(blank_stored, 16 * NSB)
            sp.wait_ge(scattered, 16 * 2 * NT)
            rows = values(tile_row, ROW_PAD, SLOTS, None, 0, X_ROWS - P)
            sp.wait_ge(filled, 16 * (NE + QT))
            for m in range(SLOTS):
                load_tile(m, 0, None, rows[m])
            sp.wait_ge(from_ready, 1)
            sp.dma_start(from_d.rearrange("b p k -> p b k"), rows_from.rearrange("p (b k) -> p b k", k=2 * QT)
                         ).then_inc(from_stored, 16)
            for q in range(LAG + 1):
                if q == LAG:
                    sp.wait_ge(from_stored, 16)
                pair(q)
            with sp.Fori(0, NPAIR - LAG - 2) as d:
                pair(LAG + 1, d)
            for q in range(NPAIR - 1, NPAIR + LAG + 1):
                pair(q)
            for j in range(2):
                sp.wait_ge(out_stored[j], 16 * NPAIR)

        @block.tensor
        def _(pe):
            def setup_bank(i):
                if i >= 2:
                    pe.wait_ge(setup_drained, i - 1)
                return ps[:, i % 2, :]

            pe.wait_ge(consts_loaded, 16 * N_CONSTS)
            bank = setup_bank(SETUP_W)
            for i in range(4):
                mm = pe.transpose(bank[:, P * i:P * (i + 1)], w_nat[:, i, :], ident[:, :])
            mm.then_inc(setup_filled, 1)
            bank = setup_bank(SETUP_GC)
            pe.transpose(bank[:, 0:NE], gw_nat[:, :], ident[0:NE, 0:NE])
            pe.wait_ge(c_ready, 2)
            pe.transpose(bank[:, NE:NE + NB], c_silu[:, :], ident[0:NB, 0:NB])
            pe.transpose(bank[:, 32:36], b_nat[:, :], ident[0:4, 0:4])
            pe.transpose(bank[:, 36:38], b_perm[:, :], ident[0:2, 0:2]).then_inc(setup_filled, 1)
            bank = setup_bank(SETUP_MOD)
            pe.wait_ge(setup_drained, SETUP_GC + 1)
            for i in range(3):
                pe.matmul(bank[:, NB * i:NB * (i + 1)], wmod_s[:, D * i:D * (i + 1)], c_t[:, :], start=True, stop=True)
            pe.matmul(bank[0:NB, D:4 * D], c_t[:, :], wmod_s[:, 3 * D:6 * D], start=True, stop=True).then_inc(setup_filled, 1)
            pe.wait_ge(ffn_loaded, 48)
            for i, (w, c0, n, width) in enumerate(FFN_GROUPS):
                bank = setup_bank(SETUP_FFN + i)
                for m in range(n):
                    mm = pe.transpose(bank[0:width, P * m:P * (m + 1)],
                                      ffn_nat[:, w, width * (c0 + m):width * (c0 + m + 1)], ident[:, :])
                mm.then_inc(setup_filled, 1)
            pe.wait_ge(setup_drained, N_SETUP)
            pe.wait_ge(fills_done, 6)

            def misc_step(kind, n, g, d):
                key = (lambda n: (kind, NG * n + g)) if kind in ("shift", "o") else (lambda n: (kind, n))
                wait(pe, misc_drained, lambda n: at[key(n)], n, d)
                if kind == "hT":
                    wait(pe, xn_ready, lambda n: n + 1, n, d)
                    for t in range(QT):
                        mm = pe.transpose(misc[:, P * t:P * (t + 1)], x_n[:, t, :], ident[:, :])
                elif kind == "q":
                    mm = pe.matmul(misc, wqT, h_t[:, :], start=True, stop=True)
                elif kind == "k":
                    mm = pe.matmul(misc, wkT, h_t[:, :], start=True, stop=True)
                elif kind == "v":
                    for t in range(QT):
                        mm = pe.matmul(misc[:, P * t:P * (t + 1)], h_t[:, P * t:P * (t + 1)], wvT,
                                       start=True, stop=True)
                elif kind == "shift":
                    wait(pe, shift_ready, lambda n: NG * n + g + 1, n, d)
                    mm = pe.transpose(misc_bf[0:8 * QT, 0:P],
                                      shift[g % 2][:, :, :, :, :].rearrange("p a b c q -> p (a b c q)"), identb[:, :])
                elif kind == "o":
                    wait(pe, pv_taken, lambda n: NG * n + g + 1, n, d)
                    for t in range(QT):
                        mm = pe.transpose(misc[:, P * t:P * (t + 1)], o_aug[g % 2][:, P * t:P * (t + 1)], ident[:, :])
                elif kind == "oT":
                    for t in range(QT):
                        mm = pe.transpose(misc[:, P * t:P * (t + 1)],
                                          o_n[:, t, :, :].rearrange("p h e -> p (h e)"), ident[:, :])
                elif kind == "y":
                    mm = pe.matmul(misc, woT, o_t[:, :], start=True, stop=True)
                elif kind == "x1":
                    for t in range(QT):
                        mm = pe.transpose(misc[:, P * t:P * (t + 1)], z[:, P * t:P * (t + 1)], ident[:, :])
                elif kind == "h2T":
                    wait(pe, h2_ready, lambda n: n + 1, n, d)
                    for t in range(QT):
                        mm = pe.transpose(misc[:, P * t:P * (t + 1)], h2[n % 2][:, t, :], ident[:, :])
                elif kind == "score":
                    for t in range(QT):
                        mm = pe.matmul(misc[:, NE * t:NE * (t + 1)], h2_t[:, P * t:P * (t + 1)], gw_t[:, :],
                                       start=True, stop=True)
                elif kind == "where":
                    wait(pe, route_step, lambda n: ROUTE_STEPS * n + 13, n, d)
                    either = route[:, 7, :, :]
                    pe.matmul(misc[:, 0:QT * NE], tri[:, :], either.rearrange("p t e -> p (t e)"), start=True, stop=False)
                    for t in range(QT - 1):
                        pe.matmul(misc[:, NE * (t + 1):QT * NE], ones[:, :],
                                  either[:, t:t + 1, :].to_broadcast([P, QT - 1 - t, NE]), start=False, stop=False)
                    mm = pe.matmul(misc[:, 0:QT * NE], ones[:, :], before[:, 0:1, :].to_broadcast([P, QT, NE]),
                                   start=False, stop=True)
                mm.then_inc(misc_filled, 1)

            def misc_steps(b, k, end, d):
                step = misc_at(b, k, end)
                if step:
                    kind, n = step
                    if kind in ("shift", "o"):
                        misc_step(kind, n // NG, n % NG, d)
                    else:
                        misc_step(kind, n, 0, d)

            def batch(b, d=None):
                for k in range(NH):
                    g, hh = divmod(k, GROUP)
                    s = NG * b + g
                    exps, looks = 0 <= s < NS, 0 <= s + 2 < NS
                    side, j = hh % 2, 2 * g + hh // 2
                    hs, gs, bs = hh ^ 1, (g + 2) % NG, b + (g + 2) // NG
                    side_s, js = hs % 2, 2 * gs + hs // 2
                    for t in range(QT):
                        if exps:
                            if hh == 0 and t == 0:
                                wait(pe, shift_stacked, lambda b: 64 * (NG * b + g + 1), b, d)
                            bank, ago = turn(QT * k + t)
                            wait(pe, exps_done, lambda b: QT * (NH * b + k) + t + 1 - ago, b, d)
                            pe.matmul(ps[:, ST_BANK + bank, :], k_st[b % 2][:, j, P * t:P * (t + 1)],
                                      q_st[b % 2][side][:, j, :], start=True, stop=True).then_inc(st_ready, 1)
                        if looks:
                            if k == 8 and t == 0:
                                wait(pe, stack_ready, lambda b: 16 * STACK_DMAS * (b + 2), b, d)
                            bank, ago = turn(QT * (GROUP * gs + hh) + t)
                            wait(pe, maxes_done, lambda b: 16 * (NG * b + g + 2) + 4 * hh + t + 1 - ago, b, d)
                            pe.matmul(ps[:, S_BANK + bank, :], q_st[bs % 2][side_s][:, js, P * t:P * (t + 1)],
                                      k_st[bs % 2][:, js, :], start=True, stop=True).then_inc(scores_ready, 1)
                        if t == 1:
                            misc_steps(b, k, 0, d)
                    if 0 <= s - 1 < NS:
                        gp, bp = (g - 1) % NG, b + (g - 1) // NG
                        if hh == 0:
                            wait(pe, exps_done, lambda b: 16 * (NG * b + g), b, d)
                            wait(pe, pv_taken, lambda b: NG * b + g - 1, b, d)
                            if gp == 0:
                                wait(pe, misc_drained, lambda b: at["v", b] + 1, b, d)
                        for i in range(GROUP):
                            mm = pe.matmul(ps[VW * i:VW * (i + 1), PV_BANK, :], v_aug[bp % 2][:, hh, GROUP * gp + i, :],
                                           probs[:, gp % 2, i, S * hh:S * (hh + 1)], start=(hh == 0), stop=(hh == QT - 1))
                        if hh == QT - 1:
                            mm.then_inc(pv_ready, 1)
                    misc_steps(b, k, 1, d)

            misc_step("hT", 0, 0, None)
            misc_step("q", 0, 0, None)
            misc_step("k", 0, 0, None)
            for b in range(-1, FIRST):
                batch(b)
            with pe.Fori(0, LOOP) as d:
                batch(FIRST, d)
                batch(FIRST + 1, d)
            for b in range(FIRST + 2 * LOOP, NB + 3):
                batch(b)

            pe.wait_ge(counts_ready, 1)
            pe.matmul(ps[0:1, 0, 0:NSB * NE], ones[:, 0:1], counts.rearrange("p s e -> p (s e)"), start=True, stop=True
                      ).then_inc(counts_summed, 1)
            pe.wait_ge(moves_ready, 1)
            pe.matmul(ps[:, 1, 0:NSB * NE], ones[0:1, :], moves, start=True, stop=True).then_inc(moves_spread, 1)
            pe.wait_ge(from_ready, 1)

            def turn_rows(m, q, d):
                along(pe, x_loaded[m % SLOTS], lambda q: 16 * ((PAIR * q + m) // SLOTS + 1), q, d)
                along(pe, xt_taken, lambda q: PAIR * q + m - 1, q, d)
                pe.transpose(ps[:, XT_BANK + m % 2, 0:P], x_in[m % SLOTS], ident[:, :]).then_inc(xt_ready, 1)

            def up(m, q, d, e):
                along(pe, xt_taken, lambda q: PAIR * q + m + 1, q, d)
                along(pe, hid_ready, lambda q: PAIR * q + m - 1, q, d)
                for i, w in enumerate((wg_t, wu_t)):
                    mm = pe.matmul(ps[:, GU_BANK + m % 2, INTER * i:INTER * (i + 1)], x_t[m % 2],
                                   w[:, :, :].rearrange("p c h -> p (c h)")[:, bass.ds(e * INTER, INTER)],
                                   start=True, stop=True)
                mm.then_inc(gu_ready, 1)

            def turn_hidden(m, q, d):
                along(pe, hid_ready, lambda q: PAIR * q + m + 1, q, d)
                along(pe, hidt_taken, lambda q: PAIR * q + m - 1, q, d)
                for i in range(2):
                    mm = pe.transpose(ps[0:HALF, HT_BANK + m % 2, P * i:P * (i + 1)], hid[m % 2][:, HALF * i:HALF * (i + 1)],
                                      ident[:, :])
                mm.then_inc(hidt_ready, 1)

            def down(m, q, d, e):
                along(pe, hidt_taken, lambda q: PAIR * q + m + 1, q, d)
                along(pe, y_taken, lambda q: PAIR * q + m - 1, q, d)
                for i in range(2):
                    mm = pe.matmul(ps[:, Y_BANK + m % 2, 0:D], hid_t[m % 2][:, P * i:P * (i + 1)],
                                   wd_t[:, bass.ds(e * 2 + i, 1), :].rearrange("p a d -> p (a d)"),
                                   start=(i == 0), stop=(i == 1))
                mm.then_inc(y_ready, 1)

            def pair(q, d=None):
                experts = {}

                def read_experts(m):
                    at = PAIR * q + m + 4
                    place = slice(at, at + 4) if d is None else bass.ds(d * PAIR + at, 4)
                    experts.update(zip(range(m, m + 4), nc.values_load_multi_w_load_instructions(
                        tile_expert[:, place], engines=[mybir.EngineType.PE], min_val=0, max_val=NE - 1,
                        skip_runtime_bounds_check_because="a count of at most NE experts, limited to NE - 1")[1]))

                if PAIR * q < NTILE:
                    read_experts(0)
                for m in range(PAIR):
                    i = PAIR * q + m
                    if i + 1 < NTILE:
                        turn_rows(m + 1, q, d)
                    if i < NTILE:
                        up(m, q, d, experts[m])
                        if m % 4 == 2 and m + 2 < PAIR:
                            read_experts(m + 2)
                    if m == 0 and i:
                        read_experts(-4)
                    if 0 <= i - 1 < NTILE:
                        turn_hidden(m - 1, q, d)
                    if 0 <= i - 2 < NTILE:
                        down(m - 2, q, d, experts[m - 2])

            turn_rows(0, 0, None)
            for q in range(LAG + 1):
                pair(q)
            with pe.Fori(0, NPAIR - LAG - 2) as d:
                pair(LAG + 1, d)
            for q in range(NPAIR - 1, NPAIR + 1):
                pair(q)

        @block.scalar
        def _(act):
            act.wait_ge(consts_loaded, 16 * N_CONSTS)
            act.activation(c_silu[:, :], c_nat[:, :], ACT.Silu).then_inc(c_ready, 1)
            act.copy(b_perm[:, :].rearrange("p (h e j) -> p j h e", h=2, e=DK),
                     b_nat[0:2, :].rearrange("p (j h e) -> p j h e", h=2, e=DK)).then_inc(c_ready, 1)
            act.wait_ge(setup_filled, SETUP_W + 1)
            bank = ps[:, SETUP_W % 2, :]
            for i in range(2):
                act.copy(w_t[:, i, :].rearrange("p (h e j) -> p j h e", h=2, e=DK),
                         bank[:, P * i:P * (i + 1)].rearrange("p (j h e) -> p j h e", h=2, e=DK))
            act.copy(w_t[:, 2:4, :].rearrange("p a d -> p (a d)"), bank[:, 2 * P:4 * P]).then_inc(setup_drained, 1)
            act.wait_ge(setup_filled, SETUP_GC + 1)
            bank = ps[:, SETUP_GC % 2, :]
            act.copy(gw_t[:, :], bank[:, 0:NE])
            act.copy(bias[:, 2:4], bank[:, 34:36])
            act.copy(bias[:, 0:2], bank[:, 36:38])
            act.copy(c_t[:, :], bank[:, NE:NE + NB]).then_inc(setup_drained, 1)
            act.wait_ge(setup_filled, SETUP_MOD + 1)
            act.copy(mod[:, :, :].rearrange("p a b -> p (a b)"), ps[:, SETUP_MOD % 2, 0:3 * NB])
            act.copy(mod_r[:, :, :].rearrange("p a d -> p (a d)"), ps[0:NB, SETUP_MOD % 2, D:4 * D]).then_inc(setup_drained, 1)
            for i, (w, c0, n, width) in enumerate(FFN_GROUPS):
                act.wait_ge(setup_filled, SETUP_FFN + i + 1)
                act.copy((wg_t, wu_t, wd_t)[w][:, c0:c0 + n, :].rearrange("p k d -> p (k d)"),
                         ps[0:width, (SETUP_FFN + i) % 2, 0:P * n]).then_inc(setup_drained, 1)

            def normalise(n, d, tiles):
                if tiles[0] == 0:
                    wait(act, xa_loaded, lambda n: 32 * (n + 1), n, d)
                    wait(act, misc_filled, lambda n: at["hT", n - 1] + 1 if n else 0, n, d)
                for t in tiles:
                    ins = act.activation(x_n[:, t, :], x_a[:, t, :], ACT.Identity,
                                         scale=prm_a[:, RSTD + t:RSTD + t + 1], bias=prm_a[:, NMR + t:NMR + t + 1])
                if tiles[-1] == QT - 1:
                    ins.then_inc(xn_ready, 1)

            def misc_drain(kind, n, d):
                wait(act, misc_filled, lambda n: at[kind, n] + 1, n, d)
                if kind == "hT":
                    ins = act.activation(h_t[:, :], misc, ACT.Identity, scale=prm_a[:, CA:CA + 1], bias=prm_a[:, SA:SA + 1])
                elif kind in ("q", "k"):
                    full, i = (q32, 0) if kind == "q" else (k32, 1)
                    wait(act, split_ready, lambda n: 2 * (n - 1) + i + 1, n, d)
                    ins = act.activation(full[:, :], misc, ACT.Identity, bias=bias[:, i:i + 1])
                elif kind == "v":
                    wait(act, pv_ready, lambda n: NG * (n - 1), n, d)
                    ins = act.copy(v_aug[n % 2][:, :, :, 0:DK], misc.rearrange("p (t h e) -> p t h e", t=QT, e=DK))
                elif kind == "oT":
                    ins = act.activation(o_t[:, :], misc, ACT.Identity, bias=bias[:, 2:3])
                elif kind == "h2T":
                    ins = act.copy(h2_t[:, :], misc)
                elif kind == "y":
                    wait(act, xr_loaded, lambda n: 32 * (n + 1), n, d)
                    ins = act.activation(z[:, :], misc, ACT.Identity, scale=prm_t[:, GA:GA + 1], bias=prm_t[:, GABO:GABO + 1])
                ins.then_inc(misc_drained, 1)

            def batch(b, d=None):
                for k in range(NH):
                    g, hh = divmod(k, GROUP)
                    s = NG * b + g
                    for t in range(QT):
                        if hh == 0 and t == 2 and 0 <= s - 2 < NS:
                            wait(act, pv_ready, lambda b: NG * b + g - 1, b, d)
                            if s - 4 >= 0:
                                wait(act, misc_filled, lambda b: at["o", NG * b + g - 4] + 1, b, d)
                            act.copy(o_aug[g % 2][:, :], ps[:, PV_BANK, :]).then_inc(pv_taken, 1)
                        if 0 <= s < NS:
                            wait(act, st_ready, lambda b: QT * (NH * b + k) + t + 1, b, d)
                            act.activation(probs[:, g % 2, hh, S * t:S * (t + 1)], ps[:, ST_BANK + turn(QT * k + t)[0], :],
                                           ACT.Exp, scale=SCALE).then_inc(exps_done, 1)
                        step = misc_at(b, k, 0)
                        if t == 1 and step and step[0] == "h2T":
                            misc_drain(*step, d)
                    if k == 13 and 0 <= b - 2 < NB:
                        wait(act, route_step, lambda b: ROUTE_STEPS * (b - 2) + 13, b, d)
                        act.activation(odds[:, 0, :], top[:, 3, :], ACT.Exp).then_inc(odds_ready, 1)
                    if 2 <= k < 2 + QT and b + 2 < NB:
                        normalise(b + 2, d, [k - 2])
                    step = misc_at(b, k, 1)
                    if step and step[0] in ("hT", "q", "k", "v", "oT", "y"):
                        misc_drain(*step, d)

            normalise(0, None, range(QT))
            misc_drain("hT", 0, None)
            misc_drain("q", 0, None)
            misc_drain("k", 0, None)
            for b in range(-1, FIRST):
                batch(b)
            with act.Fori(0, LOOP) as d:
                batch(FIRST, d)
                batch(FIRST + 1, d)
            for b in range(FIRST + 2 * LOOP, NB + 3):
                batch(b)

            def pair(q, d=None):
                for m in range(PAIR):
                    i = PAIR * q + m
                    if i + 1 < NTILE:
                        along(act, xt_ready, lambda q: PAIR * q + m + 2, q, d)
                        along(act, gu_ready, lambda q: PAIR * q + m, q, d)
                        act.copy(x_t[(m + 1) % 2], ps[:, XT_BANK + (m + 1) % 2, 0:P]).then_inc(xt_taken, 1)
                    if i < NTILE:
                        along(act, gu_ready, lambda q: PAIR * q + m + 1, q, d)
                        along(act, hid_ready, lambda q: PAIR * q + m - 1, q, d)
                        act.activation(silu[m % 2], ps[:, GU_BANK + m % 2, 0:INTER], ACT.Silu).then_inc(silu_done, 1)
                    if 0 <= i - 2 < NTILE:
                        along(act, y_ready, lambda q: PAIR * q + m - 1, q, d)
                        along(act, y_stored[(m - 2) % SLOTS], lambda q: 16 * ((PAIR * q + m - 2) // SLOTS), q, d)
                        act.copy(y_out[(m - 2) % SLOTS], ps[:, Y_BANK + m % 2, 0:D]).then_inc(y_taken, 1)

            act.wait_ge(xt_ready, 1)
            act.copy(x_t[0], ps[:, XT_BANK, 0:P]).then_inc(xt_taken, 1)
            for q in range(LAG + 1):
                pair(q)
            with act.Fori(0, NPAIR - LAG - 2) as d:
                pair(LAG + 1, d)
            for q in range(NPAIR - 1, NPAIR + 1):
                pair(q)

        @block.vector
        def _(dve):
            steps = [0]

            def settled(ins):
                steps[0] += 1
                ins.then_inc(dve_step, 1)
                dve.wait_ge(dve_step, steps[0])

            def inverse_root(step, v, y, t):
                step(dve.tensor_scalar(y.bitcast(I32), v.bitcast(I32), -0.5, ROOT_SEED, ALU.mult, ALU.add))
                for _ in range(3):
                    step(dve.scalar_tensor_tensor(t, y, -0.5, y, ALU.mult, ALU.mult))
                    step(dve.tensor_tensor(t, t, v, ALU.mult))
                    step(dve.scalar_tensor_tensor(y, t, 1.5, y, ALU.add, ALU.mult))

            settled(dve.memset(before[:, :, :], 0.0))
            for q in range(4):
                dve.wait_ge(x_all_loaded[q], 16)
                for t in range(NT // 4 * q, NT // 4 * (q + 1)):
                    ins = dve.bn_stats(st6[:, t, :], x_all[:, t, :])
                settled(ins)
                for t in range(NT // 4 * q, NT // 4 * (q + 1)):
                    ins = dve.bn_aggr(mv[:, t, :], st6[:, t, :])
            settled(ins)
            settled(dve.tensor_scalar(rs4[:, 0, :], mv[:, :, 1], EPS, None, ALU.add))
            inverse_root(settled, rs4[:, 0, :], rs4[:, 1, :], rs4[:, 2, :])
            rstd = rs4[:, 1, :].rearrange("p (b t) -> p b t", t=QT)
            settled(dve.tensor_copy(prm[:, :, RSTD:RSTD + QT], rstd))
            settled(dve.scalar_tensor_tensor(prm[:, :, NMR:NMR + QT], mv[:, :, 0].rearrange("p (b t) -> p b t", t=QT),
                                             -1.0, rstd, ALU.mult, ALU.mult))
            dve.wait_ge(setup_drained, SETUP_MOD + 1)
            dve.wait_ge(consts_loaded, 16 * N_CONSTS)

            def away_from_zero(gate, scratch, to):
                sign, size, neg = scratch
                settled(dve.tensor_scalar(sign, gate, 0.0, 2.0, ALU.is_ge, ALU.mult))
                settled(dve.tensor_scalar(sign, sign, -1.0, None, ALU.add))
                settled(dve.tensor_scalar(neg, gate, -1.0, None, ALU.mult))
                settled(dve.tensor_tensor(size, neg, gate, ALU.max))
                settled(dve.tensor_scalar(size, size, 0.25, None, ALU.max))
                settled(dve.tensor_tensor(to, sign, size, ALU.mult))

            settled(dve.tensor_copy(prm[:, :, SA], mod[:, 0, :]))
            settled(dve.tensor_scalar(prm[:, :, CA], mod[:, 1, :], 1.0, None, ALU.add))
            away_from_zero(mod[:, 2, :], (gtmp[:, i, :] for i in range(3)), prm[:, :, GA])
            settled(dve.tensor_copy(row_s[:, ROW_S:ROW_S + D], mod_r[:, 0, :]))
            settled(dve.tensor_scalar(row_s[:, ROW_C:ROW_C + D], mod_r[:, 1, :], 1.0, None, ALU.add))
            away_from_zero(mod_r[:, 2, :], (gtmp_r[:, i, :] for i in range(3)), row_s[:, ROW_G:ROW_N])
            dve.tensor_scalar(prm[:, :, GABO], prm[:, :, GA], bias[:, 3:4], None, ALU.mult).then_inc(prm_ready, 1)

            def misc_drain(kind, n, g, d):
                key = (lambda n: (kind, NG * n + g)) if kind in ("shift", "o") else (lambda n: (kind, n))
                if kind == "shift":
                    wait(dve, misc_filled, lambda n: at[key(n)] + 1, n, d)
                    wait(dve, shift_stacked, lambda n: 64 * (NG * n + g - 1), n, d)
                    dve.tensor_copy(shift_t[g % 2][:, :], misc_bf[0:8 * QT, 0:P]).then_inc(misc_drained, 1)
                elif kind == "o":
                    wait(dve, misc_filled, lambda n: at[key(n)] + 1, n, d)
                    v = misc.rearrange("p (t i e) -> p t i e", t=QT, i=GROUP)
                    dve.reciprocal(o_rs[:, :, :], v[:, :, :, DK]).then_inc(o_rs_ready, 1)
                    wait(dve, o_rs_ready, lambda n: NG * n + g + 1, n, d)
                    dve.tensor_tensor(o_n[:, :, GROUP * g:GROUP * (g + 1), :], v[:, :, :, 0:DK],
                                      o_rs[:, :, :].unsqueeze(3).to_broadcast([P, QT, GROUP, DK]), ALU.mult
                                      ).then_inc(misc_drained, 1)
                elif kind == "x1":
                    wait(dve, misc_filled, lambda n: at[key(n)] + 1, n, d)
                    wait(dve, xr_loaded, lambda n: 32 * (n + 1), n, d)
                    wait(dve, x1_stored, lambda n: 16 * n, n, d)
                    wait(dve, h2_ready, lambda n: n, n, d)
                    dve.tensor_tensor(x1_s[:, :, :].rearrange("p t d -> p (t d)"), misc,
                                      x_r[:, :, :].rearrange("p t d -> p (t d)"), ALU.add).then_inc(misc_drained, 1)

            def wide(v):
                return v.unsqueeze(2).to_broadcast([P, QT, NE])

            def router_step(i, n, d):
                scores, left, eq, tmp, place_all, place_1, place_2, either = (route[:, v, :, :] for v in range(8))
                best, second, margin = (top[:, v, :] for v in (0, 1, 3))
                first_rank = route_o[:, RT_RANK:RT_RANK + QT] if i <= 6 else route_o[:, RT_RANK + QT:RT_COLS]
                one_hot, two_hot = chosen[:, 0, :, :], chosen[:, 1, :, :]
                if 2 <= i <= 13:
                    wait(dve, route_step, lambda n: ROUTE_STEPS * n + i - 1, n, d)
                elif i >= 16:
                    wait(dve, route_step, lambda n: ROUTE_STEPS * n + i - 2, n, d)
                if i == 0:
                    wait(dve, misc_filled, lambda n: at["score", n] + 1, n, d)
                    wait(dve, route_step, lambda n: ROUTE_STEPS * n, n, d)
                    dve.tensor_copy(scores.rearrange("p t e -> p (t e)"), misc[:, 0:QT * NE]).then_inc(misc_drained, 1)
                elif i == 14:
                    wait(dve, misc_filled, lambda n: at["where", n] + 1, n, d)
                    wait(dve, row_loaded[n % 2], lambda n: 16 * (n // 2 + 1), n, d)
                    dve.tensor_tensor(place_all, misc[:, 0:QT * NE].rearrange("p (t e) -> p t e", e=NE),
                                      row[n % 2][:, ROW_BASE:ROW_G].unsqueeze(1).to_broadcast([P, QT, NE]), ALU.add
                                      ).then_inc(misc_drained, 1)
                else:
                    if i in (1, 7):
                        if i == 1:
                            wait(dve, misc_drained, lambda n: at["score", n] + 1, n, d)
                        ins = dve.tensor_reduce(best if i == 1 else second, scores if i == 1 else left, AX.X, ALU.max)
                    elif i in (2, 8):
                        ins = dve.tensor_tensor(eq, scores if i == 2 else left, wide(best if i == 2 else second), ALU.is_equal)
                    elif i in (3, 9):
                        ins = dve.tensor_tensor(tmp, eq, rank[:, :, :], ALU.mult)
                    elif i in (4, 10):
                        if i == 4:
                            wait(dve, route_stored, lambda n: 16 * n, n, d)
                        ins = dve.tensor_reduce(first_rank, tmp, AX.X, ALU.max)
                    elif i in (5, 11):
                        ins = dve.tensor_tensor(one_hot if i == 5 else two_hot, tmp, wide(first_rank), ALU.is_equal)
                    elif i == 6:
                        ins = dve.scalar_tensor_tensor(left, one_hot, -3.0e38, scores, ALU.mult, ALU.add)
                    elif i == 12:
                        ins = dve.tensor_tensor(either, one_hot, two_hot, ALU.add)
                    elif i == 13:
                        ins = dve.tensor_tensor(margin, second, best, ALU.subtract)
                    elif i == 15:
                        wait(dve, misc_drained, lambda n: at["where", n] + 1, n, d)
                        ins = dve.tensor_tensor(place_1, place_all, one_hot, ALU.mult)
                    elif i == 16:
                        ins = dve.tensor_tensor(place_2, place_all, two_hot, ALU.mult)
                    elif i == 17:
                        ins = dve.tensor_reduce(route_o[:, RT_ROW:RT_RANK], route[:, 5:7, :, :].rearrange("p a t e -> p (a t) e"),
                                                AX.X, ALU.add)
                    elif i == 18:
                        wait(dve, scattered, lambda n: 16 * 2 * QT * n, n, d)
                        ins = dve.tensor_copy(rows_o[:, :], route_o[:, RT_ROW:RT_RANK])
                    elif i == 19:
                        ins = dve.tensor_reduce(route_o[:, RT_N:RT_N + NE], either.rearrange("p t e -> p e t"), AX.X, ALU.add)
                    elif i == 20:
                        ins = dve.tensor_tensor(before[:, 1, :], before[:, 0, :], route_o[:, RT_N:RT_N + NE], ALU.add)
                    elif i == 21:
                        ins = dve.tensor_scalar(before[:, 0, :], before[:, 1, :], row[n % 2][:, ROW_KEEP:ROW_KEEP + 1], None,
                                                ALU.mult)
                    elif i == 22:
                        wait(dve, odds_ready, lambda n: n + 1, n, d)
                        ins = dve.tensor_scalar(odds[:, 1, :], odds[:, 0, :], 1.0, None, ALU.add)
                    elif i == 23:
                        ins = dve.reciprocal(route_o[:, RT_P:RT_P + QT], odds[:, 1, :])
                    elif i == 24:
                        ins = dve.tensor_tensor(route_o[:, RT_P + QT:RT_P + 2 * QT], odds[:, 0, :],
                                                route_o[:, RT_P:RT_P + QT], ALU.mult)
                    ins.then_inc(route_step, 1)

            def norm_step(i, n, d):
                v, y, nmr, t = (ln2[:, j, :] for j in range(4))
                if i == 0:
                    wait(dve, stats_ready, lambda n: n + 1, n, d)
                    wait(dve, h2_ready, lambda n: n, n, d)
                    ins = dve.tensor_scalar(v, mv_b[:, :, 1], EPS, None, ALU.add)
                else:
                    wait(dve, ln_step, lambda n: LN_STEPS * n + i, n, d)
                    if i == 1:
                        ins = dve.tensor_scalar(y.bitcast(I32), v.bitcast(I32), -0.5, ROOT_SEED, ALU.mult, ALU.add)
                    elif i == LN_STEPS - 1:
                        ins = dve.scalar_tensor_tensor(nmr, mv_b[:, :, 0], -1.0, y, ALU.mult, ALU.mult)
                    elif i % 3 == 2:
                        ins = dve.scalar_tensor_tensor(t, y, -0.5, y, ALU.mult, ALU.mult)
                    elif i % 3 == 0:
                        ins = dve.tensor_tensor(t, t, v, ALU.mult)
                    else:
                        ins = dve.scalar_tensor_tensor(y, t, 1.5, y, ALU.add, ALU.mult)
                ins.then_inc(ln_step, 1)

            BATCH_TILES = NH * QT
            AGGR_AT = 53
            NORM_AT = [54 + i for i in range(LN_STEPS)]
            ROUTER_AT = ([BATCH_TILES + 38 + i for i in range(14)]
                         + [BATCH_TILES + 58 + i for i in range(11)])

            def later_steps(b, spot, d):
                for lag in (1, 2, 3):
                    n, place = b - lag, BATCH_TILES * (lag - 1) + spot
                    if 0 <= n < NB:
                        if place in NORM_AT:
                            norm_step(NORM_AT.index(place), n, d)
                        if place in ROUTER_AT:
                            router_step(ROUTER_AT.index(place), n, d)

            def batch(b, d=None):
                for k in range(NH):
                    g, hh = divmod(k, GROUP)
                    s = NG * b + g
                    looks = 0 <= s + 2 < NS
                    for t in range(QT):
                        spot = QT * k + t
                        if 0 <= b - 1 < NB:
                            if k == 12 and t == 0:
                                wait(dve, misc_drained, lambda b: at["x1", b - 1] + 1, b, d)
                                wait(dve, stats_ready, lambda b: b - 1, b, d)
                            if spot == AGGR_AT:
                                wait(dve, x1_stats, lambda b: 4 * b, b, d)
                                wait(dve, ln_step, lambda b: LN_STEPS * (b - 1), b, d)
                        if looks:
                            hs = hh ^ 1
                            wait(dve, scores_ready, lambda b: 16 * (NG * b + g + 2) + 4 * hh + t + 1, b, d)
                            bank = turn(QT * (GROUP * ((g + 2) % NG) + hh) + t)[0]
                            dve.tensor_reduce(maxes[g % 2][:, hs % 2, hs // 2, t:t + 1], ps[:, S_BANK + bank, :],
                                              AX.X, ALU.max).then_inc(maxes_done, 1)
                        if 0 <= b - 1 < NB:
                            if k == 12:
                                dve.bn_stats(st_b[:, t, :], x1_s[:, t, :]).then_inc(x1_stats, 1)
                            if spot == AGGR_AT:
                                for i in range(QT):
                                    ins = dve.bn_aggr(mv_b[:, i, :], st_b[:, i, :])
                                ins.then_inc(stats_ready, 1)
                        later_steps(b, spot, d)
                    if looks and hh == GROUP - 1:
                        wait(dve, maxes_done, lambda b: 16 * (NG * b + g + 3), b, d)
                        if s >= 0:
                            wait(dve, misc_filled, lambda b: at["shift", NG * b + g] + 1, b, d)
                        m = maxes[g % 2][:, :, :, :].rearrange("p a c q -> p a (c q)")
                        high, low = (shift[g % 2][:, :, i, :, :].rearrange("p a c q -> p a (c q)") for i in range(2))
                        dve.tensor_scalar(high, m, -1.0, None, ALU.mult).then_inc(shift_high, 1)
                        wait(dve, shift_high, lambda b: NG * b + g + 3, b, d)
                        dve.scalar_tensor_tensor(low, m, -1.0, high, ALU.mult, ALU.subtract).then_inc(shift_ready, 1)
                    step = misc_at(b, k, 1)
                    if step and step[0] in ("shift", "o"):
                        misc_drain(step[0], step[1] // NG, step[1] % NG, d)
                    elif step and step[0] == "x1":
                        misc_drain(step[0], step[1], 0, d)

            for b in range(-1, FIRST):
                batch(b)
            with dve.Fori(0, LOOP) as d:
                batch(FIRST, d)
                batch(FIRST + 1, d)
            for b in range(FIRST + 2 * LOOP, NB + 3):
                batch(b)

            dve.wait_ge(counts_loaded, 16)
            dve.tensor_reduce(counts, route_all[:, :, RT_N:RT_N + NE].rearrange("p (s b) e -> p s e b", b=SBB), AX.X, ALU.add).then_inc(counts_ready, 1)
            dve.wait_ge(counts_summed, 1)
            count = ps[0:1, 0, 0:NSB * NE]
            settled(dve.tensor_tensor(needs.rearrange("p (r k) -> p r k", k=FULL),
                                      count.unsqueeze(2).to_broadcast([1, NSB * NE, FULL]),
                                      maps[:, MAP_THR:MAP_THR + FULL].unsqueeze(1).to_broadcast([1, NSB * NE, FULL]), ALU.is_gt))
            settled(dve.tensor_reduce(need, needs.rearrange("p (r k) -> p r k", k=FULL), AX.X, ALU.add))
            by_expert = need.rearrange("p (s e) -> p s e", e=NE)
            for i in range(NSB):
                ins = dve.tensor_tensor(uptos.rearrange("p (s e f) -> p s e f", e=NE, f=NE)[:, i],
                                        by_expert[:, i:i + 1, :].to_broadcast([1, NE, NE]),
                                        maps[:, MAP_TRI:MAP_THR].rearrange("p (e f) -> p e f", f=NE), ALU.mult)
            settled(ins)
            settled(dve.tensor_reduce(upto, uptos.rearrange("p (r f) -> p r f", f=NE), AX.X, ALU.add))
            done_of = done.rearrange("p (s i e) -> p s i e", i=TILES, e=NE)
            for i in range(NSB):
                ins = dve.tensor_tensor(done_of[:, i], upto[:, NE * i:NE * (i + 1)].unsqueeze(1).to_broadcast([1, TILES, NE]),
                                        maps[:, MAP_TILE:MAP_TRI].unsqueeze(2).to_broadcast([1, TILES, NE]), ALU.is_le)
            settled(ins)
            settled(dve.tensor_reduce(owner, done.rearrange("p (i e) -> p i e", e=NE), AX.X, ALU.add))
            for i in range(NSB):
                ins = dve.tensor_tensor(done_of[:, i], done_of[:, i],
                                        by_expert[:, i:i + 1, :].to_broadcast([1, TILES, NE]), ALU.mult)
            settled(ins)
            settled(dve.tensor_reduce(start, done.rearrange("p (i e) -> p i e", e=NE), AX.X, ALU.add))
            settled(dve.tensor_tensor(start, maps[:, MAP_BASE:MAP_FROM], start, ALU.subtract))
            settled(dve.scalar_tensor_tensor(start, owner, float(REGION), start, ALU.mult, ALU.add))
            settled(dve.tensor_scalar(tile_row[:, ROW_PAD:ROW_PAD + NTILE], start, float(P), None, ALU.mult))
            settled(dve.tensor_scalar(tile_row[:, ROW_PAD + NTILE:], maps[:, 0:SLOTS], 0.0, None, ALU.mult))
            settled(dve.tensor_scalar(tile_expert[:, 0:4], maps[:, 0:4], 0.0, None, ALU.mult))
            settled(dve.tensor_scalar(tile_expert[:, 4:4 + NTILE], owner, float(NE - 1), None, ALU.min))
            settled(dve.tensor_tensor(fill_row[:, 0:NSB * NE], count, maps[:, MAP_FILL:MAP_FILL + NSB * NE], ALU.add))
            dve.tensor_copy(fill_row[:, NSB * NE:NSB * NE + SPARE], maps[:, MAP_FILL + NSB * NE:MAP_N]).then_inc(map_ready, 1)
            settled(dve.tensor_tensor(moves, upto, need, ALU.subtract))
            dve.scalar_tensor_tensor(moves, moves, float(P), maps[:, MAP_FROM:MAP_FILL], ALU.mult, ALU.add).then_inc(moves_ready, 1)
            dve.wait_ge(moves_spread, 1)
            by_choice = is_expert.rearrange("p (b v e) -> p b v e", v=2 * QT, e=NE)
            for i in range(NB):
                ins = dve.tensor_tensor(by_choice[:, i],
                                        route_all[:, i, RT_RANK:RT_COLS].unsqueeze(2).to_broadcast([P, 2 * QT, NE]),
                                        rank[:, 0:1, :].to_broadcast([P, 2 * QT, NE]), ALU.is_equal)
            settled(ins)
            for i in range(NB):
                ins = dve.tensor_tensor(by_choice[:, i], by_choice[:, i],
                                        ps[:, 1, NE * (i // SBB):NE * (i // SBB + 1)].unsqueeze(1).to_broadcast([P, 2 * QT, NE]),
                                        ALU.mult)
            settled(ins)
            settled(dve.tensor_reduce(rows_move, is_expert.rearrange("p (v e) -> p v e", e=NE), AX.X, ALU.add))
            dve.tensor_tensor(rows_from.rearrange("p (b k) -> p b k", k=2 * QT), route_all[:, :, RT_ROW:RT_RANK],
                              rows_move.rearrange("p (b k) -> p b k", k=2 * QT), ALU.add).then_inc(from_ready, 1)

            def sum_tile(j, t, half, q, d):
                spot = 4 * (QT * j + t)
                first, second = picked[j][t]
                p = [route_l[j][:, RT_P + QT * v + t:RT_P + QT * v + t + 1] for v in range(2)]
                dst = out_s[j][:, D * t:D * (t + 1)]

                def settle(i):
                    along(dve, sum_step, lambda q: 32 * (q - LAG) + spot + i, q, d)

                if half == 0:
                    along(dve, gathered[j][t], lambda q: 32 * (q - LAG + 1), q, d)
                    dve.tensor_scalar(second, second, p[1], None, ALU.mult).then_inc(sum_step, 1)
                    settle(1)
                    dve.scalar_tensor_tensor(second, first, p[0], second, ALU.mult, ALU.add).then_inc(sum_step, 1)
                else:
                    settle(2)
                    dve.tensor_tensor(second, second, gate_l[j], ALU.mult).then_inc(sum_step, 1)
                    settle(3)
                    if t == 0:
                        along(dve, out_stored[j], lambda q: 16 * (q - LAG), q, d)
                    dve.tensor_tensor(dst, second, x1_l[j][:, D * t:D * (t + 1)], ALU.add).then_inc(sum_step, 1)

            SUM_AT = [13 + i for i in range(4 * QT)]

            def pair(q, d=None):
                for m in range(PAIR):
                    i = PAIR * q + m
                    if 0 <= i - 1 < NTILE:
                        along(dve, hidt_ready, lambda q: PAIR * q + m, q, d)
                        along(dve, y_ready, lambda q: PAIR * q + m - 2, q, d)
                        dve.tensor_copy(hid_t[(m - 1) % 2], ps[0:HALF, HT_BANK + (m - 1) % 2, 0:2 * P]).then_inc(hidt_taken, 1)
                    if i < NTILE:
                        along(dve, silu_done, lambda q: PAIR * q + m + 1, q, d)
                        along(dve, hidt_ready, lambda q: PAIR * q + m - 1, q, d)
                        dve.tensor_tensor(hid[m % 2], silu[m % 2], ps[:, GU_BANK + m % 2, INTER:2 * INTER], ALU.mult
                                          ).then_inc(hid_ready, 1)
                    for v, spot in enumerate(SUM_AT):
                        late = spot // PAIR
                        if spot % PAIR == m and LAG <= q - late < NPAIR + LAG:
                            sum_tile(v // (2 * QT), v // 2 % QT, v % 2, q - late, d)

            for q in range(LAG + 1):
                pair(q)
            with dve.Fori(0, NPAIR - LAG - 2) as d:
                pair(LAG + 1, d)
            for q in range(NPAIR - 1, NPAIR + LAG + 1):
                pair(q)

        @block.gpsimd
        def _(pool):
            pool.memset(ones_rows, 1.0).then_inc(ones_ready, 1)
            pool.memset(one[:, :], 1.0).then_inc(one_ready, 1)
            pool.memset(zeros[:, :], 0.0).then_inc(one_ready, 1)
            pool.wait_ge(one_ready, 2)
            for i in range(2):
                for side in range(2):
                    pool.memset(q_st[i][side][SIDE * (1 - side):SIDE * (2 - side), :, :], 0.0).then_inc(zeros_ready, 1)
                    pool.wait_ge(zeros_ready, 2 * i + side + 1)
            for i in range(2):
                pool.memset(v_aug[i][:, :, :, DK + 1:VW], 0.0).then_inc(fills_done, 1)
                pool.memset(v_aug[i][:, :, :, DK:DK + 1], 1.0).then_inc(fills_done, 1)

            pool.wait_ge(consts_loaded, 16 * N_CONSTS)
            pool.tensor_copy(identb[:, :], ident[:, :]).then_inc(fills_done, 1)
            pool.memset(ones[:, :], 1.0).then_inc(fills_done, 1)

            def split(kind, n, d):
                i = 0 if kind == "q" else 1
                full, parts, high, mid, low = (q32, q_parts, 0, 1, 2) if kind == "q" else (k32, k_parts, 1, 2, 0)
                wait(pool, misc_drained, lambda n: at[kind, n] + 1, n, d)
                wait(pool, parts_stored, lambda n: 32 * n, n, d)
                pool.tensor_tensor(parts[:, high, :], full[:, :], one[:, :].to_broadcast([P, S]), ALU.mult).then_inc(pool_step, 1)
                wait(pool, pool_step, lambda n: 6 * n + 3 * i + 1, n, d)
                pool.tensor_tensor(parts[:, mid, :], full[:, :], parts[:, high, :], ALU.subtract).then_inc(pool_step, 1)
                wait(pool, split_ready, lambda n: 2 * n + i, n, d)
                pool.tensor_tensor(rest[:, :], full[:, :], parts[:, high, :], ALU.subtract).then_inc(pool_step, 1)
                wait(pool, pool_step, lambda n: 6 * n + 3 * i + 3, n, d)
                pool.tensor_tensor(parts[:, low, :], rest[:, :], parts[:, mid, :], ALU.subtract).then_inc(split_ready, 1)

            def second_norm(n, d):
                rstd, nmr = (ln2[:, v, :].unsqueeze(2).to_broadcast([P, QT, D]) for v in (1, 2))
                scale, shift_by = (row[n % 2][:, c0:c0 + D].unsqueeze(1).to_broadcast([P, QT, D]) for c0 in (ROW_C, ROW_S))
                to = h2[n % 2][:, :, :]
                wait(pool, row_loaded[n % 2], lambda n: 16 * (n // 2 + 1), n, d)
                wait(pool, route_step, lambda n: ROUTE_STEPS * (n - 1) + 17, n, d)
                wait(pool, ln_step, lambda n: LN_STEPS * (n + 1), n, d)
                pool.tensor_tensor(to, x1_s[:, :, :], rstd, ALU.mult).then_inc(ln2_step, 1)
                wait(pool, ln2_step, lambda n: 3 * n + 1, n, d)
                pool.tensor_tensor(to, to, nmr, ALU.add).then_inc(ln2_step, 1)
                wait(pool, ln2_step, lambda n: 3 * n + 2, n, d)
                pool.tensor_tensor(to, to, scale, ALU.mult).then_inc(ln2_step, 1)
                wait(pool, ln2_step, lambda n: 3 * n + 3, n, d)
                pool.tensor_tensor(to, to, shift_by, ALU.add).then_inc(h2_ready, 1)

            def scatter(n, d):
                if n == NB - 1:
                    pool.wait_ge(route_step, ROUTE_STEPS * n + 17)
                for v in range(2 * QT):
                    pool.indirect_dma_start(xs_d, bass.IndirectOffsetOnAxis(ap=rows_o[:, v:v + 1], axis=0),
                                            h2[n % 2][:, v % QT, :], None).then_inc(scattered, 16)

            def batch(b, d=None):
                if 0 <= b - 2 < NB:
                    second_norm(b - 2, d)
                if 0 <= b - 3 < NB:
                    scatter(b - 3, d)
                if b + 2 < NB:
                    split("q", b + 2, d)
                    split("k", b + 2, d)

            split("q", 0, None)
            split("k", 0, None)
            for b in range(-1, FIRST):
                batch(b)
            with pool.Fori(0, LOOP) as d:
                batch(FIRST, d)
                batch(FIRST + 1, d)
            for b in range(FIRST + 2 * LOOP, NB + 3):
                batch(b)

            def pair(q, d, block_of):
                rows = (block_of + 1) * TILES * P
                for j in range(2):
                    along(pool, gone_step, lambda q: 2 * (q - LAG) + j, q, d)
                    along(pool, sum_step, lambda q: 32 * (q - LAG - 1) + 16 * (j + 1), q, d)
                    along(pool, sums_loaded[j], lambda q: 64 * (q - LAG + 1), q, d)
                    pool.tensor_tensor(gone[:, :], one[:, :], one[:, :], ALU.mult).then_inc(gone_step, 1)
                    for t in range(QT):
                        for v in range(2):
                            pool.indirect_dma_start(picked[j][t][v], None, ys_d[0:rows, :],
                                                    bass.IndirectOffsetOnAxis(ap=rows_l[j][:, QT * v + t:QT * v + t + 1], axis=0)
                                                    ).then_inc(gathered[j][t], 16)

            for q in range(LAG):
                pair(LAG + q, None, 0)
            for i in range(1, NSB):
                with pool.Fori(0, LAG) as d:
                    pair(LAG * (i + 1), d, i)


_INS = ["L0_attn_x", "L0_attn_Wq", "L0_attn_bq", "L0_attn_Wk", "L0_attn_bk", "L0_attn_Wv", "L0_attn_bv",
        "L0_attn_Wo", "L0_attn_bo", "L0_ffn_gate_w", "L0_ffn_wg", "L0_ffn_wu", "L0_ffn_wd", "L0_c", "L0_wmod"]


def shape_constants():
    f32 = np.float32
    rank = np.broadcast_to(np.arange(NE, 0, -1, dtype=f32), (P, QT, NE))
    batches = np.arange(NB)
    slots = np.zeros((NB, 1 + NE), f32)
    slots[:, 0] = (batches + 1) % SBB != 0
    slots[:, 1:] = ((batches // SBB)[:, None] * REGIONS + np.arange(NE)[None, :]) * REGION * P
    tiles = np.arange(NTILE)
    regions = (np.arange(NSB)[:, None] * REGIONS + np.arange(NE)[None, :]).reshape(-1) * REGION * P
    spare = X_ROWS - SPARE * P + np.arange(SPARE) * P
    results = np.repeat(np.arange(NSB) * TILES * P, NE) - regions
    maps = np.concatenate([np.arange(TILES), np.tril(np.ones((NE, NE))).reshape(-1), np.arange(FULL) * P,
                           tiles // TILES * REGIONS * REGION + tiles % TILES, results, regions, spare])
    return {"ident_c": np.eye(P, dtype=f32), "tri_c": np.triu(np.ones((P, P), f32), 1),
            "rank_c": np.ascontiguousarray(rank), "slots_c": slots, "map_c": maps.astype(f32)[None, :]}


def kernel(**inputs):
    import concourse.bacc as bacc
    from concourse.bass_utils import run_bass_kernel_spmd

    nc = bacc.Bacc("TRN2", target_bir_lowering=False, num_devices=1)
    arrays = {name: np.ascontiguousarray(inputs[name]) for name in _INS}
    arrays.update(shape_constants())
    args = [nc.dram_tensor(name, a.shape, mybir.dt.from_np(a.dtype), kind="ExternalInput").ap()
            for name, a in arrays.items()]
    args.append(nc.dram_tensor("out", (NB, S, D), F32, kind="ExternalOutput").ap())
    adaln_block(nc, *args)
    result = run_bass_kernel_spmd(nc, [arrays], core_ids=[0])
    return result.results[0]["out"]
```

```python
import math
from contextlib import ExitStack

import concourse.bass as bass
import numpy as np
from concourse import mybir

F32 = mybir.dt.float32
BF16 = mybir.dt.bfloat16
I32 = mybir.dt.int32
U32 = mybir.dt.uint32
ALU = mybir.AluOpType
ACT = mybir.ActivationFunctionType
AX = mybir.AxisListType

P = 128
NB, S, D = 16, 512, 128
NH, DK = 16, 8
NE, INTER = 8, 176
QT = S // P
NT = NB * QT
HID = NE * INTER
NC = HID // P
HALF = INTER // 2
EPS = 1e-5
SCALE = 1.0 / math.sqrt(DK)
PAIRS = NH // 2
GROUP = 4
NG = NH // GROUP
NS = NB * NG
TERMS = 6
SIDE = 64
SHIFT = TERMS * DK
VW = 32
STACK_DMAS = 18
PRM = 12
RSTD, NMR, CA, SA, GA, GABO = 0, 4, 8, 9, 10, 11
ST_BANK, S_BANK, PV_BANK, MISC_BANK = 0, 3, 6, 7
XT_BANK, GU_BANK, HT_BANK, Y_BANK = 0, 1, 3, 4
TURN = 3
SBB = 8
NSB = NB // SBB
FULL = SBB * QT
REGION = FULL + 1
REGIONS = NE + 1
TILES = 2 * SBB * QT + NE
X_ROWS = NSB * REGIONS * REGION * P
XW = D + 2
BLANKS = 2 * NSB * NE
Y_ROWS = 2 * NB * S + BLANKS * P
NTILE = NSB * TILES
PAIR = 2 * TILES // SBB
NPAIR = NTILE // PAIR
SLOTS = 18
AHEAD = 8
LAG = SBB // 2
PADDED = -(-PAIR // 4) * 4
ROW_C, ROW_S, ROW_KEEP, ROW_AT, ROW_BASE, ROW_G = (sum((D, D, 1, 1, NE)[:i]) for i in range(6))
ROW_N = ROW_G + D
MAP_TILE, MAP_TRI, MAP_THR, MAP_FILL, MAP_N = (sum((TILES, NE * NE, FULL, NSB * NE)[:i]) for i in range(5))
MAP_STEPS = 14
ROOT_SEED = float(0x5F3759DF)
LATE = [(NB, k) for k in range(GROUP, NH)] + [(NB + 1, k) for k in range(NH)] + [(NB + 2, k) for k in range(2)]
LATE_PAIRS = 2
MAP_BURST = 3
LN_STEPS, ROUTE_STEPS = 12, 25


def lin(f, n, d):
    if d is None:
        return f(n)
    assert f(n + 4) - f(n + 2) == f(n + 2) - f(n)
    return d * (f(n + 2) - f(n)) + f(n)


def wait(eng, sem, f, n, d):
    v = lin(f, n, d)
    if not isinstance(v, int) or v > 0:
        eng.wait_ge(sem, v)


def batch_of(n, d):
    return n if d is None else d * 2 + n


def turn(i):
    last = NH * QT - 1
    before = i - TURN if i >= TURN else max(j for j in range(last + 1) if j % TURN == i % TURN) - last - 1
    return i % TURN, i - before


def along(eng, sem, f, q, d):
    v = f(q) if d is None else d * (f(q + 1) - f(q)) + f(q)
    if not isinstance(v, int) or v > 0:
        eng.wait_ge(sem, v)


def misc_at(b, k, end):
    g, r = divmod(k, GROUP)
    s = NG * b + g
    if not end:
        step = {4: ("h2T", b - 2, NB), 6: ("score", b - 2, NB), 13: ("where", b - 2, NB)}.get(k)
    elif r == 0:
        step = ("shift", s + 1, NS)
    elif r == 1:
        step = ("o", s - 2, NS)
    else:
        step = {3: ("v", b + 1, NB), 6: ("oT", b - 1, NB), 7: ("y", b - 1, NB), 10: ("x1", b - 1, NB),
                11: ("hT", b + 2, NB), 14: ("q", b + 2, NB), 15: ("k", b + 2, NB)}.get(k)
    return step[:2] if step and 0 <= step[1] < step[2] else None


def misc_order():
    steps = [("hT", 0), ("q", 0), ("k", 0)]
    for b in range(-1, NB + 3):
        steps += [misc_at(b, k, end) for k in range(NH) for end in (0, 1) if misc_at(b, k, end)]
    return {step: i for i, step in enumerate(steps)}


def adaln_block(nc, x, Wq, bq, Wk, bk, Wv, bv, Wo, bo, gate_w, wg, wu, wd, c, wmod,
                ident_c, tri_c, rank_c, slots_c, map_c, place_c, out):
    with ExitStack() as ctx:
        def sb(name, shape, dt=F32):
            return ctx.enter_context(nc.sbuf_tensor(name, shape, dt))

        def sem(name):
            return ctx.enter_context(nc.semaphore(name))

        q_parts_d = nc.dram_tensor("q_parts_d", [NB, 3, P, S], BF16, kind="Internal").ap()
        k_parts_d = nc.dram_tensor("k_parts_d", [NB, 3, P, S], BF16, kind="Internal").ap()
        prm_d = nc.dram_tensor("prm_d", [NB, P, PRM], F32, kind="Internal").ap()
        row_d = nc.dram_tensor("row_d", [NB, ROW_N], F32, kind="Internal").ap()
        xs_d = nc.dram_tensor("xs_d", [X_ROWS, XW], F32, kind="Internal").ap()
        ys_d = nc.dram_tensor("ys_d", [Y_ROWS, D], F32, kind="Internal").ap()
        x1_d = nc.dram_tensor("x1_d", [NB, S, D], F32, kind="Internal").ap()

        ident = sb("ident", [P, P])
        identb = sb("identb", [P, P], BF16)
        tri = sb("tri", [P, P])
        ones = sb("ones", [P, P])
        blank = sb("blank", [P, XW - 1 + BLANKS])
        place = sb("place", [P, 2 * QT + BLANKS])
        maps = sb("maps", [1, MAP_N])
        rank = sb("rank", [P, QT, NE])
        w_t = sb("w_t", [P, 4, D])
        wqT, wkT, wvT, woT = (w_t[:, i, :] for i in range(4))
        bias = sb("bias", [P, 4])
        b_nat = sb("b_nat", [4, D])
        b_perm = sb("b_perm", [2, D])
        c_nat = sb("c_nat", [NB, D])
        c_silu = sb("c_silu", [NB, D])
        gw_nat = sb("gw_nat", [NE, D])
        gw_t = sb("gw_t", [P, NE])
        c_t = sb("c_t", [P, NB])
        mod = sb("mod", [P, 3, NB])
        gtmp = sb("gtmp", [P, 3, NB])
        row_s = sb("row_s", [NB, ROW_N])
        wg_t = sb("wg_t", [P, NC, P])
        wu_t = sb("wu_t", [P, NC, P])
        wd_t = sb("wd_t", [HALF, 2 * NE, D])
        prm = sb("prm", [P, NB, PRM])
        mv = sb("mv", [P, NT, 2])

        probs = sb("probs", [P, 2, GROUP, QT * S])
        x_all = probs[:, 0, :, :].rearrange("p a (t d) -> p (a t) d", d=D)
        ffn_nat = probs[:, 1, 0:3, 0:HID]
        ones_rows = probs[0:2, 1, 3, 0:S // 2].bitcast(BF16)
        wmod_s = probs[:, 1, 3, S // 2:S // 2 + 6 * D]
        mod_r = probs[0:NB, 1, 3, S // 2 + 6 * D:S // 2 + 9 * D].rearrange("p (a d) -> p a d", d=D)
        w_nat = probs[:, 1, 0, HID:HID + 4 * D].rearrange("p (a d) -> p a d", d=D)
        st6 = probs[:, 1, 1, HID:HID + 6 * NT].rearrange("p (t k) -> p t k", k=6)
        rs4 = probs[:, 1, 1, HID + 6 * NT:HID + 10 * NT].rearrange("p (a t) -> p a t", t=NT)
        gtmp_r = probs[0:NB, 1, 2, HID:HID + 3 * D].rearrange("p (a d) -> p a d", d=D)
        q_st = [[sb(f"q_st{i}_{side}", [P, PAIRS, S], BF16) for side in range(2)] for i in range(2)]
        k_st = [sb(f"k_st{i}", [P, PAIRS, S], BF16) for i in range(2)]
        v_aug = [sb(f"v_aug{i}", [P, QT, NH, VW]) for i in range(2)]
        x_a = sb("x_a", [P, QT, D])
        prm_a = sb("prm_a", [P, PRM])
        x_n = sb("x_n", [P, QT, D])
        h_t = sb("h_t", [P, S])
        q32 = sb("q32", [P, S])
        k32 = sb("k32", [P, S])
        q_parts = sb("q_parts", [P, 3, S], BF16)
        k_parts = sb("k_parts", [P, 3, S], BF16)
        rest = sb("rest", [P, S])
        one = sb("one", [P, 1])
        maxes = [sb(f"maxes{i}", [P, 2, 2, QT]) for i in range(2)]
        shift = [sb(f"shift{i}", [P, 2, 2, 2, QT], BF16) for i in range(2)]
        shift_t = [sb(f"shift_t{i}", [4 * 2 * QT, P], BF16) for i in range(2)]
        o_aug = [sb(f"o_aug{i}", [P, S]) for i in range(2)]
        o_rs = sb("o_rs", [P, QT, GROUP])
        o_n = sb("o_n", [P, QT, NH, DK])
        o_t = sb("o_t", [P, S])
        z = sb("z", [P, S])
        x_r = sb("x_r", [P, QT, D])
        prm_t = sb("prm_t", [P, PRM])
        x1_s = sb("x1_s", [P, QT, D])
        st_b = sb("st_b", [P, QT, 6])
        mv_b = sb("mv_b", [P, QT, 2])
        ln2 = sb("ln2", [P, 4, QT])
        row = [sb(f"row{i}", [P, ROW_G]) for i in range(2)]
        h2 = [sb(f"h2_{i}", [P, 2, QT, XW]) for i in range(2)]
        h2_t = sb("h2_t", [P, S])
        route = sb("route", [P, 8, QT, NE])
        chosen = sb("chosen", [P, 2, QT, NE])
        top = sb("top", [P, 4, QT])
        odds = sb("odds", [P, 2, QT])
        before = sb("before", [P, 2, NE])
        chosen_n = sb("chosen_n", [P, NE])
        chosen_all = sb("chosen_all", [P, NB, NE])
        rows_f = sb("rows_f", [P, 2 * QT])
        rows_o = sb("rows_o", [P, 2 * QT], U32)

        def parts(area):
            taken = [0]

            def part(n):
                taken[0] += n
                return area[:, taken[0] - n:taken[0]]
            return part

        part = parts(probs[:, :, :, :].rearrange("p a b s -> p (a b s)"))
        y_out = [part(D) for _ in range(SLOTS)]
        x_t = [part(P) for _ in range(2)]
        silu = [part(INTER) for _ in range(2)]
        hid = [part(INTER) for _ in range(2)]
        hid_t = [part(2 * P)[0:HALF] for _ in range(2)]
        y_sum = [part(2 * S) for _ in range(2)]
        x1_l = [part(S) for _ in range(2)]
        gate_l = [part(D) for _ in range(2)]
        gate_last = part(SBB * D)
        x1_last = [part(S) for _ in range(SBB)]
        y_last = [part(2 * S) for _ in range(SBB // 2)]

        def stack(st):
            return st[:, :, :].rearrange("p j s -> p (j s)").bitcast(F32)

        x_in = [stack((q_st[0][0], k_st[0])[i % 2])[:, XW * (i // 2):XW * (i // 2 + 1)] for i in range(SLOTS)]
        part = parts(stack(q_st[0][1]))
        tile_row = part(NPAIR * PADDED)[0:1].bitcast(I32).rearrange("p (q m) -> p q m", m=PADDED)
        tile_expert = part(NPAIR * PADDED)[0:1].bitcast(I32).rearrange("p (q m) -> p q m", m=PADDED)
        fill_row = part(NSB * NE)[0:1].bitcast(I32)
        counts = part(NE)
        needs = part(NE * FULL)[0:1].rearrange("p (e k) -> p e k", k=FULL)
        need = part(NE)[0:1]
        uptos = part(NE * NE)[0:1].rearrange("p (e f) -> p e f", f=NE)
        upto = part(NE)[0:1]
        done = part(TILES * NE)[0:1].rearrange("p (i e) -> p i e", e=NE)
        owner = part(TILES)[0:1]
        start = part(TILES)[0:1]
        y_last = y_last + [stack(q_st[1][i // 2])[:, 2 * S * (i % 2):2 * S * (i % 2 + 1)] for i in range(SBB - len(y_last))]
        gone = sb("gone", [P, 1])

        ps = ctx.enter_context(nc.psum_tensor("ps", [P, 8, S], F32))
        misc = ps[:, MISC_BANK, :]
        misc_bf = misc.bitcast(BF16)

        consts_loaded = sem("consts_loaded")
        more_loaded = sem("more_loaded")
        x_all_loaded = [sem(f"x_all_loaded{i}") for i in range(4)]
        ffn_loaded = sem("ffn_loaded")
        c_ready = sem("c_ready")
        setup_filled = sem("setup_filled")
        setup_drained = sem("setup_drained")
        fills_done = sem("fills_done")
        ones_ready = sem("ones_ready")
        one_ready = sem("one_ready")
        ones_stacked = sem("ones_stacked")
        zeros_ready = sem("zeros_ready")
        zeros_stacked = sem("zeros_stacked")
        dve_step = sem("dve_step")
        prm_ready = sem("prm_ready")
        prm_stored = sem("prm_stored")
        xa_loaded = sem("xa_loaded")
        xn_ready = sem("xn_ready")
        misc_filled = sem("misc_filled")
        misc_drained = sem("misc_drained")
        pool_step = sem("pool_step")
        split_ready = sem("split_ready")
        parts_stored = [sem(f"{kind}_parts_stored") for kind in "qk"]
        stack_ready = sem("stack_ready")
        scores_ready = sem("scores_ready")
        maxes_done = sem("maxes_done")
        shift_high = sem("shift_high")
        shift_ready = sem("shift_ready")
        shift_stacked = sem("shift_stacked")
        st_ready = sem("st_ready")
        exps_done = sem("exps_done")
        pv_ready = sem("pv_ready")
        pv_taken = sem("pv_taken")
        o_rs_ready = sem("o_rs_ready")
        xr_loaded = sem("xr_loaded")
        x1_stats = sem("x1_stats")
        stats_ready = sem("stats_ready")
        x1_stored = sem("x1_stored")
        row_stored = sem("row_stored")
        row_loaded = [sem(f"row_loaded{i}") for i in range(2)]
        blank_stored = sem("blank_stored")
        ln_step = sem("ln_step")
        ln2_step = sem("ln2_step")
        h2_ready = sem("h2_ready")
        route_step = sem("route_step")
        odds_ready = sem("odds_ready")
        scattered = sem("scattered")
        counts_summed = sem("counts_summed")
        map_step = sem("map_step")
        filled = sem("filled")
        gone_step = sem("gone_step")
        x_loaded = [sem(f"x_loaded{i}") for i in range(SLOTS)]
        y_stored = [sem(f"y_stored{i}") for i in range(SLOTS)]
        xt_ready = sem("xt_ready")
        xt_taken = sem("xt_taken")
        gu_ready = sem("gu_ready")
        silu_done = sem("silu_done")
        hid_ready = sem("hid_ready")
        hidt_ready = sem("hidt_ready")
        hidt_taken = sem("hidt_taken")
        y_ready = sem("y_ready")
        y_taken = sem("y_taken")
        sums_loaded = [sem(f"sums_loaded{i}") for i in range(2)]
        sum_step = [sem(f"sum_step{i}") for i in range(2)]
        out_stored = [sem(f"out_stored{i}") for i in range(2)]
        gates_loaded = sem("gates_loaded")
        last_loaded = [sem(f"last_loaded{i}") for i in range(SBB)]
        last_step = [sem(f"last_step{i}") for i in range(SBB)]
        last_stored = sem("last_stored")

        at = misc_order()
        N_CONSTS, N_MORE = 12, 5
        EARLY = NB // 4
        SETUP_W, SETUP_GC, SETUP_MOD, SETUP_MOD2, SETUP_FFN = range(5)
        FFN_GROUPS = ([(w, c0, min(4, NC - c0), P) for w in range(2) for c0 in range(0, NC, 4)]
                      + [(2, c0, 4, HALF) for c0 in range(0, 2 * NE, 4)])
        N_SETUP = SETUP_FFN + len(FFN_GROUPS)
        FIRST, LOOP = 4, (NB - 6) // 2
        MAP_AT, COUNT_BANK = 8, S_BANK

        block = ctx.enter_context(nc.Block())

        def gated(eng, y, gate):
            y, n = y.rearrange("p (t d) -> p t d", d=D), y.shape[1] // D
            return eng.tensor_tensor(y, y, gate.unsqueeze(1).to_broadcast([P, n, D]), ALU.mult)

        LAST_BY_POOL = (1, 4)

        def last_sum(eng, i):
            y = y_last[i][:, 0:S]
            eng.wait_ge(last_loaded[i], 48)
            eng.tensor_tensor(y, y, y_last[i][:, S:2 * S], ALU.add).then_inc(last_step[i], 1)
            eng.wait_ge(gates_loaded, 16)
            eng.wait_ge(last_step[i], 1)
            gated(eng, y, gate_last[:, D * i:D * (i + 1)]).then_inc(last_step[i], 1)
            eng.wait_ge(last_step[i], 2)
            eng.tensor_tensor(y, y, x1_last[i], ALU.add).then_inc(last_step[i], 1)

        @block.sync
        def _(sp):
            def load_const(dst, src, loaded=consts_loaded):
                sp.dma_start(dst, src).then_inc(loaded, 16)

            def load_x(q):
                n = NT // 4
                sp.dma_start(x_all[:, n * q:n * (q + 1), :],
                             x.rearrange("b (t p) d -> p (b t) d", p=P)[:, n * q:n * (q + 1), :]
                             ).then_inc(x_all_loaded[q], 16)

            load_const(ident[:, :], ident_c)
            load_const(c_nat[:, :], c)
            load_x(0)
            load_const(wmod_s[:, :], wmod)
            load_const(gw_nat[:, :], gate_w)
            for i, v in enumerate((bq, bk, bv, bo)):
                load_const(b_nat[i:i + 1, :], v.rearrange("(o n) -> o n", o=1))
            for i, w in enumerate((Wq, Wk, Wv, Wo)):
                load_const(w_nat[:, i, :], w)
            for q in range(1, 4):
                load_x(q)
            load_const(rank[:, :, :], rank_c, more_loaded)
            load_const(tri[:, :], tri_c, more_loaded)
            load_const(row_s[:, ROW_KEEP:ROW_G], slots_c, more_loaded)
            load_const(maps[:, :], map_c, more_loaded)
            load_const(place[:, :], place_c, more_loaded)
            sp.dma_start(ffn_nat[:, 0, :].rearrange("p (k d) -> p k d", d=D),
                         wg.rearrange("e i d -> (e i) d").rearrange("(k p) d -> p k d", p=P)).then_inc(ffn_loaded, 16)
            sp.dma_start(ffn_nat[:, 1, :].rearrange("p (k d) -> p k d", d=D),
                         wu.rearrange("e i d -> (e i) d").rearrange("(k p) d -> p k d", p=P)).then_inc(ffn_loaded, 16)
            sp.dma_start(ffn_nat[:, 2, :].rearrange("p (e i) -> p e i", e=NE),
                         wd.rearrange("e d i -> d e i")).then_inc(ffn_loaded, 16)
            sp.wait_ge(ones_ready, 1)
            for i in range(2):
                for side in range(2):
                    r0 = SIDE * side + SHIFT
                    sp.dma_start(k_st[i][r0:r0 + 2, :, :], ones_rows.unsqueeze(1).to_broadcast([2, PAIRS, S])
                                 ).then_inc(ones_stacked, 16)
            sp.wait_ge(zeros_ready, 4)
            for i in range(2):
                for side in range(2):
                    unused = slice(SIDE * side + SHIFT + 2, SIDE * (side + 1))
                    for st in (q_st[i][side], k_st[i]):
                        sp.dma_start(st[unused, :, :], q_st[i][1 - side][unused, :, :]).then_inc(zeros_stacked, 16)
            def store_prm(batches):
                sp.dma_start(prm_d.rearrange("b p k -> p b k")[:, batches], prm[:, batches, :]).then_inc(prm_stored, 16)

            def load_x_a(n, d):
                wait(sp, misc_drained, lambda n: at["hT", n - 1] + 1 if n > 1 else 0, n, d)
                b = batch_of(n, d)
                sp.dma_start(x_a[:, :, :], x[b].rearrange("(t p) d -> p t d", p=P)).then_inc(xa_loaded, 16)
                sp.dma_start(prm_a[:, :], prm_d[b]).then_inc(xa_loaded, 16)

            def load_x_r(n, d):
                wait(sp, misc_drained, lambda n: at["x1", n - 1] + 1 if n else 0, n, d)
                b = batch_of(n, d)
                sp.dma_start(x_r[:, :, :], x[b].rearrange("(t p) d -> p t d", p=P)).then_inc(xr_loaded, 16)
                sp.dma_start(prm_t[:, :], prm_d[b]).then_inc(xr_loaded, 16)

            def stack_shift(b, g, d):
                wait(sp, misc_drained, lambda b: at["shift", NG * b + g] + 1, b, d)
                for side in range(2):
                    for part in range(2):
                        row = SIDE * side + SHIFT + part
                        src = 2 * QT * (2 * side + part)
                        sp.dma_start(q_st[b % 2][side][row:row + 1, 2 * g:2 * g + 2, :],
                                     shift_t[g % 2][src:src + 2 * QT, :]).then_inc(shift_stacked, 16)

            def store_parts(i, n, d):
                b = batch_of(n, d)
                parts, dram = ((q_parts, q_parts_d), (k_parts, k_parts_d))[i]
                wait(sp, split_ready, lambda n: 2 * n + i + 1, n, d)
                sp.dma_start(dram[b].rearrange("t r s -> r t s"), parts[:, :, :]).then_inc(parts_stored[i], 16)

            def load_parts(st, dram, lo, hi, u, parts):
                first, second = parts
                if first == second:
                    for t in range(2):
                        sp.dma_start(st[lo + DK * (2 * u + t):lo + DK * (2 * u + t + 1), :, :],
                                     dram[first, lo:hi, :].rearrange("(e j) s -> e j s", e=DK)).then_inc(stack_ready, 16)
                else:
                    sp.dma_start(st[lo + 2 * DK * u:lo + 2 * DK * (u + 1), :, :].rearrange("p j s -> p (j s)"),
                                 dram[first:second + 1:second - first, lo:hi, :].rearrange("t (e j) s -> t e (j s)", e=DK)
                                 ).then_inc(stack_ready, 16)

            def load_stacks(n, d):
                b = batch_of(n, d)
                if d is None and n <= 1:
                    sp.wait_ge(ones_stacked, 64)
                    sp.wait_ge(zeros_stacked, 128)
                both = [(side, SIDE * side, SIDE * (side + 1)) for side in range(2)]
                for side, lo, hi in both:
                    sp.dma_start(q_st[n % 2][side][lo + SHIFT:lo + SHIFT + 2, :, :],
                                 q_st[n % 2][1 - side][lo + SHIFT:lo + SHIFT + 2, :, :]).then_inc(stack_ready, 16)
                wait(sp, parts_stored[0], lambda n: 16 * (n + 1), n, d)
                for side, lo, hi in both:
                    for u, parts in enumerate(((0, 0), (1, 1), (0, 2))):
                        load_parts(q_st[n % 2][side], q_parts_d[b], lo, hi, u, parts)
                wait(sp, parts_stored[1], lambda n: 16 * (n + 1), n, d)
                for side, lo, hi in both:
                    for u, parts in enumerate(((1, 2), (1, 2), (0, 1))):
                        load_parts(k_st[n % 2], k_parts_d[b], lo, hi, u, parts)

            def store_x1(n, d):
                wait(sp, misc_drained, lambda n: at["x1", n] + 1, n, d)
                b = batch_of(n, d)
                sp.dma_start(x1_d[b].rearrange("(t p) d -> p t d", p=P), x1_s[:, :, :]).then_inc(x1_stored, 16)

            def load_row(n, d):
                wait(sp, route_step, lambda n: ROUTE_STEPS * (n - 1), n, d)
                b = batch_of(n, d)
                sp.dma_start(row[n % 2][:, :], row_d[bass.ds(b, 1), 0:ROW_G].to_broadcast([P, ROW_G])
                             ).then_inc(row_loaded[n % 2], 16)

            def values(table, high):
                return nc.values_load_multi_w_load_instructions(
                    table, engines=[mybir.EngineType.SP], min_val=0, max_val=high,
                    skip_runtime_bounds_check_because="a place within its expert's region, or behind its last row")[1]

            def fill(i):
                sp.wait_ge(map_step, MAP_STEPS * i + 2)
                for e in range(0, NE, 4):
                    n = NE * i + e
                    for j, r0 in enumerate(values(fill_row[:, n:n + 4], X_ROWS - P)):
                        sp.dma_start(xs_d[bass.ds(r0, P), :], blank[:, n + j:n + j + XW]).then_inc(filled, 16)

            def batch(b, d=None):
                if b + 2 < NB and b >= 0:
                    load_x_a(b + 2, d)
                if 0 <= b < NB:
                    stack_shift(b, 1, d)
                if b + 1 < NB:
                    store_parts(1, b + 1, d)
                    load_stacks(b + 1, d)
                if b == -1:
                    load_x_a(1, d)
                if 0 <= b - 1 < NB:
                    load_x_r(b - 1, d)
                if 0 <= b < NB:
                    stack_shift(b, 2, d)
                if 0 <= b < NB:
                    stack_shift(b, 3, d)
                if b == NB - 1:
                    fill(0)
                if b + 1 < NB:
                    stack_shift(b + 1, 0, d)
                if 0 <= b - 1 < NB:
                    store_x1(b - 1, d)
                    load_row(b - 1, d)
                if b + 2 < NB:
                    store_parts(0, b + 2, d)

            sp.wait_ge(prm_ready, 2)
            store_prm(slice(0, EARLY))
            store_parts(0, 0, None)
            sp.wait_ge(prm_stored, 16)
            batch(-1)
            sp.wait_ge(prm_ready, 3)
            sp.wait_ge(more_loaded, 16 * N_MORE)
            store_prm(slice(EARLY, NB))
            sp.dma_start(row_d, row_s[:, :]).then_inc(row_stored, 16)
            sp.wait_ge(prm_stored, 32)
            sp.wait_ge(row_stored, 16)
            for b in range(FIRST):
                batch(b)
            sp.wait_ge(one_ready, 3)
            for i in range(NSB):
                for e in range(NE):
                    r0 = ((i * REGIONS + NE) * REGION + e) * P
                    n = (NSB + i) * NE + e
                    sp.dma_start(xs_d[r0:r0 + P, :], blank[:, n:n + XW]).then_inc(blank_stored, 16)
            with sp.Fori(0, LOOP) as d:
                batch(FIRST, d)
                batch(FIRST + 1, d)
            for b in range(FIRST + 2 * LOOP, NB):
                batch(b)
            load_x_r(NB - 1, None)
            load_row(NB - 1, None)

            def load_tile(m, q, d, row):
                along(sp, y_stored[m % SLOTS], lambda q: 16 * ((PAIR * q + m) // SLOTS), q, d)
                sp.dma_start(x_in[m % SLOTS], xs_d[bass.ds(row, P), :]).then_inc(x_loaded[m % SLOTS], 16)

            def results(n, d, v):
                return ys_d[bass.ds(n * S + v * NB * S if d is None else d * (2 * S) + (n * S + v * NB * S), S), :
                            ].rearrange("(t p) d -> p t d", p=P)

            def by_tile(v):
                return v.rearrange("p (t d) -> p t d", d=D)

            def load_sums(j, q, d):
                along(sp, out_stored[j], lambda q: 16 * (q - LAG), q, d)
                n = 2 * (q - LAG) + j
                b = n if d is None else d * 2 + n
                for v in range(2):
                    sp.dma_start(by_tile(y_sum[j][:, S * v:S * (v + 1)]), results(n, d, v)).then_inc(sums_loaded[j], 16)
                sp.dma_start(by_tile(x1_l[j]), x1_d[b].rearrange("(t p) d -> p t d", p=P)).then_inc(sums_loaded[j], 16)
                sp.dma_start(gate_l[j], row_d[bass.ds(b, 1), ROW_G:ROW_N].to_broadcast([P, D])).then_inc(sums_loaded[j], 16)

            def store_out(j, q, d):
                along(sp, sum_step[j], lambda q: 6 * (q - LAG + 1), q, d)
                n = 2 * (q - LAG) + j
                b = n if d is None else d * 2 + n
                sp.dma_start(out[b].rearrange("(t p) d -> p t d", p=P), by_tile(y_sum[j][:, 0:S])).then_inc(out_stored[j], 16)

            def pair(q, d=None):
                for m in range(PAIR):
                    ahead, on = (m + AHEAD) % PAIR, (m + AHEAD) // PAIR
                    if PAIR * q + m + AHEAD < NTILE:
                        if m == 0 or ahead % 4 == 0:
                            rows = rows_of(q + on, ahead // 4 * 4, d)
                        load_tile(m + AHEAD, q, d, rows[ahead % 4])
                    if (q, m) == STORE_X1_AT:
                        store_x1(NB - 1, None)
                    if q >= LAG and m in LOAD_AT:
                        load_sums(LOAD_AT.index(m), q, d)
                    if q >= LAG and m >= PAIR - 2:
                        store_out(m - (PAIR - 2), q, d)

            def rows_of(q, m, d):
                place_q = slice(q, q + 1) if d is None else bass.ds(d + q, 1)
                return values(tile_row[:, place_q, m:m + 4].rearrange("p q m -> p (q m)"), X_ROWS - P)

            LOAD_AT = [SLOTS - AHEAD, SLOTS - AHEAD + 1]
            STORE_X1_AT = divmod(LATE.index((NB, 10)) + 2, PAIR)

            def open_superblock(i):
                sp.wait_ge(map_step, MAP_STEPS * (i + 1))
                sp.wait_ge(scattered, 16 * 2 * QT * SBB * (i + 1))
                sp.wait_ge(filled, 16 * NE * (i + 1))

            sp.wait_ge(blank_stored, 16 * NSB * NE)
            open_superblock(0)
            for m in range(AHEAD):
                if m % 4 == 0:
                    rows = rows_of(0, m, None)
                load_tile(m, 0, None, rows[m % 4])
            for q in range(LATE_PAIRS):
                pair(q)
            fill(1)
            open_superblock(1)
            with sp.Fori(0, LAG - LATE_PAIRS) as d:
                pair(LATE_PAIRS, d)
            pair(LAG)
            with sp.Fori(0, NPAIR - LAG - 2) as d:
                pair(LAG + 1, d)
            sp.wait_ge(x1_stored, 16 * NB)
            sp.dma_start(gate_last.rearrange("p (b d) -> p b d", d=D),
                         row_d[NB - SBB:NB, ROW_G:ROW_N].unsqueeze(0).to_broadcast([P, SBB, D])).then_inc(gates_loaded, 16)
            for i in range(SBB):
                sp.dma_start(by_tile(x1_last[i]), x1_d[NB - SBB + i].rearrange("(t p) d -> p t d", p=P)
                             ).then_inc(last_loaded[i], 16)
            pair(NPAIR - 1)
            for m in range(SLOTS):
                sp.wait_ge(y_stored[m], 16 * NTILE // SLOTS)
            for i in range(SBB):
                for v in range(2):
                    sp.dma_start(by_tile(y_last[i][:, S * v:S * (v + 1)]), results(NB - SBB + i, None, v)
                                 ).then_inc(last_loaded[i], 16)
            for i in range(SBB):
                sp.wait_ge(last_step[i], 3)
                sp.dma_start(out[NB - SBB + i].rearrange("(t p) d -> p t d", p=P), by_tile(y_last[i][:, 0:S])
                             ).then_inc(last_stored, 16)
            for j in range(2):
                sp.wait_ge(out_stored[j], 16 * (NPAIR - LAG))
            sp.wait_ge(last_stored, 16 * SBB)

        @block.tensor
        def _(pe):
            def setup_bank(i):
                if i >= 2:
                    pe.wait_ge(setup_drained, i - 1)
                return ps[:, i % 2, :]

            pe.wait_ge(consts_loaded, 16 * N_CONSTS)
            bank = setup_bank(SETUP_W)
            for i in range(4):
                mm = pe.transpose(bank[:, P * i:P * (i + 1)], w_nat[:, i, :], ident[:, :])
            mm.then_inc(setup_filled, 1)
            bank = setup_bank(SETUP_GC)
            pe.transpose(bank[:, 0:NE], gw_nat[:, :], ident[0:NE, 0:NE])
            pe.wait_ge(c_ready, 2)
            pe.transpose(bank[:, NE:NE + NB], c_silu[:, :], ident[0:NB, 0:NB])
            pe.transpose(bank[:, 32:36], b_nat[:, :], ident[0:4, 0:4])
            pe.transpose(bank[:, 36:38], b_perm[:, :], ident[0:2, 0:2]).then_inc(setup_filled, 1)
            bank = setup_bank(SETUP_MOD)
            pe.wait_ge(setup_drained, SETUP_GC + 1)
            for i in range(3):
                mm = pe.matmul(bank[:, NB * i:NB * (i + 1)], wmod_s[:, D * i:D * (i + 1)], c_t[:, :], start=True, stop=True)
            mm.then_inc(setup_filled, 1)

            def ffn_weights():
                bank = setup_bank(SETUP_MOD2)
                pe.matmul(bank[0:NB, 0:3 * D], c_t[:, :], wmod_s[:, 3 * D:6 * D], start=True, stop=True).then_inc(setup_filled, 1)
                pe.wait_ge(ffn_loaded, 48)
                for i, (w, c0, n, width) in enumerate(FFN_GROUPS):
                    bank = setup_bank(SETUP_FFN + i)
                    for m in range(n):
                        mm = pe.transpose(bank[0:width, P * m:P * (m + 1)],
                                          ffn_nat[:, w, width * (c0 + m):width * (c0 + m + 1)], ident[:, :])
                    mm.then_inc(setup_filled, 1)

            pe.wait_ge(setup_drained, SETUP_MOD + 1)

            def misc_step(kind, n, g, d):
                key = (lambda n: (kind, NG * n + g)) if kind in ("shift", "o") else (lambda n: (kind, n))
                wait(pe, misc_drained, lambda n: at[key(n)], n, d)
                if kind == "hT":
                    wait(pe, xn_ready, lambda n: n + 1, n, d)
                    for t in range(QT):
                        mm = pe.transpose(misc[:, P * t:P * (t + 1)], x_n[:, t, :], ident[:, :])
                elif kind == "q":
                    mm = pe.matmul(misc, wqT, h_t[:, :], start=True, stop=True)
                elif kind == "k":
                    mm = pe.matmul(misc, wkT, h_t[:, :], start=True, stop=True)
                elif kind == "v":
                    for t in range(QT):
                        mm = pe.matmul(misc[:, P * t:P * (t + 1)], h_t[:, P * t:P * (t + 1)], wvT,
                                       start=True, stop=True)
                elif kind == "shift":
                    wait(pe, shift_ready, lambda n: NG * n + g + 1, n, d)
                    mm = pe.transpose(misc_bf[0:8 * QT, 0:P],
                                      shift[g % 2][:, :, :, :, :].rearrange("p a b c q -> p (a b c q)"), identb[:, :])
                elif kind == "o":
                    wait(pe, pv_taken, lambda n: NG * n + g + 1, n, d)
                    for t in range(QT):
                        mm = pe.transpose(misc[:, P * t:P * (t + 1)], o_aug[g % 2][:, P * t:P * (t + 1)], ident[:, :])
                elif kind == "oT":
                    for t in range(QT):
                        mm = pe.transpose(misc[:, P * t:P * (t + 1)],
                                          o_n[:, t, :, :].rearrange("p h e -> p (h e)"), ident[:, :])
                elif kind == "y":
                    mm = pe.matmul(misc, woT, o_t[:, :], start=True, stop=True)
                elif kind == "x1":
                    for t in range(QT):
                        mm = pe.transpose(misc[:, P * t:P * (t + 1)], z[:, P * t:P * (t + 1)], ident[:, :])
                elif kind == "h2T":
                    wait(pe, h2_ready, lambda n: n + 1, n, d)
                    for t in range(QT):
                        mm = pe.transpose(misc[:, P * t:P * (t + 1)], h2[n % 2][:, 0, t, 0:D], ident[:, :])
                elif kind == "score":
                    for t in range(QT):
                        mm = pe.matmul(misc[:, NE * t:NE * (t + 1)], h2_t[:, P * t:P * (t + 1)], gw_t[:, :],
                                       start=True, stop=True)
                elif kind == "where":
                    wait(pe, route_step, lambda n: ROUTE_STEPS * n + 13, n, d)
                    either = route[:, 7, :, :]
                    pe.matmul(misc[:, 0:QT * NE], tri[:, :], either.rearrange("p t e -> p (t e)"), start=True, stop=False)
                    for t in range(QT - 1):
                        pe.matmul(misc[:, NE * (t + 1):QT * NE], ones[:, :],
                                  either[:, t:t + 1, :].to_broadcast([P, QT - 1 - t, NE]), start=False, stop=False)
                    mm = pe.matmul(misc[:, 0:QT * NE], ones[:, :], before[:, 0:1, :].to_broadcast([P, QT, NE]),
                                   start=False, stop=True)
                mm.then_inc(misc_filled, 1)

            def misc_steps(b, k, end, d):
                step = misc_at(b, k, end)
                if step:
                    kind, n = step
                    if kind in ("shift", "o"):
                        misc_step(kind, n // NG, n % NG, d)
                    else:
                        misc_step(kind, n, 0, d)

            def slot(b, k, d=None):
                    g, hh = divmod(k, GROUP)
                    s = NG * b + g
                    exps, looks = 0 <= s < NS, 0 <= s + 2 < NS
                    side, j = hh % 2, 2 * g + hh // 2
                    hs, gs, bs = hh ^ 1, (g + 2) % NG, b + (g + 2) // NG
                    side_s, js = hs % 2, 2 * gs + hs // 2
                    for t in range(QT):
                        if exps:
                            if hh == 0 and t == 0:
                                wait(pe, shift_stacked, lambda b: 64 * (NG * b + g + 1), b, d)
                            bank, ago = turn(QT * k + t)
                            wait(pe, exps_done, lambda b: QT * (NH * b + k) + t + 1 - ago, b, d)
                            pe.matmul(ps[:, ST_BANK + bank, :], k_st[b % 2][:, j, P * t:P * (t + 1)],
                                      q_st[b % 2][side][:, j, :], start=True, stop=True).then_inc(st_ready, 1)
                        if looks:
                            if k == 8 and t == 0:
                                wait(pe, stack_ready, lambda b: 16 * STACK_DMAS * (b + 2), b, d)
                            bank, ago = turn(QT * (GROUP * gs + hh) + t)
                            wait(pe, maxes_done, lambda b: 16 * (NG * b + g + 2) + 4 * hh + t + 1 - ago, b, d)
                            pe.matmul(ps[:, S_BANK + bank, :], q_st[bs % 2][side_s][:, js, P * t:P * (t + 1)],
                                      k_st[bs % 2][:, js, :], start=True, stop=True).then_inc(scores_ready, 1)
                        if t == 2:
                            misc_steps(b, k, 0, d)
                    if 0 <= s - 1 < NS:
                        gp, bp = (g - 1) % NG, b + (g - 1) // NG
                        if hh == 0:
                            wait(pe, exps_done, lambda b: 16 * (NG * b + g), b, d)
                            wait(pe, pv_taken, lambda b: NG * b + g - 1, b, d)
                            if gp == 0:
                                wait(pe, misc_drained, lambda b: at["v", b] + 1, b, d)
                        for i in range(GROUP):
                            mm = pe.matmul(ps[VW * i:VW * (i + 1), PV_BANK, :], v_aug[bp % 2][:, hh, GROUP * gp + i, :],
                                           probs[:, gp % 2, i, S * hh:S * (hh + 1)], start=(hh == 0), stop=(hh == QT - 1))
                        if hh == QT - 1:
                            mm.then_inc(pv_ready, 1)
                    misc_steps(b, k, 1, d)

            def batch(b, d=None):
                for k in range(NH):
                    slot(b, k, d)

            def count_tokens(i, bank):
                pe.wait_ge(map_step, MAP_STEPS * i + 1)
                pe.matmul(ps[0:1, bank, 0:NE], ones[:, 0:1], counts, start=True, stop=True).then_inc(counts_summed, 1)

            misc_step("hT", 0, 0, None)
            misc_step("q", 0, 0, None)
            misc_step("k", 0, 0, None)
            ffn_weights()
            pe.wait_ge(setup_drained, N_SETUP)
            pe.wait_ge(fills_done, 6)
            pe.wait_ge(more_loaded, 16 * N_MORE)
            for b in range(-1, FIRST):
                batch(b)
            with pe.Fori(0, LOOP) as d:
                batch(FIRST, d)
                batch(FIRST + 1, d)
            for b in range(FIRST + 2 * LOOP, NB - 1):
                batch(b)
            for k in range(NH):
                slot(NB - 1, k)
                if k == MAP_AT:
                    count_tokens(0, COUNT_BANK)
            for k in range(GROUP):
                slot(NB, k)

            pe.wait_ge(map_step, MAP_STEPS)
            pe.wait_ge(exps_done, QT * NH * NB)

            def turn_rows(m, q, d):
                along(pe, x_loaded[m % SLOTS], lambda q: 16 * ((PAIR * q + m) // SLOTS + 1), q, d)
                along(pe, xt_taken, lambda q: PAIR * q + m, q, d)
                pe.transpose(ps[:, XT_BANK, 0:P], x_in[m % SLOTS][:, 0:D], ident[:, :]).then_inc(xt_ready, 1)

            def up(m, q, d, e):
                along(pe, xt_taken, lambda q: PAIR * q + m + 1, q, d)
                along(pe, hid_ready, lambda q: PAIR * q + m - 1, q, d)
                for i, w in enumerate((wg_t, wu_t)):
                    mm = pe.matmul(ps[:, GU_BANK + m % 2, INTER * i:INTER * (i + 1)], x_t[m % 2],
                                   w[:, :, :].rearrange("p c h -> p (c h)")[:, bass.ds(e * INTER, INTER)],
                                   start=True, stop=True)
                mm.then_inc(gu_ready, 1)

            def turn_hidden(m, q, d):
                along(pe, hid_ready, lambda q: PAIR * q + m + 1, q, d)
                along(pe, hidt_taken, lambda q: PAIR * q + m, q, d)
                for i in range(2):
                    mm = pe.transpose(ps[0:HALF, HT_BANK, P * i:P * (i + 1)], hid[m % 2][:, HALF * i:HALF * (i + 1)],
                                      ident[:, :])
                mm.then_inc(hidt_ready, 1)

            def down(m, q, d, e):
                along(pe, hidt_taken, lambda q: PAIR * q + m + 1, q, d)
                along(pe, y_taken, lambda q: PAIR * q + m - 1, q, d)
                for i in range(2):
                    mm = pe.matmul(ps[:, Y_BANK + m % 2, 0:D], hid_t[m % 2][:, P * i:P * (i + 1)],
                                   wd_t[:, bass.ds(e * 2 + i, 1), :].rearrange("p a d -> p (a d)"),
                                   start=(i == 0), stop=(i == 1))
                mm.then_inc(y_ready, 1)

            def pair(q, d=None):
                experts = {}

                def read_experts(m, back=0):
                    place_q = slice(q - back, q - back + 1) if d is None else bass.ds(d + (q - back), 1)
                    experts.update(zip(range(m - back * PAIR, min(m + 4, PAIR) - back * PAIR), nc.values_load_multi_w_load_instructions(
                        tile_expert[:, place_q, m:m + 4].rearrange("p q m -> p (q m)"),
                        engines=[mybir.EngineType.PE], min_val=0, max_val=NE - 1,
                        skip_runtime_bounds_check_because="a count of at most NE experts, limited to NE - 1")[1]))

                if PAIR * q < NTILE:
                    read_experts(0)
                for m in range(PAIR):
                    i = PAIR * q + m
                    if i < NTILE:
                        up(m, q, d, experts[m])
                    if i + 1 < NTILE:
                        turn_rows(m + 1, q, d)
                    if i < NTILE:
                        if m % 4 == 2 and m + 2 < PAIR:
                            read_experts(m + 2)
                    if m == 0 and i:
                        read_experts((PAIR - 2) // 4 * 4, 1)
                    if 0 <= i - 1 < NTILE:
                        turn_hidden(m - 1, q, d)
                    if 0 <= i - 2 < NTILE:
                        down(m - 2, q, d, experts[m - 2])
                    if i < len(LATE):
                        slot(*LATE[i])
                    elif i == len(LATE):
                        count_tokens(NSB - 1, MISC_BANK)

            turn_rows(0, 0, None)
            for q in range(LATE_PAIRS):
                pair(q)
            with pe.Fori(0, LAG - LATE_PAIRS) as d:
                pair(LATE_PAIRS, d)
            pe.wait_ge(map_step, MAP_STEPS * NSB)
            with pe.Fori(0, NPAIR - LAG - 1) as d:
                pair(LAG, d)
            pair(NPAIR - 1)
            pair(NPAIR)

        @block.scalar
        def _(act):
            act.wait_ge(consts_loaded, 16 * N_CONSTS)
            act.activation(c_silu[:, :], c_nat[:, :], ACT.Silu).then_inc(c_ready, 1)
            act.copy(b_perm[:, :].rearrange("p (h e j) -> p j h e", h=2, e=DK),
                     b_nat[0:2, :].rearrange("p (j h e) -> p j h e", h=2, e=DK)).then_inc(c_ready, 1)
            act.wait_ge(setup_filled, SETUP_W + 1)
            bank = ps[:, SETUP_W % 2, :]
            for i in range(2):
                act.copy(w_t[:, i, :].rearrange("p (h e j) -> p j h e", h=2, e=DK),
                         bank[:, P * i:P * (i + 1)].rearrange("p (j h e) -> p j h e", h=2, e=DK))
            act.copy(w_t[:, 2:4, :].rearrange("p a d -> p (a d)"), bank[:, 2 * P:4 * P]).then_inc(setup_drained, 1)
            act.wait_ge(setup_filled, SETUP_GC + 1)
            bank = ps[:, SETUP_GC % 2, :]
            act.copy(gw_t[:, :], bank[:, 0:NE])
            act.copy(bias[:, 2:4], bank[:, 34:36])
            act.copy(bias[:, 0:2], bank[:, 36:38])
            act.copy(c_t[:, :], bank[:, NE:NE + NB]).then_inc(setup_drained, 1)
            act.wait_ge(setup_filled, SETUP_MOD + 1)
            act.copy(mod[:, :, :].rearrange("p a b -> p (a b)"), ps[:, SETUP_MOD % 2, 0:3 * NB]).then_inc(setup_drained, 1)

            def ffn_weights():
                act.wait_ge(setup_filled, SETUP_MOD2 + 1)
                act.copy(mod_r[:, :, :].rearrange("p a d -> p (a d)"), ps[0:NB, SETUP_MOD2 % 2, 0:3 * D]).then_inc(setup_drained, 1)
                for i, (w, c0, n, width) in enumerate(FFN_GROUPS):
                    act.wait_ge(setup_filled, SETUP_FFN + i + 1)
                    act.copy((wg_t, wu_t, wd_t)[w][:, c0:c0 + n, :].rearrange("p k d -> p (k d)"),
                             ps[0:width, (SETUP_FFN + i) % 2, 0:P * n]).then_inc(setup_drained, 1)

            def prm_of(n):
                return prm_a if n else prm[:, 0, :]

            def normalise(n, d, tiles):
                rows = x_a if n else x_all
                if n == 0:
                    act.wait_ge(prm_ready, 1)
                elif tiles[0] == 0:
                    wait(act, xa_loaded, lambda n: 32 * n, n, d)
                    wait(act, misc_filled, lambda n: at["hT", n - 1] + 1 if n else 0, n, d)
                for t in tiles:
                    ins = act.activation(x_n[:, t, :], rows[:, t, :], ACT.Identity,
                                         scale=prm_of(n)[:, RSTD + t:RSTD + t + 1], bias=prm_of(n)[:, NMR + t:NMR + t + 1])
                if tiles[-1] == QT - 1:
                    ins.then_inc(xn_ready, 1)

            def misc_drain(kind, n, d):
                wait(act, misc_filled, lambda n: at[kind, n] + 1, n, d)
                if kind == "hT":
                    ins = act.activation(h_t[:, :], misc, ACT.Identity, scale=prm_of(n)[:, CA:CA + 1], bias=prm_of(n)[:, SA:SA + 1])
                elif kind in ("q", "k"):
                    full, i = (q32, 0) if kind == "q" else (k32, 1)
                    wait(act, split_ready, lambda n: 2 * (n - 1) + i + 1, n, d)
                    ins = act.activation(full[:, :], misc, ACT.Identity, bias=bias[:, i:i + 1])
                elif kind == "v":
                    wait(act, pv_ready, lambda n: NG * (n - 1), n, d)
                    ins = act.copy(v_aug[n % 2][:, :, :, 0:DK], misc.rearrange("p (t h e) -> p t h e", t=QT, e=DK))
                elif kind == "oT":
                    ins = act.activation(o_t[:, :], misc, ACT.Identity, bias=bias[:, 2:3])
                elif kind == "h2T":
                    ins = act.copy(h2_t[:, :], misc)
                elif kind == "y":
                    wait(act, xr_loaded, lambda n: 32 * (n + 1), n, d)
                    ins = act.activation(z[:, :], misc, ACT.Identity, scale=prm_t[:, GA:GA + 1], bias=prm_t[:, GABO:GABO + 1])
                ins.then_inc(misc_drained, 1)

            def slot(b, k, d=None):
                    g, hh = divmod(k, GROUP)
                    s = NG * b + g
                    for t in range(QT):
                        if hh == 0 and t == 1 and 0 <= s - 2 < NS:
                            wait(act, pv_ready, lambda b: NG * b + g - 1, b, d)
                            if s - 4 >= 0:
                                wait(act, misc_filled, lambda b: at["o", NG * b + g - 4] + 1, b, d)
                            act.copy(o_aug[g % 2][:, :], ps[:, PV_BANK, :]).then_inc(pv_taken, 1)
                        if 0 <= s < NS:
                            wait(act, st_ready, lambda b: QT * (NH * b + k) + t + 1, b, d)
                            act.activation(probs[:, g % 2, hh, S * t:S * (t + 1)], ps[:, ST_BANK + turn(QT * k + t)[0], :],
                                           ACT.Exp, scale=SCALE).then_inc(exps_done, 1)
                        step = misc_at(b, k, 0)
                        if t == 2 and step and step[0] == "h2T":
                            misc_drain(*step, d)
                    if k == 12 and 0 <= b - 2 < NB:
                        wait(act, route_step, lambda b: ROUTE_STEPS * (b - 2) + 13, b, d)
                        act.activation(odds[:, 0, :], top[:, 3, :], ACT.Exp).then_inc(odds_ready, 1)
                    if 7 <= k < 7 + QT and b + 2 < NB:
                        normalise(b + 2, d, [k - 7])
                    step = misc_at(b, k, 1)
                    if step and step[0] in ("hT", "q", "k", "v", "oT", "y"):
                        misc_drain(*step, d)

            def batch(b, d=None):
                for k in range(NH):
                    slot(b, k, d)

            normalise(0, None, range(QT))
            misc_drain("hT", 0, None)
            misc_drain("q", 0, None)
            misc_drain("k", 0, None)
            ffn_weights()
            for b in range(-1, FIRST):
                batch(b)
            with act.Fori(0, LOOP) as d:
                batch(FIRST, d)
                batch(FIRST + 1, d)
            for b in range(FIRST + 2 * LOOP, NB):
                batch(b)
            for k in range(GROUP):
                slot(NB, k)

            def pair(q, d=None):
                for m in range(PAIR):
                    i = PAIR * q + m
                    if i + 1 < NTILE:
                        along(act, xt_ready, lambda q: PAIR * q + m + 2, q, d)
                        along(act, gu_ready, lambda q: PAIR * q + m, q, d)
                        act.copy(x_t[(m + 1) % 2], ps[:, XT_BANK, 0:P]).then_inc(xt_taken, 1)
                    if i < NTILE:
                        along(act, gu_ready, lambda q: PAIR * q + m + 1, q, d)
                        along(act, hid_ready, lambda q: PAIR * q + m - 1, q, d)
                        act.activation(silu[m % 2], ps[:, GU_BANK + m % 2, 0:INTER], ACT.Silu).then_inc(silu_done, 1)
                    if 0 <= i - 2 < NTILE:
                        along(act, y_ready, lambda q: PAIR * q + m - 1, q, d)
                        along(act, y_stored[(m - 2) % SLOTS], lambda q: 16 * ((PAIR * q + m - 2) // SLOTS), q, d)
                        act.activation(y_out[(m - 2) % SLOTS], ps[:, Y_BANK + m % 2, 0:D], ACT.Identity,
                                       scale=x_in[(m - 2) % SLOTS][:, D:D + 1]).then_inc(y_taken, 1)
                    if i < len(LATE):
                        slot(*LATE[i])

            act.wait_ge(xt_ready, 1)
            act.copy(x_t[0], ps[:, XT_BANK, 0:P]).then_inc(xt_taken, 1)
            for q in range(LATE_PAIRS):
                pair(q)
            with act.Fori(0, NPAIR - LATE_PAIRS - 1) as d:
                pair(LATE_PAIRS, d)
            pair(NPAIR - 1)
            pair(NPAIR)

        @block.vector
        def _(dve):
            steps = [0]

            def settled(ins):
                steps[0] += 1
                ins.then_inc(dve_step, 1)
                dve.wait_ge(dve_step, steps[0])

            def inverse_root(step, v, y, t):
                step(dve.tensor_scalar(y.bitcast(I32), v.bitcast(I32), -0.5, ROOT_SEED, ALU.mult, ALU.add))
                for _ in range(3):
                    step(dve.scalar_tensor_tensor(t, y, -0.5, y, ALU.mult, ALU.mult))
                    step(dve.tensor_tensor(t, t, v, ALU.mult))
                    step(dve.scalar_tensor_tensor(y, t, 1.5, y, ALU.add, ALU.mult))

            settled(dve.memset(before[:, :, :], 0.0))
            def moments(quarters):
                for q in quarters:
                    dve.wait_ge(x_all_loaded[q], 16)
                    for t in range(NT // 4 * q, NT // 4 * (q + 1)):
                        ins = dve.bn_stats(st6[:, t, :], x_all[:, t, :])
                    settled(ins)
                    for t in range(NT // 4 * q, NT // 4 * (q + 1)):
                        ins = dve.bn_aggr(mv[:, t, :], st6[:, t, :])
                settled(ins)
                tiles = slice(NT // 4 * quarters[0], NT // 4 * (quarters[-1] + 1))
                batches = slice(NB // 4 * quarters[0], NB // 4 * (quarters[-1] + 1))
                settled(dve.tensor_scalar(rs4[:, 0, tiles], mv[:, tiles, 1], EPS, None, ALU.add))
                inverse_root(settled, rs4[:, 0, tiles], rs4[:, 1, tiles], rs4[:, 2, tiles])
                rstd = rs4[:, 1, tiles].rearrange("p (b t) -> p b t", t=QT)
                settled(dve.tensor_copy(prm[:, batches, RSTD:RSTD + QT], rstd))
                return dve.scalar_tensor_tensor(prm[:, batches, NMR:NMR + QT],
                                                mv[:, tiles, 0].rearrange("p (b t) -> p b t", t=QT), -1.0, rstd, ALU.mult, ALU.mult)

            def away_from_zero(gate, scratch, to):
                sign, size, neg = scratch
                settled(dve.tensor_scalar(sign, gate, 0.0, 2.0, ALU.is_ge, ALU.mult))
                settled(dve.tensor_scalar(sign, sign, -1.0, None, ALU.add))
                settled(dve.tensor_scalar(neg, gate, -1.0, None, ALU.mult))
                settled(dve.tensor_tensor(size, neg, gate, ALU.max))
                settled(dve.tensor_scalar(size, size, 0.25, None, ALU.max))
                return dve.tensor_tensor(to, sign, size, ALU.mult)

            settled(moments([0]))
            dve.wait_ge(setup_drained, SETUP_MOD + 1)
            settled(dve.tensor_copy(prm[:, :, SA], mod[:, 0, :]))
            dve.tensor_scalar(prm[:, :, CA], mod[:, 1, :], 1.0, None, ALU.add).then_inc(prm_ready, 1)
            settled(away_from_zero(mod[:, 2, :], (gtmp[:, i, :] for i in range(3)), prm[:, :, GA]))
            dve.tensor_scalar(prm[:, :, GABO], prm[:, :, GA], bias[:, 3:4], None, ALU.mult).then_inc(prm_ready, 1)
            settled(moments([1, 2, 3]))
            dve.wait_ge(setup_drained, SETUP_MOD2 + 1)
            settled(dve.tensor_copy(row_s[:, ROW_S:ROW_S + D], mod_r[:, 0, :]))
            settled(dve.tensor_scalar(row_s[:, ROW_C:ROW_C + D], mod_r[:, 1, :], 1.0, None, ALU.add))
            away_from_zero(mod_r[:, 2, :], (gtmp_r[:, i, :] for i in range(3)), row_s[:, ROW_G:ROW_N]).then_inc(prm_ready, 1)
            dve.wait_ge(more_loaded, 16 * N_MORE)

            def misc_drain(kind, n, g, d):
                key = (lambda n: (kind, NG * n + g)) if kind in ("shift", "o") else (lambda n: (kind, n))
                if kind == "shift":
                    wait(dve, misc_filled, lambda n: at[key(n)] + 1, n, d)
                    wait(dve, shift_stacked, lambda n: 64 * (NG * n + g - 1), n, d)
                    dve.tensor_copy(shift_t[g % 2][:, :], misc_bf[0:8 * QT, 0:P]).then_inc(misc_drained, 1)
                elif kind == "o":
                    wait(dve, misc_filled, lambda n: at[key(n)] + 1, n, d)
                    v = misc.rearrange("p (t i e) -> p t i e", t=QT, i=GROUP)
                    dve.reciprocal(o_rs[:, :, :], v[:, :, :, DK]).then_inc(o_rs_ready, 1)
                    wait(dve, o_rs_ready, lambda n: NG * n + g + 1, n, d)
                    dve.tensor_tensor(o_n[:, :, GROUP * g:GROUP * (g + 1), :], v[:, :, :, 0:DK],
                                      o_rs[:, :, :].unsqueeze(3).to_broadcast([P, QT, GROUP, DK]), ALU.mult
                                      ).then_inc(misc_drained, 1)
                elif kind == "x1":
                    wait(dve, misc_filled, lambda n: at[key(n)] + 1, n, d)
                    wait(dve, xr_loaded, lambda n: 32 * (n + 1), n, d)
                    wait(dve, x1_stored, lambda n: 16 * n, n, d)
                    wait(dve, h2_ready, lambda n: n, n, d)
                    dve.tensor_tensor(x1_s[:, :, :].rearrange("p t d -> p (t d)"), misc,
                                      x_r[:, :, :].rearrange("p t d -> p (t d)"), ALU.add).then_inc(misc_drained, 1)

            def wide(v):
                return v.unsqueeze(2).to_broadcast([P, QT, NE])

            def router_step(i, n, d):
                scores, left, eq, tmp, place_all, place_1, place_2, either = (route[:, v, :, :] for v in range(8))
                best, second, first_rank, margin = (top[:, v, :] for v in range(4))
                odds_to, odds_sum = odds[:, 0, :], odds[:, 1, :]
                weight, result_at = h2[n % 2][:, :, :, D], h2[n % 2][:, :, :, D + 1].bitcast(U32)
                one_hot, two_hot = chosen[:, 0, :, :], chosen[:, 1, :, :]
                if 2 <= i <= 13:
                    wait(dve, route_step, lambda n: ROUTE_STEPS * n + i - 1, n, d)
                elif 16 <= i <= 24:
                    wait(dve, route_step, lambda n: ROUTE_STEPS * n + i - 2, n, d)
                if i == 0:
                    wait(dve, misc_filled, lambda n: at["score", n] + 1, n, d)
                    wait(dve, route_step, lambda n: ROUTE_STEPS * n, n, d)
                    dve.tensor_copy(scores.rearrange("p t e -> p (t e)"), misc[:, 0:QT * NE]).then_inc(misc_drained, 1)
                elif i == 14:
                    wait(dve, misc_filled, lambda n: at["where", n] + 1, n, d)
                    wait(dve, row_loaded[n % 2], lambda n: 16 * (n // 2 + 1), n, d)
                    dve.tensor_tensor(place_all, misc[:, 0:QT * NE].rearrange("p (t e) -> p t e", e=NE),
                                      row[n % 2][:, ROW_BASE:ROW_G].unsqueeze(1).to_broadcast([P, QT, NE]), ALU.add
                                      ).then_inc(misc_drained, 1)
                else:
                    if i in (1, 7):
                        if i == 1:
                            wait(dve, misc_drained, lambda n: at["score", n] + 1, n, d)
                        ins = dve.tensor_reduce(best if i == 1 else second, scores if i == 1 else left, AX.X, ALU.max)
                    elif i in (2, 8):
                        ins = dve.tensor_tensor(eq, scores if i == 2 else left, wide(best if i == 2 else second), ALU.is_equal)
                    elif i in (3, 9):
                        ins = dve.tensor_tensor(tmp, eq, rank[:, :, :], ALU.mult)
                    elif i in (4, 10):
                        ins = dve.tensor_reduce(first_rank, tmp, AX.X, ALU.max)
                    elif i in (5, 11):
                        ins = dve.tensor_tensor(one_hot if i == 5 else two_hot, tmp, wide(first_rank), ALU.is_equal)
                    elif i == 6:
                        ins = dve.scalar_tensor_tensor(left, one_hot, -3.0e38, scores, ALU.mult, ALU.add)
                    elif i == 12:
                        ins = dve.tensor_tensor(either, one_hot, two_hot, ALU.add)
                    elif i == 13:
                        ins = dve.tensor_tensor(margin, second, best, ALU.subtract)
                    elif i == 15:
                        wait(dve, misc_drained, lambda n: at["where", n] + 1, n, d)
                        ins = dve.tensor_tensor(place_1, place_all, one_hot, ALU.mult)
                    elif i == 16:
                        ins = dve.tensor_tensor(place_2, place_all, two_hot, ALU.mult)
                    elif i == 17:
                        ins = dve.tensor_reduce(rows_f[:, :], route[:, 5:7, :, :].rearrange("p a t e -> p (a t) e"),
                                                AX.X, ALU.add)
                    elif i == 18:
                        wait(dve, scattered, lambda n: 16 * 2 * QT * n, n, d)
                        ins = dve.tensor_copy(rows_o[:, :], rows_f[:, :])
                    elif i == 19:
                        ins = dve.tensor_reduce(chosen_n[:, :], either.rearrange("p t e -> p e t"), AX.X, ALU.add)
                    elif i == 20:
                        ins = dve.tensor_tensor(before[:, 1, :], before[:, 0, :], chosen_n[:, :], ALU.add)
                    elif i == 21:
                        ins = dve.tensor_scalar(before[:, 0, :], before[:, 1, :], row[n % 2][:, ROW_KEEP:ROW_KEEP + 1], None,
                                                ALU.mult)
                    elif i == 22:
                        wait(dve, odds_ready, lambda n: n + 1, n, d)
                        ins = dve.tensor_scalar(odds_sum, odds_to, 1.0, None, ALU.add)
                    elif i == 23:
                        ins = dve.reciprocal(weight[:, 0, :], odds_sum)
                    elif i == 24:
                        ins = dve.tensor_tensor(weight[:, 1, :], odds_to, weight[:, 0, :], ALU.mult)
                    elif i == 25:
                        ins = dve.tensor_scalar(result_at, place[:, 0:2 * QT].rearrange("p (v t) -> p v t", t=QT),
                                                row[n % 2][:, ROW_AT:ROW_AT + 1], None, ALU.add)
                    elif i == 26:
                        ins = dve.tensor_copy(chosen_all[:, batch_of(n, d) if d is None else bass.ds(batch_of(n, d), 1), :],
                                              chosen_n[:, :])
                    ins.then_inc(route_step, 1)

            def norm_step(i, n, d):
                v, y, nmr, t = (ln2[:, j, :] for j in range(4))
                if i == 0:
                    wait(dve, stats_ready, lambda n: n + 1, n, d)
                    wait(dve, h2_ready, lambda n: n, n, d)
                    ins = dve.tensor_scalar(v, mv_b[:, :, 1], EPS, None, ALU.add)
                else:
                    wait(dve, ln_step, lambda n: LN_STEPS * n + i, n, d)
                    if i == 1:
                        ins = dve.tensor_scalar(y.bitcast(I32), v.bitcast(I32), -0.5, ROOT_SEED, ALU.mult, ALU.add)
                    elif i == LN_STEPS - 1:
                        ins = dve.scalar_tensor_tensor(nmr, mv_b[:, :, 0], -1.0, y, ALU.mult, ALU.mult)
                    elif i % 3 == 2:
                        ins = dve.scalar_tensor_tensor(t, y, -0.5, y, ALU.mult, ALU.mult)
                    elif i % 3 == 0:
                        ins = dve.tensor_tensor(t, t, v, ALU.mult)
                    else:
                        ins = dve.scalar_tensor_tensor(y, t, 1.5, y, ALU.add, ALU.mult)
                ins.then_inc(ln_step, 1)

            BATCH_TILES = NH * QT
            AGGR_AT = 49
            NORM_AT = [50 + i for i in range(LN_STEPS)]
            ROUTER_AT = ([BATCH_TILES + 27 + i for i in range(14)]
                         + [BATCH_TILES + 53 + i for i in range(13)])

            def later_steps(b, spot, d):
                for lag in (1, 2, 3):
                    n, place = b - lag, BATCH_TILES * (lag - 1) + spot
                    if 0 <= n < NB:
                        if place in NORM_AT:
                            norm_step(NORM_AT.index(place), n, d)
                        if place in ROUTER_AT:
                            router_step(ROUTER_AT.index(place), n, d)

            def slot(b, k, d=None):
                    g, hh = divmod(k, GROUP)
                    s = NG * b + g
                    looks = 0 <= s + 2 < NS
                    for t in range(QT):
                        spot = QT * k + t
                        if 0 <= b - 1 < NB:
                            if k == 11 and t == 0:
                                wait(dve, misc_drained, lambda b: at["x1", b - 1] + 1, b, d)
                                wait(dve, stats_ready, lambda b: b - 1, b, d)
                            if spot == AGGR_AT:
                                wait(dve, x1_stats, lambda b: 4 * b, b, d)
                                wait(dve, ln_step, lambda b: LN_STEPS * (b - 1), b, d)
                        if looks:
                            hs = hh ^ 1
                            wait(dve, scores_ready, lambda b: 16 * (NG * b + g + 2) + 4 * hh + t + 1, b, d)
                            bank = turn(QT * (GROUP * ((g + 2) % NG) + hh) + t)[0]
                            dve.tensor_reduce(maxes[g % 2][:, hs % 2, hs // 2, t:t + 1], ps[:, S_BANK + bank, :],
                                              AX.X, ALU.max).then_inc(maxes_done, 1)
                        if 0 <= b - 1 < NB:
                            if k == 11:
                                dve.bn_stats(st_b[:, t, :], x1_s[:, t, :]).then_inc(x1_stats, 1)
                            if spot == AGGR_AT:
                                for i in range(QT):
                                    ins = dve.bn_aggr(mv_b[:, i, :], st_b[:, i, :])
                                ins.then_inc(stats_ready, 1)
                        later_steps(b, spot, d)
                    if looks and hh == GROUP - 1:
                        wait(dve, maxes_done, lambda b: 16 * (NG * b + g + 3), b, d)
                        if s >= 0:
                            wait(dve, misc_filled, lambda b: at["shift", NG * b + g] + 1, b, d)
                        m = maxes[g % 2][:, :, :, :].rearrange("p a c q -> p a (c q)")
                        high, low = (shift[g % 2][:, :, i, :, :].rearrange("p a c q -> p a (c q)") for i in range(2))
                        dve.tensor_scalar(high, m, -1.0, None, ALU.mult).then_inc(shift_high, 1)
                        wait(dve, shift_high, lambda b: NG * b + g + 3, b, d)
                        dve.scalar_tensor_tensor(low, m, -1.0, high, ALU.mult, ALU.subtract).then_inc(shift_ready, 1)
                    step = misc_at(b, k, 1)
                    if step and step[0] in ("shift", "o"):
                        misc_drain(step[0], step[1] // NG, step[1] % NG, d)
                    elif step and step[0] == "x1":
                        misc_drain(step[0], step[1], 0, d)

            def batch(b, d=None):
                for k in range(NH):
                    slot(b, k, d)

            def make_map(s, i, bank):
                count = ps[0:1, bank, 0:NE]
                if i == 0:
                    dve.wait_ge(route_step, ROUTE_STEPS * SBB * (s + 1))
                    ins = dve.tensor_reduce(counts, chosen_all[:, SBB * s:SBB * (s + 1), :].rearrange("p b e -> p e b"), AX.X, ALU.add)
                else:
                    dve.wait_ge(map_step, MAP_STEPS * s + i)
                if i == 1:
                    dve.wait_ge(counts_summed, s + 1)
                    ins = dve.tensor_tensor(fill_row[:, NE * s:NE * (s + 1)], count,
                                            maps[:, MAP_FILL + NE * s:MAP_FILL + NE * (s + 1)], ALU.add)
                elif i == 2:
                    ins = dve.tensor_tensor(needs, count.unsqueeze(2).to_broadcast([1, NE, FULL]),
                                            maps[:, MAP_THR:MAP_FILL].unsqueeze(1).to_broadcast([1, NE, FULL]), ALU.is_gt)
                elif i == 3:
                    ins = dve.tensor_reduce(need, needs, AX.X, ALU.add)
                elif i == 4:
                    ins = dve.tensor_tensor(uptos, need.unsqueeze(1).to_broadcast([1, NE, NE]),
                                            maps[:, MAP_TRI:MAP_THR].rearrange("p (e f) -> p e f", f=NE), ALU.mult)
                elif i == 5:
                    ins = dve.tensor_reduce(upto, uptos, AX.X, ALU.add)
                elif i == 6:
                    ins = dve.tensor_tensor(done, upto.unsqueeze(1).to_broadcast([1, TILES, NE]),
                                            maps[:, MAP_TILE:MAP_TRI].unsqueeze(2).to_broadcast([1, TILES, NE]), ALU.is_le)
                elif i == 7:
                    ins = dve.tensor_reduce(owner, done, AX.X, ALU.add)
                elif i == 8:
                    ins = dve.tensor_tensor(done, done, need.unsqueeze(1).to_broadcast([1, TILES, NE]), ALU.mult)
                elif i == 9:
                    ins = dve.tensor_reduce(start, done, AX.X, ALU.add)
                elif i == 10:
                    ins = dve.tensor_tensor(start, maps[:, MAP_TILE:MAP_TRI], start, ALU.subtract)
                elif i == 11:
                    ins = dve.scalar_tensor_tensor(start, owner, float(REGION), start, ALU.mult, ALU.add)
                elif i in (12, 13):
                    table, v, ops = ((tile_row, start, (float(s * REGIONS * REGION), float(P), ALU.add, ALU.mult)),
                                     (tile_expert, owner, (float(NE - 1), None, ALU.min)))[i - 12]
                    ins = dve.tensor_scalar(table[:, LAG * s:LAG * (s + 1), 0:PAIR], v.rearrange("p (q m) -> p q m", m=PAIR), *ops)
                ins.then_inc(map_step, 1)

            for b in range(-1, FIRST):
                batch(b)
            with dve.Fori(0, LOOP) as d:
                batch(FIRST, d)
                batch(FIRST + 1, d)
            for b in range(FIRST + 2 * LOOP, NB - 1):
                batch(b)
            for k in range(NH):
                slot(NB - 1, k)
                if k == MAP_AT:
                    for table in (tile_row, tile_expert):
                        settled(dve.memset(table[:, :, :], 0))
                    make_map(0, 0, COUNT_BANK)
                for i in range(1 + MAP_BURST * (k - MAP_AT - 1), 1 + MAP_BURST * (k - MAP_AT)):
                    if 0 < i < MAP_STEPS:
                        make_map(0, i, COUNT_BANK)
            for k in range(GROUP):
                slot(NB, k)

            def sum_part(j, i, q, d):
                op, half = divmod(i, 2)
                own = slice(half * S // 2, (half + 1) * S // 2)
                y = y_sum[j][:, own]
                if i == 0:
                    along(dve, sums_loaded[j], lambda q: 64 * (q - LAG + 1), q, d)
                if op:
                    along(dve, sum_step[j], lambda q: 6 * (q - LAG) + i - 1, q, d)
                if op == 0:
                    ins = dve.tensor_tensor(y, y, y_sum[j][:, S + half * S // 2:S + (half + 1) * S // 2], ALU.add)
                elif op == 1:
                    ins = gated(dve, y, gate_l[j])
                else:
                    ins = dve.tensor_tensor(y, y, x1_l[j][:, own], ALU.add)
                ins.then_inc(sum_step[j], 1)

            SUM_AT = [PAIR - 8, PAIR - 7]

            def pair(q, d=None):
                for m in range(PAIR):
                    i = PAIR * q + m
                    if 0 <= i - 1 < NTILE:
                        along(dve, hidt_ready, lambda q: PAIR * q + m, q, d)
                        along(dve, y_ready, lambda q: PAIR * q + m - 2, q, d)
                        dve.tensor_copy(hid_t[(m - 1) % 2], ps[0:HALF, HT_BANK, 0:2 * P]).then_inc(hidt_taken, 1)
                    if i < NTILE:
                        along(dve, silu_done, lambda q: PAIR * q + m + 1, q, d)
                        along(dve, hidt_ready, lambda q: PAIR * q + m - 1, q, d)
                        dve.tensor_tensor(hid[m % 2], silu[m % 2], ps[:, GU_BANK + m % 2, INTER:2 * INTER], ALU.mult
                                          ).then_inc(hid_ready, 1)
                    late = i - len(LATE)
                    if late < 0:
                        slot(*LATE[i])
                    elif late == 0:
                        make_map(NSB - 1, 0, MISC_BANK)
                    elif q < LATE_PAIRS:
                        for step in range(1 + MAP_BURST * (late - 1), min(1 + MAP_BURST * late, MAP_STEPS)):
                            make_map(NSB - 1, step, MISC_BANK)
                    if LAG <= q < NPAIR:
                        for j in range(2):
                            if 0 <= m - SUM_AT[j] < 6:
                                sum_part(j, m - SUM_AT[j], q, d)

            for q in range(LATE_PAIRS):
                pair(q)
            with dve.Fori(0, LAG - LATE_PAIRS) as d:
                pair(LATE_PAIRS, d)
            with dve.Fori(0, NPAIR - LAG - 1) as d:
                pair(LAG, d)
            pair(NPAIR - 1)
            pair(NPAIR)
            for i in range(SBB):
                if i not in LAST_BY_POOL:
                    last_sum(dve, i)

        @block.gpsimd
        def _(pool):
            pool.memset(ones_rows, 1.0).then_inc(ones_ready, 1)
            pool.memset(one[:, :], 1.0).then_inc(one_ready, 1)
            pool.memset(blank[:, :], 0.0).then_inc(one_ready, 1)
            pool.wait_ge(one_ready, 2)
            for i in range(2):
                for side in range(2):
                    pool.memset(q_st[i][side][SIDE * (1 - side):SIDE * (2 - side), :, :], 0.0).then_inc(zeros_ready, 1)
                    pool.wait_ge(zeros_ready, 2 * i + side + 1)
            for i in range(2):
                pool.memset(v_aug[i][:, :, :, DK + 1:VW], 0.0).then_inc(fills_done, 1)
                pool.memset(v_aug[i][:, :, :, DK:DK + 1], 1.0).then_inc(fills_done, 1)

            pool.wait_ge(consts_loaded, 16 * N_CONSTS)
            pool.tensor_copy(identb[:, :], ident[:, :]).then_inc(fills_done, 1)
            pool.memset(ones[:, :], 1.0).then_inc(fills_done, 1)
            pool.wait_ge(more_loaded, 16 * N_MORE)
            pool.tensor_copy(blank[:, XW - 1:].bitcast(U32), place[:, 2 * QT:]).then_inc(one_ready, 1)

            def split(kind, n, d):
                i = 0 if kind == "q" else 1
                full, parts, high, mid, low = (q32, q_parts, 0, 1, 2) if kind == "q" else (k32, k_parts, 1, 2, 0)
                wait(pool, misc_drained, lambda n: at[kind, n] + 1, n, d)
                wait(pool, parts_stored[i], lambda n: 16 * n, n, d)
                pool.tensor_tensor(parts[:, high, :], full[:, :], one[:, :].to_broadcast([P, S]), ALU.mult).then_inc(pool_step, 1)
                wait(pool, pool_step, lambda n: 6 * n + 3 * i + 1, n, d)
                pool.tensor_tensor(parts[:, mid, :], full[:, :], parts[:, high, :], ALU.subtract).then_inc(pool_step, 1)
                wait(pool, split_ready, lambda n: 2 * n + i, n, d)
                pool.tensor_tensor(rest[:, :], full[:, :], parts[:, high, :], ALU.subtract).then_inc(pool_step, 1)
                wait(pool, pool_step, lambda n: 6 * n + 3 * i + 3, n, d)
                pool.tensor_tensor(parts[:, low, :], rest[:, :], parts[:, mid, :], ALU.subtract).then_inc(split_ready, 1)

            def second_norm(n, d):
                rstd, nmr = (ln2[:, v, :].unsqueeze(2).to_broadcast([P, QT, D]) for v in (1, 2))
                scale, shift_by = (row[n % 2][:, c0:c0 + D].unsqueeze(1).to_broadcast([P, QT, D]) for c0 in (ROW_C, ROW_S))
                to, again = (h2[n % 2][:, v, :, 0:D] for v in range(2))
                wait(pool, row_loaded[n % 2], lambda n: 16 * (n // 2 + 1), n, d)
                wait(pool, route_step, lambda n: ROUTE_STEPS * n, n, d)
                wait(pool, ln_step, lambda n: LN_STEPS * (n + 1), n, d)
                pool.tensor_tensor(to, x1_s[:, :, :], rstd, ALU.mult).then_inc(ln2_step, 1)
                wait(pool, ln2_step, lambda n: 3 * n + 1, n, d)
                pool.tensor_tensor(to, to, nmr, ALU.add).then_inc(ln2_step, 1)
                wait(pool, ln2_step, lambda n: 3 * n + 2, n, d)
                pool.tensor_tensor(to, to, scale, ALU.mult).then_inc(ln2_step, 1)
                wait(pool, ln2_step, lambda n: 3 * n + 3, n, d)
                pool.tensor_tensor(again, to, shift_by, ALU.add)
                pool.tensor_tensor(to, to, shift_by, ALU.add).then_inc(h2_ready, 1)

            def scatter(n, d, choices=range(2 * QT)):
                if n == NB - 1:
                    pool.wait_ge(route_step, ROUTE_STEPS * NB)
                for v in choices:
                    pool.indirect_dma_start(xs_d, bass.IndirectOffsetOnAxis(ap=rows_o[:, v:v + 1], axis=0),
                                            h2[n % 2][:, v // QT, v % QT, :], None).then_inc(scattered, 16)

            def batch(b, d=None):
                if 0 <= b - 2 < NB:
                    second_norm(b - 2, d)
                if 0 <= b - 3 < NB:
                    scatter(b - 3, d)
                if b + 2 < NB:
                    split("q", b + 2, d)
                    split("k", b + 2, d)

            split("q", 0, None)
            split("k", 0, None)
            for b in range(-1, FIRST):
                batch(b)
            with pool.Fori(0, LOOP) as d:
                batch(FIRST, d)
                batch(FIRST + 1, d)
            for b in range(FIRST + 2 * LOOP, NB + 1):
                batch(b)

            def pair(q, d=None):
                for m in range(PAIR):
                    i = PAIR * q + m
                    if i == NORM_AT:
                        second_norm(NB - 1, None)
                    for n, first, burst in ((NB - 2, NORM_AT + 2, 1), (NB - 1, len(LATE), 2)):
                        if 0 <= i - first < 2 * QT // burst:
                            scatter(n, None, range(burst * (i - first), burst * (i - first + 1)))
                    if d is None:
                        pool.wait_ge(y_taken, i + 1)
                    else:
                        along(pool, gone_step, lambda q: PAIR * (q - LATE_PAIRS) + m + 1, q, d)
                        along(pool, y_taken, lambda q: PAIR * q + m + 1, q, d)
                        pool.tensor_tensor(gone[:, :], one[:, :], one[:, :], ALU.mult).then_inc(gone_step, 1)
                    pool.indirect_dma_start(ys_d, bass.IndirectOffsetOnAxis(ap=x_in[m % SLOTS][:, D + 1:XW].bitcast(U32), axis=0),
                                            y_out[m % SLOTS], None).then_inc(y_stored[m % SLOTS], 16)

            NORM_AT = LATE.index((NB + 1, 0)) - 2
            for q in range(LATE_PAIRS):
                pair(q)
            pool.tensor_tensor(gone[:, :], one[:, :], one[:, :], ALU.mult).then_inc(gone_step, 1)
            with pool.Fori(0, NPAIR - LATE_PAIRS - 1) as d:
                pair(LATE_PAIRS, d)
            pair(NPAIR - 1)
            for i in LAST_BY_POOL:
                last_sum(pool, i)


_INS = ["L0_attn_x", "L0_attn_Wq", "L0_attn_bq", "L0_attn_Wk", "L0_attn_bk", "L0_attn_Wv", "L0_attn_bv",
        "L0_attn_Wo", "L0_attn_bo", "L0_ffn_gate_w", "L0_ffn_wg", "L0_ffn_wu", "L0_ffn_wd", "L0_c", "L0_wmod"]


def shape_constants():
    f32 = np.float32
    rank = np.broadcast_to(np.arange(NE, 0, -1, dtype=f32), (P, QT, NE))
    batches = np.arange(NB)
    slots = np.zeros((NB, 2 + NE), f32)
    slots[:, 0] = (batches + 1) % SBB != 0
    slots[:, 1] = batches * S
    slots[:, 2:] = ((batches // SBB)[:, None] * REGIONS + np.arange(NE)[None, :]) * REGION * P
    regions = (np.arange(NSB)[:, None] * REGIONS + np.arange(NE)[None, :]).reshape(-1) * REGION * P
    maps = np.concatenate([np.arange(TILES), np.tril(np.ones((NE, NE))).reshape(-1), np.arange(FULL) * P, regions])
    place = np.arange(P)[:, None] + np.concatenate([np.arange(QT) * P, NB * S + np.arange(QT) * P,
                                                    2 * NB * S + np.arange(BLANKS) * P])[None, :]
    return {"ident_c": np.eye(P, dtype=f32), "tri_c": np.triu(np.ones((P, P), f32), 1),
            "rank_c": np.ascontiguousarray(rank), "slots_c": slots, "map_c": maps.astype(f32)[None, :], "place_c": place.astype(f32)}


def kernel(**inputs):
    import concourse.bacc as bacc
    from concourse.bass_utils import run_bass_kernel_spmd

    nc = bacc.Bacc("TRN2", target_bir_lowering=False, num_devices=1)
    arrays = {name: np.ascontiguousarray(inputs[name]) for name in _INS}
    arrays.update(shape_constants())
    args = [nc.dram_tensor(name, a.shape, mybir.dt.from_np(a.dtype), kind="ExternalInput").ap()
            for name, a in arrays.items()]
    args.append(nc.dram_tensor("out", (NB, S, D), F32, kind="ExternalOutput").ap())
    adaln_block(nc, *args)
    result = run_bass_kernel_spmd(nc, [arrays], core_ids=[0])
    return result.results[0]["out"]
```
